# Optimizing a Trainium2 kernel written in Bass

```python
import numpy as np
import jax
import jax.numpy as jnp

def _softmax(x, axis=-1):
    return jax.nn.softmax(x, axis=axis)

def _gelu(x):
    return jax.nn.gelu(x, approximate=True)

def _silu(x):
    return jax.nn.silu(x)

def _sigmoid(x):
    return jax.nn.sigmoid(x)

def _layernorm(x, axis=-1, eps=1e-05):
    m = jnp.mean(x, axis=axis, keepdims=True)
    v = jnp.var(x, axis=axis, keepdims=True)
    return (x - m) / jnp.sqrt(v + eps)

def _scatter_add(tgt, idx, src, axis=0):
    return tgt.at[idx].add(src)

def _segment_sum(src, seg, n):
    return jax.ops.segment_sum(src, seg, n)
kernel_name = 'mk_xattn_seq_d2_seqx_r4_3d58a9'

def setup_inputs(seed: int=0):
    np.random.seed(seed)
    _w = jnp.asarray

    def _rec_inputs():
        import jax
        import jax.numpy as jnp
        _rk = jax.random.key(seed)
        x = -0.0003929 + 0.9999 * jax.random.normal(jax.random.fold_in(_rk, 1), (2, 512, 256), jnp.float32)
        _lenS = 512 - jax.random.randint(jax.random.fold_in(_rk, 7), (2,), 0, max(1, 512 // 4) + 1, jnp.int32)
        _lenS2 = 1024 - jax.random.randint(jax.random.fold_in(_rk, 8), (2,), 0, max(1, 1024 // 4) + 1, jnp.int32)
        _ctx_768P = jax.random.normal(jax.random.fold_in(_rk, 11), (2, 16, 192), jnp.float32)
        _ctx_768c = jax.random.dirichlet(jax.random.fold_in(_rk, 511), 0.3 * jnp.ones((16,), jnp.float32), (2, 1024))
        _ctx_768t = jnp.einsum('bsk,bkd->bsd', _ctx_768c, _ctx_768P)
        _ctx_768t = _ctx_768t * jax.lax.rsqrt(jnp.mean(jnp.square(_ctx_768t)) + 1e-12) * 0.953939
        ctx_768 = -7.36909e-05 + 0.999899 * (_ctx_768t + 0.3 * jax.random.normal(jax.random.fold_in(_rk, 611), (2, 1024, 192), jnp.float32))
        _validS = jnp.arange(512)[None, :] < _lenS[:, None]
        _validS2 = jnp.arange(1024)[None, :] < _lenS2[:, None]
        _causal = jnp.tril(jnp.ones((512, 512), dtype=bool))
        mask_BxS2_if1 = jnp.where(jnp.ones((2, 1024), dtype=bool), 1, 0).astype(jnp.int32)
        return (x, ctx_768, mask_BxS2_if1)
    x, ctx_768, mask_BxS2_if1 = _rec_inputs()

    def _L0_xattn_setup():
        import jax, jax.numpy as jnp
        import numpy as np
        EPS = 1e-05

        def _layer_norm(x, gamma, beta):
            mu = jnp.mean(x, axis=-1, keepdims=True)
            var = jnp.mean(jnp.square(x - mu), axis=-1, keepdims=True)
            return (x - mu) * jax.lax.rsqrt(var + EPS) * gamma + beta
        key = jax.random.key(seed)
        ks = jax.random.split(key, 12)
        B, Nq, Nkv = (8, 512, 512)
        E, Q, KV = (256, 256, 192)

        def lin(k, fan_in, shape):
            bound = 1.0 / np.sqrt(fan_in)
            return jax.random.uniform(k, shape, jnp.float32, -bound, bound)
        return {'q_feat': jax.random.normal(ks[0], (B, Nq, Q), jnp.float32), 'kv_feat': jax.random.normal(ks[1], (B, Nkv, KV), jnp.float32), 'Wq': lin(ks[2], Q, (E, Q)), 'bq': lin(ks[3], Q, (E,)), 'Wk': lin(ks[4], KV, (E, KV)), 'bk': lin(ks[5], KV, (E,)), 'Wv': lin(ks[6], KV, (E, KV)), 'bv': lin(ks[7], KV, (E,)), 'Wd': lin(ks[8], E, (E, E)), 'bd': lin(ks[9], E, (E,)), 'g_q': jnp.ones((Q,), jnp.float32), 'be_q': jnp.zeros((Q,), jnp.float32), 'g_kv': jnp.ones((KV,), jnp.float32), 'be_kv': jnp.zeros((KV,), jnp.float32)}
    _L0_xattn_all = _L0_xattn_setup()
    _L0_xattn_in = {k: v for k, v in _L0_xattn_all.items() if k in ('Wq', 'bq', 'Wk', 'bk', 'Wv', 'bv', 'Wd', 'bd', 'g_q', 'be_q', 'g_kv', 'be_kv')}
    del _L0_xattn_all

    def _L1_xattn_setup():
        import jax, jax.numpy as jnp
        import numpy as np
        import math
        H = 8
        D = 256
        D_I = 256
        D_L = 192
        EPS = 1e-05
        key = jax.random.key(seed)
        ks = jax.random.split(key, 8)
        B, NQ, NK = (8, 196, 128)
        img_embed = jax.random.normal(ks[0], (B, NQ, D_I), dtype=jnp.float32)
        sent_embed = jax.random.normal(ks[1], (B, NK, D_L), dtype=jnp.float32)
        atten_mask = jnp.ones((B, NK), dtype=jnp.int32)
        Wq = jax.random.normal(ks[2], (D_I, H * D), dtype=jnp.float32) * (1.0 / math.sqrt(D_I))
        Wk = jax.random.normal(ks[3], (D_L, H * D), dtype=jnp.float32) * (1.0 / math.sqrt(D_L))
        Wv = jax.random.normal(ks[4], (D_L, H * D), dtype=jnp.float32) * (1.0 / math.sqrt(D_L))
        Wo = jax.random.normal(ks[5], (H * D, D_I), dtype=jnp.float32) * (1.0 / math.sqrt(H * D))
        gamma = jnp.ones((D_I,), dtype=jnp.float32)
        beta = jnp.zeros((D_I,), dtype=jnp.float32)
        return {'img_embed': img_embed, 'sent_embed': sent_embed, 'atten_mask': atten_mask, 'Wq': Wq, 'Wk': Wk, 'Wv': Wv, 'Wo': Wo, 'gamma': gamma, 'beta': beta}
    _L1_xattn_all = _L1_xattn_setup()
    _L1_xattn_in = {k: v for k, v in _L1_xattn_all.items() if k in ('Wq', 'Wk', 'Wv', 'Wo', 'gamma', 'beta')}
    del _L1_xattn_all
    return {'x': x, 'ctx_768': ctx_768, 'mask_BxS2_if1': mask_BxS2_if1, 'L0_xattn_Wq': _L0_xattn_in['Wq'], 'L0_xattn_bq': _L0_xattn_in['bq'], 'L0_xattn_Wk': _L0_xattn_in['Wk'], 'L0_xattn_bk': _L0_xattn_in['bk'], 'L0_xattn_Wv': _L0_xattn_in['Wv'], 'L0_xattn_bv': _L0_xattn_in['bv'], 'L0_xattn_Wd': _L0_xattn_in['Wd'], 'L0_xattn_bd': _L0_xattn_in['bd'], 'L0_xattn_g_q': _L0_xattn_in['g_q'], 'L0_xattn_be_q': _L0_xattn_in['be_q'], 'L0_xattn_g_kv': _L0_xattn_in['g_kv'], 'L0_xattn_be_kv': _L0_xattn_in['be_kv'], 'L1_xattn_Wq': _L1_xattn_in['Wq'], 'L1_xattn_Wk': _L1_xattn_in['Wk'], 'L1_xattn_Wv': _L1_xattn_in['Wv'], 'L1_xattn_Wo': _L1_xattn_in['Wo'], 'L1_xattn_gamma': _L1_xattn_in['gamma'], 'L1_xattn_beta': _L1_xattn_in['beta']}

def reference(x, ctx_768, mask_BxS2_if1, L0_xattn_Wq, L0_xattn_bq, L0_xattn_Wk, L0_xattn_bk, L0_xattn_Wv, L0_xattn_bv, L0_xattn_Wd, L0_xattn_bd, L0_xattn_g_q, L0_xattn_be_q, L0_xattn_g_kv, L0_xattn_be_kv, L1_xattn_Wq, L1_xattn_Wk, L1_xattn_Wv, L1_xattn_Wo, L1_xattn_gamma, L1_xattn_beta):
    import jax
    import jax.numpy as jnp

    def _L0_xattn_ref(q_feat, kv_feat, Wq, bq, Wk, bk, Wv, bv, Wd, bd, g_q, be_q, g_kv, be_kv):
        import jax, jax.numpy as jnp
        import numpy as np
        EPS = 1e-05

        def _layer_norm(x, gamma, beta):
            mu = jnp.mean(x, axis=-1, keepdims=True)
            var = jnp.mean(jnp.square(x - mu), axis=-1, keepdims=True)
            return (x - mu) * jax.lax.rsqrt(var + EPS) * gamma + beta
        qn = _layer_norm(q_feat, g_q, be_q)
        kvn = _layer_norm(kv_feat, g_kv, be_kv)
        q = jnp.einsum('bnq,eq->bne', qn, Wq) + bq
        k = jnp.einsum('bmk,ek->bme', kvn, Wk) + bk
        v = jnp.einsum('bmk,ek->bme', kvn, Wv) + bv
        scores = jnp.einsum('bne,bme->bnm', q, k)
        attn = jax.nn.softmax(scores, axis=-1)
        ctx = jnp.einsum('bnm,bme->bne', attn, v)
        hidden = jnp.einsum('bne,fe->bnf', ctx, Wd) + bd
        return q_feat + hidden

    def _L1_xattn_ref(img_embed, sent_embed, atten_mask, Wq, Wk, Wv, Wo, gamma, beta):
        import jax, jax.numpy as jnp
        import numpy as np
        import math
        H = 8
        D = 256
        D_I = 256
        D_L = 192
        EPS = 1e-05
        B = img_embed.shape[0]
        Q = (img_embed @ Wq).reshape(B, -1, H, D).transpose(0, 2, 1, 3)
        K = (sent_embed @ Wk).reshape(B, -1, H, D).transpose(0, 2, 1, 3)
        V = (sent_embed @ Wv).reshape(B, -1, H, D).transpose(0, 2, 1, 3)
        score = jnp.einsum('bhqd,bhkd->bhqk', Q, K) / math.sqrt(D)
        mask = (atten_mask != 0)[:, None, None, :]
        score = jnp.where(mask, score, -jnp.inf)
        attn = jax.nn.softmax(score, axis=-1)
        ctx = jnp.einsum('bhqk,bhkd->bqhd', attn, V).reshape(B, -1, H * D)
        out = ctx @ Wo + img_embed
        mu = jnp.mean(out, axis=-1, keepdims=True)
        var = jnp.var(out, axis=-1, keepdims=True)
        return (out - mu) * jax.lax.rsqrt(var + EPS) * gamma + beta
    x = _L0_xattn_ref(x, ctx_768, L0_xattn_Wq, L0_xattn_bq, L0_xattn_Wk, L0_xattn_bk, L0_xattn_Wv, L0_xattn_bv, L0_xattn_Wd, L0_xattn_bd, L0_xattn_g_q, L0_xattn_be_q, L0_xattn_g_kv, L0_xattn_be_kv)
    x = _L1_xattn_ref(x, ctx_768, mask_BxS2_if1, L1_xattn_Wq, L1_xattn_Wk, L1_xattn_Wv, L1_xattn_Wo, L1_xattn_gamma, L1_xattn_beta)
    return x

_drawn_inputs = setup_inputs


def setup_inputs(seed=0):
    import zlib

    import numpy as np

    out = dict(_drawn_inputs(seed))
    spreads = {'L0_xattn_g_q': (1.0, 0.2),
     'L0_xattn_be_q': (0.0, 0.306),
     'L0_xattn_g_kv': (1.0, 0.2),
     'L0_xattn_be_kv': (0.0, 0.275),
     'L1_xattn_gamma': (1.0, 0.2),
     'L1_xattn_beta': (0.0, 0.1)}
    factors = {'L0_xattn_bq': 4.167, 'L0_xattn_bk': 8.0, 'L0_xattn_bv': 2.795}
    for name, (base, spread) in spreads.items():
        noise = np.random.default_rng([zlib.crc32(name.encode()), seed]).standard_normal(out[name].shape)
        drawn = base * np.exp(spread * noise) if base else spread * noise
        out[name] = jnp.asarray(drawn.astype(out[name].dtype))
    for name, factor in factors.items():
        out[name] = (out[name] * factor).astype(out[name].dtype)
    return out
```

```python
import concourse.bass as bass
from concourse import mybir
from concourse.alu_op_type import AluOpType as ALU
from contextlib import ExitStack

P = 128
BATCHES = 2
QUERIES = 512
KEYS = 1024
DIM = 256
CTX = 192
REM = CTX - P
HEADS = 8
QT = QUERIES // P
KT = KEYS // P
DT = DIM // P
BANK = 512
EPS = 1e-5
LN_TILES = KT + QT
BIG = 3.0e38

C_BQ, C_BK, C_BV, C_GQ, C_BEQ, C_GKV, C_BEKV, N_COLS = 0, 2, 4, 6, 8, 10, 12, 14
(PC_A0, PC_B0, PC_A1, PC_KA0, PC_KR0, PC_V00, PC_V01, PC_KA1, PC_KR1, PC_V10, PC_V11) = range(11)
(T_A0, T_A0b, T_VEC, T_Q0, T_Q0b, T_C0, T_B0, T_B0b, T_OUTB, T_Q1, T_Q1b, T_C1,
 T_A1, T_A1b, T_QH, T_QHb, TASKS0) = range(17)


def slot_no(h, j):
    return 8 * h + (8 + j)


def task_no(h, j):
    if isinstance(h, int) and h == HEADS - 1 and j >= 6:
        return TASKS0 + 8 * h + (j - 4)
    return 8 * h + (TASKS0 + j)


def pieces_a(h):
    return 2 * h + (PC_V11 + 2)


def pieces_b(h):
    if isinstance(h, int) and h == HEADS - 1:
        return 2 * h + (PC_V11 + 2)
    return 2 * h + (PC_V11 + 3)


def build(nc, x, context, mask, weights_a, weights_b, keys_t, vectors, rows, identity, out):
    f32, f32r, i32 = mybir.dt.float32, mybir.dt.float32r, mybir.dt.int32
    ACT = mybir.ActivationFunctionType
    AX = mybir.AxisListType

    x_tiles = x.rearrange("(t p) d -> p t d", p=P)
    out_tiles = out.rearrange("(t p) d -> p t d", p=P)
    ctx_tiles = context.rearrange("(t p) l -> p t l", p=P)

    with ExitStack() as stack:
        def sb(name, shape, dt=f32, on=stack):
            return on.enter_context(nc.sbuf_tensor(name, shape, dt))

        def sem(name):
            return stack.enter_context(nc.semaphore(name))

        key_hi = [sb(f"key_hi{b}", [P, KEYS], f32r) for b in range(BATCHES)]
        key_lo = [sb(f"key_lo{b}", [P, KEYS], f32r) for b in range(BATCHES)]
        key_rem = [sb(f"key_rem{b}", [P, KEYS], f32r) for b in range(BATCHES)]
        val_hi = [sb(f"val_hi{b}", [P, KT, P], f32r) for b in range(BATCHES)]
        val_lo = [sb(f"val_lo{b}", [P, KT, P], f32r) for b in range(BATCHES)]
        val_rem = [sb(f"val_rem{b}", [P, KT, P], f32r) for b in range(BATCHES)]
        xt_hi = sb("xt_hi", [P, DT, BATCHES * QUERIES], f32r)
        xt_lo = sb("xt_lo", [P, DT, BATCHES * QUERIES], f32r)
        q_hi = [sb(f"q_hi{b}", [P, 2, QUERIES], f32r) for b in range(BATCHES)]
        q_lo = [sb(f"q_lo{b}", [P, 2, QUERIES], f32r) for b in range(BATCHES)]
        a_hi, a_lo = sb("a_hi", [P, DT, DIM], f32r), sb("a_lo", [P, DT, DIM], f32r)
        b_hi, b_lo = sb("b_hi", [P, 2, DIM], f32r), sb("b_lo", [P, 2, DIM], f32r)
        b_full = sb("b_full", [P, 2, DIM])
        ring = [sb(f"ring{r}", [P, 1024]) for r in range(2)]
        w_hi, w_lo = sb("w_hi", [P, 1024], f32r), sb("w_lo", [P, 1024], f32r)
        neg_scores = sb("neg_scores", [P, KEYS])
        probs = sb("probs", [P, KEYS])
        mask_bias = sb("mask_bias", [P, BATCHES, KEYS])
        resid = sb("resid", [P, BATCHES * QT, DIM])
        ident = sb("ident", [P, P])
        cols = sb("cols", [P, N_COLS])
        row_vecs = sb("row_vecs", [P, 3, DIM])
        stats = sb("stats", [P, LN_TILES, 6])
        moments = sb("moments", [P, BATCHES * LN_TILES, 2])
        var_eps = sb("var_eps", [P, BATCHES * LN_TILES])
        rstd = sb("rstd", [P, BATCHES * LN_TILES])
        minus_half = sb("minus_half", [P, BATCHES * LN_TILES])
        row_min = sb("row_min", [P, 2 * QT])
        row_sum = sb("row_sum", [P, 2 * QT])
        row_inv = sb("row_inv", [P, 2 * QT])
        neg_bq = sb("neg_bq", [P, 2])
        wq_bk = sb("wq_bk", [P, DT, 2], f32r)
        bq_bk = sb("bq_bk", [P, 1])
        neg_shift = sb("neg_shift", [P, BATCHES * QT])
        probs_t_hi = [sb("probs_t_hi0", [P, KT, QUERIES], f32r)]
        probs_t_lo = [sb("probs_t_lo0", [P, KT, QUERIES], f32r)]
        with ExitStack() as early:
            ctx_raw = sb("ctx_raw", [P, BATCHES * KT, CTX], on=early)
            kvn = sb("kvn", [P, BATCHES * KT, 2 * P], on=early)
            xn = sb("xn", [P, BATCHES * QT, DIM], on=early)
            turned = sb("turned", [P, 2, BANK], on=early)
        probs_t_hi.append(sb("probs_t_hi1", [P, KT, QUERIES], f32r))
        probs_t_lo.append(sb("probs_t_lo1", [P, KT, QUERIES], f32r))
        o_hi, o_lo = sb("o_hi", [P, 2, QUERIES], f32r), sb("o_lo", [P, 2, QUERIES], f32r)
        spread = mask_bias[:, 0, 0:6 * P].rearrange("p (n q) -> p n q", n=6)
        outb = row_vecs[:, 0, :]
        finals = [probs, neg_scores]

        def rem_scratch(b, c):
            return w_hi[REM:P, (c - 2) * BANK:(c - 1) * BANK] if b else probs_t_hi[0][REM:P, c - 2, :]

        def ps(name, width):
            return stack.enter_context(nc.psum_tensor(name, [P, width], f32))
        ps_scores = ps("ps_scores", 2 * BANK)
        ps_turn = [ps(f"ps_turn{c}", BANK) for c in range(2)]
        ps_o = [ps(f"ps_o{c}", BANK) for c in range(2)]
        ps_out = ps("ps_out", BANK)
        ps_task = ps("ps_task", BANK)

        def out_bank(idx):
            s0, s1 = ps_scores[:, 0:DIM], ps_scores[:, BANK:BANK + DIM]
            t0, t1, w = ps_turn[0][:, 0:DIM], ps_turn[1][:, 0:DIM], ps_out[:, 0:DIM]
            first = {0: w, 1: s0, 2: s1, 3: w, 4: w, 5: t0, 6: t1, 7: w}
            last = {68: w, 69: s0, 70: s1, 71: t0}
            return {**first, **last}.get(idx, w) if isinstance(idx, int) else w

        ring_loaded = [sem(f"ring_loaded{r}") for r in range(2)]
        ctx_loaded = [sem(f"ctx_loaded{b}") for b in range(BATCHES)]
        x_loaded = [sem(f"x_loaded{b}") for b in range(BATCHES)]
        small_loaded = sem("small_loaded")
        mask_loaded = sem("mask_loaded")
        mask_made = sem("mask_made")
        stored = sem("stored")
        half_set = sem("half_set")
        ones_set = sem("ones_set")
        spread_made = sem("spread_made")
        stats_made = sem("stats_made")
        moments_made = sem("moments_made")
        var_made = sem("var_made")
        rstd_made = sem("rstd_made")
        normed = sem("normed")
        doubled = sem("doubled")
        chunk_turned = sem("chunk_turned")
        chunk_copied = sem("chunk_copied")
        chunk_rounded = sem("chunk_rounded")
        chunk_split = sem("chunk_split")
        piece_hi = sem("piece_hi")
        piece_split = sem("piece_split")
        vals0_hi = sem("vals0_hi")
        vals0_split = sem("vals0_split")
        vec_copied = sem("vec_copied")
        vec_made = sem("vec_made")
        shift_made = sem("shift_made")
        outb_made = sem("outb_made")
        biased = sem("biased")
        task_done = sem("task_done")
        task_hi = sem("task_hi")
        task_free = sem("task_free")
        b_scaled = sem("b_scaled")
        b_hi_made = sem("b_hi_made")
        b_split = sem("b_split")
        scored = sem("scored")
        min_made = sem("min_made")
        exped = sem("exped")
        probs_turned = sem("probs_turned")
        pt_hi_made = sem("pt_hi_made")
        pt_split = sem("pt_split")
        inv_made = sem("inv_made")
        valued = sem("valued")
        o_hi_made = sem("o_hi_made")
        o_split = sem("o_split")
        projected = sem("projected")
        added = sem("added")
        y_turned = sem("y_turned")
        y_hi_made = sem("y_hi_made")
        y_split = sem("y_split")
        fin_stats = sem("fin_stats")
        fin_moments = sem("fin_moments")
        fin_var = sem("fin_var")
        fin_rstd = sem("fin_rstd")
        fin_centred = sem("fin_centred")
        fin_made = sem("fin_made")

        block = stack.enter_context(nc.Block())

        @block.sync
        def _(sp):
            for g in range(2):
                t = slice(g * KT // 2, (g + 1) * KT // 2)
                sp.dma_start(ctx_raw[:, t, :], ctx_tiles[:, t, :]).then_inc(ctx_loaded[0], 16)
            sp.dma_start(resid[:, 0:QT, :], x_tiles[:, 0:QT, :]).then_inc(x_loaded[0], 16)
            sp.dma_start(ring[0][:, :], weights_a[0]).then_inc(ring_loaded[0], 16)
            sp.dma_start(ctx_raw[:, KT:, :], ctx_tiles[:, KT:, :]).then_inc(ctx_loaded[1], 16)
            sp.dma_start(resid[:, QT:, :], x_tiles[:, QT:, :]).then_inc(x_loaded[1], 16)

            def piece(k, src, dst=None):
                dst = ring[k % 2][:, :] if dst is None else dst
                sp.wait_ge(piece_split, k - 1)
                sp.dma_start(dst, src).then_inc(ring_loaded[k % 2], 16)

            def values(k, b, g):
                t = b * KT + g * KT // 2
                piece(k, ctx_tiles[:, t:t + KT // 2, :],
                      ring[k % 2][:, 0:CTX * KT // 2].rearrange("p (t l) -> p t l", l=CTX))

            sp.wait_ge(task_done, T_VEC + 1)
            piece(PC_A1, weights_a[1])
            sp.wait_ge(task_done, T_OUTB + 1)
            sp.dma_start(mask_bias[:, :, :].bitcast(i32), mask.partition_broadcast(P)).then_inc(mask_loaded, 16)
            piece(PC_KA0, keys_t[0, 0])
            piece(PC_KR0, keys_t[0, 1])
            values(PC_V00, 0, 0)
            values(PC_V01, 0, 1)
            piece(PC_KA1, keys_t[1, 0])
            piece(PC_KR1, keys_t[1, 1])
            values(PC_V10, 1, 0)
            values(PC_V11, 1, 1)

            def body(h):
                if not (isinstance(h, int) and h == HEADS - 1):
                    sp.wait_ge(piece_split, pieces_a(h) - 2)
                    sp.dma_start(ring[1][:, :], weights_a[h + 2]).then_inc(ring_loaded[1], 16)
                sp.wait_ge(piece_split, 2 * h + (PC_V11 + 1))
                sp.dma_start(ring[0][:, :], weights_b[h + 1]).then_inc(ring_loaded[0], 16)

            body(0)
            with sp.Fori(1, HEADS - 1) as h:
                body(h)
            body(HEADS - 1)

            for b in range(BATCHES):
                sp.wait_ge(fin_made, QT * (b + 1))
                sp.dma_start(out_tiles[:, b * QT:(b + 1) * QT, :],
                             finals[b][:, :].rearrange("p (t d) -> p t d", t=QT)).then_inc(stored, 16)
            sp.wait_ge(stored, 16 * BATCHES)

        @block.gpsimd
        def _(pool):
            nc.gpsimd.memset(minus_half[:, :], -0.5).then_inc(half_set, 1)
            pool.wait_ge(half_set, 1)
            for b in range(BATCHES):
                t = slice(b * LN_TILES, (b + 1) * LN_TILES)
                pool.wait_ge(var_made, b + 1)
                nc.gpsimd.tensor_tensor(rstd[:, t], var_eps[:, t], minus_half[:, t], ALU.pow)\
                    .then_inc(rstd_made, 1)
            pool.wait_ge(normed, BATCHES * LN_TILES)
            pool.wait_ge(outb_made, 1)
            for t in range(BATCHES * QT):
                nc.gpsimd.tensor_tensor(resid[:, t, :], resid[:, t, :], outb, ALU.add)\
                    .then_inc(biased, 1)
            for b in range(BATCHES):
                t = slice(b * QT, (b + 1) * QT)
                pool.wait_ge(fin_var, b + 1)
                nc.gpsimd.tensor_tensor(rstd[:, t], var_eps[:, t], minus_half[:, t], ALU.pow)\
                    .then_inc(fin_rstd, 1)

        @block.tensor
        def _(pe):
            def three(dst, left, right, start, stop):
                (lh, ll), (rh, rl) = left, right
                pe.matmul(dst, lh, rh, start=start, stop=False)
                pe.matmul(dst, lh, rl, start=False, stop=False)
                return pe.matmul(dst, ll, rh, start=False, stop=stop)

            def absorb(m):
                dst = ps_task[:, 0:DIM]
                for k in range(DT):
                    left, right = slice(k * DIM + m * P, k * DIM + (m + 1) * P), slice((DT + k) * DIM, (DT + k + 1) * DIM)
                    last = three(dst, (w_hi[:, left], w_lo[:, left]), (w_hi[:, right], w_lo[:, right]),
                                 k == 0, k == DT - 1)
                last.then_inc(task_done, 1)

            def queries(b, m):
                for k in range(DT):
                    s, mv = slice(m * P, (m + 1) * P), slice(b * QUERIES, (b + 1) * QUERIES)
                    last = three(ps_task[:, :], (a_hi[:, k, s], a_lo[:, k, s]),
                                 (xt_hi[:, k, mv], xt_lo[:, k, mv]), k == 0, k == DT - 1)
                last.then_inc(task_done, 1)

            def scores(h, j):
                b, q = j // QT, slice((j % QT) * P, (j % QT + 1) * P)
                s = slot_no(h, j)
                if not (isinstance(s, int) and s == 0):
                    pe.wait_ge(min_made, s)
                passes = ((q_hi[b][:, 0, q], key_hi[b]), (q_hi[b][:, 0, q], key_lo[b]),
                          (q_lo[b][:, 0, q], key_hi[b]), (q_hi[b][:, 1, q], key_rem[b]),
                          (q_lo[b][:, 1, q], key_rem[b]))
                for i, (left, right) in enumerate(passes):
                    for half in range(2):
                        n = slice(half * BANK, (half + 1) * BANK)
                        last = pe.matmul(ps_scores[:, n], left, right[:, n],
                                         start=(i == 0), stop=(i == len(passes) - 1))
                last.then_inc(scored, 1)

            def turn_probs(h, j):
                s = slot_no(h, j)
                for c in range(2):
                    if c == 0:
                        pe.wait_ge(exped, s + 1)
                    if not (isinstance(s, int) and s == 0):
                        pe.wait_ge(pt_split, 2 * s + (c - 1))
                    for k in range(4):
                        kt = 4 * c + k
                        last = pe.transpose(ps_turn[c][:, k * P:(k + 1) * P],
                                            probs[:, kt * P:(kt + 1) * P], ident[:, :])
                    last.then_inc(probs_turned, 1)

            def values(h, b, c):
                if c == 0:
                    s = slot_no(h, b * QT)
                    pe.wait_ge(pt_split, 2 * s + 2 * QT)
                    if not (isinstance(s, int) and s == 0):
                        pe.wait_ge(o_split, 4 * h + (4 + 2 * b))
                hi, lo = probs_t_hi[b], probs_t_lo[b]
                for kt in (2 * c, 2 * c + 1):
                    first, end = kt == 0, kt == KT - 1
                    pe.matmul(ps_o[0][:, :], val_hi[b][:, kt, :], hi[:, kt, :], start=first, stop=False)
                    pe.matmul(ps_o[0][:, :], val_hi[b][:, kt, :], lo[:, kt, :], start=False, stop=False)
                    pe.matmul(ps_o[0][:, :], val_lo[b][:, kt, :], hi[:, kt, :], start=False, stop=end)
                    pe.matmul(ps_o[1][:, :], val_rem[b][:, kt, :], hi[:, kt, :], start=first, stop=False)
                    last = pe.matmul(ps_o[1][:, :], val_rem[b][:, kt, :], lo[:, kt, :], start=False, stop=end)
                last.then_inc(valued, 1)

            def project(h, j):
                s = slot_no(h, j)
                q = slice((j % QT) * P, (j % QT + 1) * P)
                if j % QT == 0:
                    pe.wait_ge(o_split, 4 * h + (4 + 2 * (j // QT) + 2))
                    if j == 0:
                        pe.wait_ge(b_split, h + 2)
                if isinstance(s, int) and s in (3, 7):
                    pe.wait_ge(added, s - 2)
                elif isinstance(s, int) and s in (1, 2, 5, 6, 69, 70, 71):
                    pass
                elif not (isinstance(s, int) and s == 0):
                    pe.wait_ge(added, s)
                dst = out_bank(s)
                for k in range(2):
                    last = three(dst, (o_hi[:, k, q], o_lo[:, k, q]), (b_hi[:, k, :], b_lo[:, k, :]),
                                 k == 0, k == 1)
                last.then_inc(projected, 1)

            def turn_y(b):
                pe.wait_ge(added, QT * (b + 1))
                for c in range(DT):
                    for t in range(QT):
                        last = pe.transpose(ps_turn[c][:, t * P:(t + 1) * P],
                                            resid[:, b * QT + t, c * P:(c + 1) * P], ident[:, :])
                    last.then_inc(y_turned, 1)

            def turn_chunk(b, c):
                i = 6 * b + c
                if c < 4:
                    pe.wait_ge(normed, LN_TILES * b + KT)
                    if c == 2:
                        pe.wait_ge(doubled, b + 1)
                else:
                    pe.wait_ge(normed, LN_TILES * (b + 1))
                if i >= 2:
                    pe.wait_ge(chunk_rounded, i - 1)
                for t in range(4):
                    if c < 4:
                        src = kvn[:, b * KT + (c % 2) * 4 + t, (c // 2) * P:(c // 2 + 1) * P]
                    else:
                        src = xn[:, b * QT + t, (c - 4) * P:(c - 3) * P]
                    last = pe.transpose(ps_o[i % 2][:, t * P:(t + 1) * P], src, ident[:, :])
                last.then_inc(chunk_turned, 1)

            def shift(b):
                for t in range(QT):
                    q = slice((b * QT + t) * P, (b * QT + t + 1) * P)
                    n = 0
                    for k in range(DT):
                        for left in (xt_hi, xt_lo):
                            last = pe.matmul(ps_task[:, 2 * t:2 * t + 2], left[:, k, q], wq_bk[:, k, :],
                                             start=(n == 0), stop=(n == 2 * DT - 1))
                            n += 1
                last.then_inc(task_done, 1)

            pe.wait_ge(small_loaded, 48)
            pe.wait_ge(piece_split, PC_A0 + 1)
            absorb(0)
            pe.wait_ge(task_free, T_A0b)
            absorb(1)
            pe.wait_ge(spread_made, 6)
            pe.wait_ge(task_free, T_VEC)
            raw = ring[0]
            for n, (left, right) in enumerate((
                    [(raw[:, (DT + k) * DIM:(DT + k) * DIM + P], cols[:, C_BQ + k:C_BQ + k + 1]) for k in range(DT)],
                    [(raw[:, (DT + k) * DIM + P:(DT + k + 1) * DIM], cols[:, C_BQ + k:C_BQ + k + 1]) for k in range(DT)],
                    [(raw[:, k * DIM:k * DIM + P], cols[:, C_BK + k:C_BK + k + 1]) for k in range(DT)],
                    [(raw[:, k * DIM + P:(k + 1) * DIM], cols[:, C_BK + k:C_BK + k + 1]) for k in range(DT)],
                    [(spread[:, k, :], cols[:, C_BK + k:C_BK + k + 1]) for k in range(DT)])):
                pe.matmul(ps_task[:, n:n + 1], *left, start=True, stop=False)
                last = pe.matmul(ps_task[:, n:n + 1], *right, start=False, stop=True)
            last.then_inc(task_done, 1)
            for c in range(6):
                turn_chunk(0, c)
            pe.wait_ge(chunk_split, 6)
            pe.wait_ge(task_free, T_Q0)
            queries(0, 0)
            pe.wait_ge(task_free, T_Q0b)
            queries(0, 1)
            pe.wait_ge(task_free, T_C0)
            pe.wait_ge(vec_made, 3)
            shift(0)
            pe.wait_ge(task_free, T_C0)

            scores(-1, 0)
            pe.wait_ge(piece_split, PC_B0 + 1)
            pe.wait_ge(task_free, T_B0)
            absorb(0)
            pe.wait_ge(task_free, T_B0b)
            absorb(1)
            turn_probs(-1, 0)
            scores(-1, 1)
            for c in range(3):
                turn_chunk(1, c)
            pe.wait_ge(task_free, T_OUTB)
            raw = ring[1]
            dst = ps_task[:, 0:DIM]
            for k in range(DT):
                pe.matmul(dst, spread[:, DT + k, :], raw[:, (DT + k) * DIM:(DT + k + 1) * DIM],
                          start=(k == 0), stop=False)
            pe.matmul(dst, spread[:, 2 * DT, :], b_full[:, 0, :], start=False, stop=False)
            pe.matmul(dst, spread[0:REM, 2 * DT + 1, :], b_full[0:REM, 1, :], start=False, stop=True)\
                .then_inc(task_done, 1)
            turn_probs(-1, 1)
            scores(-1, 2)
            for c in range(3, 6):
                turn_chunk(1, c)
            turn_probs(-1, 2)
            scores(-1, 3)
            pe.wait_ge(chunk_split, 12)
            pe.wait_ge(task_free, T_Q1)
            queries(1, 0)
            pe.wait_ge(task_free, T_Q1b)
            queries(1, 1)
            pe.wait_ge(task_free, T_C1)
            shift(1)

            for j in range(QT):
                turn_probs(-1, QT + j - 1)
                scores(-1, QT + j)
                if j < 2:
                    if j == 0:
                        pe.wait_ge(piece_split, PC_A1 + 1)
                    pe.wait_ge(task_free, T_A1 + j)
                    absorb(j)
                if j == 0:
                    pe.wait_ge(vals0_split, 2)
                values(-1, 0, j)
            turn_probs(-1, 7)
            pe.wait_ge(vals0_split, 4)
            values(-1, 1, 0)
            for j in range(QT):
                project(-1, j)
            values(-1, 1, 1)
            values(-1, 1, 2)
            turn_y(0)
            values(-1, 1, 3)
            pe.wait_ge(y_split, DT)
            for m in range(2):
                pe.wait_ge(task_free, T_QH + m)
                queries(0, m)
            for j in range(QT, 2 * QT):
                project(-1, j)

            def body(h):
                at = lambda n: isinstance(h, int) and h == n
                for j in range(2 * QT):
                    b = j // QT
                    if j > 0:
                        turn_probs(h, j - 1)
                    elif not at(0):
                        turn_probs(h - 1, 2 * QT - 1)
                    if at(0) and j == 0:
                        pe.wait_ge(piece_split, PC_KR0 + 1)
                    if at(0) and j == QT:
                        pe.wait_ge(piece_split, PC_V11 + 1)
                    if j % QT == 0:
                        pe.wait_ge(task_free, TASKS0 if at(0) and j == 0 else task_no(h, -2 if j == 0 else 2))
                    scores(h, j)
                    if at(0) and j == 0:
                        turn_y(1)
                        pe.wait_ge(y_split, 2 * DT)
                    if not (at(HEADS - 1) and 2 <= j < 6):
                        pe.wait_ge(task_free, task_no(h, j))
                        if j < 2:
                            queries(1, j)
                        elif j < 4:
                            if j == 2:
                                pe.wait_ge(piece_split, pieces_a(h))
                            absorb(j - 2)
                        elif j < 6:
                            queries(0, j - 4)
                        else:
                            if j == 6:
                                pe.wait_ge(piece_split, pieces_b(h))
                            absorb(j - 6)
                    if b == 1:
                        values(h, 0, j - QT)
                    elif not at(0):
                        values(h - 1, 1, j)
                    if not at(0):
                        project(h - 1, j)

            body(0)
            with pe.Fori(1, HEADS - 1) as h:
                body(h)
            body(HEADS - 1)
            turn_probs(HEADS - 1, 2 * QT - 1)
            for c in range(QT):
                values(HEADS - 1, 1, c)
                project(HEADS - 1, c)
            for c in range(QT):
                project(HEADS - 1, QT + c)

        @block.scalar
        def _(act):
            act.dma_start(ident[:, :], identity).then_inc(small_loaded, 16)
            act.dma_start(cols[:, :], vectors).then_inc(small_loaded, 16)
            act.dma_start(row_vecs[:, :, :], rows.partition_broadcast(P)).then_inc(small_loaded, 16)
            act.dma_start(ring[1][:, :], weights_b[0]).then_inc(ring_loaded[1], 16)

            def exp(h, j):
                s = slot_no(h, j)
                if not (isinstance(s, int) and s == 0):
                    act.wait_ge(probs_turned, 2 * s)
                act.wait_ge(min_made, s + 1)
                act.activation(probs[:, :], neg_scores[:, :], ACT.Exp, bias=row_min[:, j:j + 1],
                               scale=-1.0, accum_out=row_sum[:, j:j + 1]).then_inc(exped, 1)

            def round_probs(h, j):
                s, b = slot_no(h, j), j // QT
                if j % QT == 0 and not (isinstance(s, int) and s < 8):
                    act.wait_ge(valued, s - 4)
                q = slice((j % QT) * P, (j % QT + 1) * P)
                for c in range(2):
                    act.wait_ge(probs_turned, 2 * s + (c + 1))
                    act.activation(probs_t_hi[b][:, 4 * c:4 * c + 4, q],
                                   ps_turn[c][:, :].rearrange("p (k q) -> p k q", k=4), ACT.Copy)\
                        .then_inc(pt_hi_made, 1)

            def round_outputs(h, b):
                s = slot_no(h, b * QT)
                act.wait_ge(valued, s + 4)
                if not (isinstance(s, int) and s == 0):
                    act.wait_ge(projected, s)
                for k in range(2):
                    act.activation(o_hi[:, k, :], ps_o[k][:, :], ACT.Copy).then_inc(o_hi_made, 1)

            def round_a(task, m, scale):
                act.wait_ge(task_done, task + 1)
                act.activation(a_hi[:, m, :], ps_task[:, 0:DIM], ACT.Copy, scale=scale).then_inc(task_hi, 1)

            def round_queries(task, b, m, layer):
                act.wait_ge(task_done, task + 1)
                if layer:
                    act.activation(q_hi[b][:, m, :], ps_task[:, :], ACT.Copy).then_inc(task_hi, 1)
                else:
                    act.activation(q_hi[b][:, m, :], ps_task[:, :], ACT.Identity,
                                   bias=neg_bq[:, m:m + 1]).then_inc(task_hi, 1)

            def keep_b(task, m):
                act.wait_ge(task_done, task + 1)
                act.activation(b_full[:, m, :], ps_task[:, 0:DIM], ACT.Copy).then_inc(task_free, 1)

            def round_weights(loaded, r):
                act.wait_ge(ring_loaded[r], loaded)
                act.activation(w_hi[:, :], ring[r][:, :], ACT.Copy).then_inc(piece_hi, 1)

            def round_keys(k, b):
                act.wait_ge(scored, 4 * (b + 1))
                act.wait_ge(ring_loaded[k % 2], 16 * (k // 2 + 1))
                act.activation(key_hi[b][:, :], ring[k % 2][:, :], ACT.Copy).then_inc(piece_hi, 1)
                k += 1
                act.wait_ge(ring_loaded[k % 2], 16 * (k // 2 + 1))
                act.activation(key_rem[b][0:REM, :], ring[k % 2][0:REM, :], ACT.Copy).then_inc(piece_hi, 1)
                act.activation(w_hi[REM:P, :], ring[k % 2][REM:P, :], ACT.Copy).then_inc(piece_hi, 1)

            def round_values(k, b):
                act.wait_ge(valued, 4 * (b + 1))
                for g in range(2):
                    src = ring[(k + g) % 2][:, 0:CTX * KT // 2].rearrange("p (t l) -> p t l", l=CTX)
                    t = slice(g * KT // 2, (g + 1) * KT // 2)
                    act.wait_ge(ring_loaded[(k + g) % 2], 16 * ((k + g) // 2 + 1))
                    act.activation(val_hi[b][:, t, :], src[:, :, 0:P], ACT.Copy).then_inc(piece_hi, 1)
                    act.activation(val_rem[b][:, t, 0:REM], src[:, :, P:CTX], ACT.Copy).then_inc(piece_hi, 1)

            def double_context(b):
                t = slice(b * KT, (b + 1) * KT)
                act.wait_ge(normed, LN_TILES * b + KT)
                act.activation(kvn[:, t, CTX:2 * P], kvn[:, t, P:CTX], ACT.Copy).then_inc(doubled, 1)

            def take_chunk(b, c):
                i = 6 * b + c
                src = ps_o[i % 2]
                f = c // 2 if c < 4 else c - 4
                g, be = (C_GKV, C_BEKV) if c < 4 else (C_GQ, C_BEQ)
                gain, bias = cols[:, g + f:g + f + 1], cols[:, be + f:be + f + 1]
                act.wait_ge(chunk_turned, i + 1)
                if i >= 2:
                    act.wait_ge(chunk_split, i - 1)
                act.activation(turned[:, i % 2, :], src[:, :], ACT.Identity, bias=bias, scale=gain)\
                    .then_inc(chunk_copied, 1)
                n = slice((c % 2) * BANK, (c % 2 + 1) * BANK)
                if c < 2:
                    act.activation(key_hi[b][:, n], src[:, :], ACT.Identity, bias=bias, scale=gain)\
                        .then_inc(chunk_rounded, 1)
                elif c < 4:
                    act.activation(key_rem[b][0:REM, n], src[0:REM, :], ACT.Identity,
                                   bias=cols[0:REM, be + f:be + f + 1], scale=cols[0:REM, g + f:g + f + 1])\
                        .then_inc(chunk_copied, 1)
                    act.activation(rem_scratch(b, c), src[REM:P, :],
                                   ACT.Identity, bias=cols[REM:P, be + f:be + f + 1],
                                   scale=cols[REM:P, g + f:g + f + 1]).then_inc(chunk_rounded, 1)
                else:
                    act.activation(xt_hi[:, f, b * QUERIES:(b + 1) * QUERIES], src[:, :], ACT.Identity,
                                   bias=bias, scale=gain).then_inc(chunk_rounded, 1)

            def round_vals0(b):
                t = slice(b * KT, (b + 1) * KT)
                act.activation(val_hi[b][:, :, :], kvn[:, t, 0:P], ACT.Copy).then_inc(vals0_hi, 1)
                act.activation(val_rem[b][:, :, 0:REM], kvn[:, t, P:CTX], ACT.Copy).then_inc(vals0_hi, 1)

            def round_y(b):
                for c in range(DT):
                    act.wait_ge(y_turned, DT * b + c + 1)
                    act.activation(xt_hi[:, c, b * QUERIES:(b + 1) * QUERIES], ps_turn[c][:, :], ACT.Copy)\
                        .then_inc(y_hi_made, 1)

            round_weights(16, 0)
            act.wait_ge(small_loaded, 48)
            round_a(T_A0, 0, -1.0)
            round_a(T_A0b, 1, -1.0)
            double_context(0)
            for c in range(6):
                take_chunk(0, c)
            act.wait_ge(vec_made, 1)
            round_queries(T_Q0, 0, 0, 0)
            round_queries(T_Q0b, 0, 1, 0)
            round_weights(16, 1)
            exp(-1, 0)
            keep_b(T_B0, 0)
            keep_b(T_B0b, 1)
            round_probs(-1, 0)
            exp(-1, 1)
            double_context(1)
            for c in range(3):
                take_chunk(1, c)
            round_vals0(0)
            round_probs(-1, 1)
            exp(-1, 2)
            for c in range(3, 6):
                take_chunk(1, c)
            round_probs(-1, 2)
            exp(-1, 3)
            act.wait_ge(scored, 4)
            round_queries(T_Q1, 1, 0, 0)
            round_queries(T_Q1b, 1, 1, 0)
            round_vals0(1)
            act.wait_ge(chunk_split, 12)
            round_weights(16 * (PC_A1 // 2 + 1), 0)
            for j in range(QT):
                round_probs(-1, QT + j - 1)
                exp(-1, QT + j)
                if j < 2:
                    round_a(T_A1 + j, j, -1.0 / 16)
                if j == 2:
                    round_keys(PC_KA0, 0)
            round_outputs(-1, 0)
            round_probs(-1, 7)
            round_values(PC_V00, 0)
            round_y(0)
            round_queries(T_QH, 0, 0, 1)
            round_queries(T_QHb, 0, 1, 1)
            round_outputs(-1, 1)

            def body(h):
                at = lambda n: isinstance(h, int) and h == n
                for j in range(2 * QT):
                    if j > 0:
                        round_probs(h, j - 1)
                    elif not at(0):
                        round_probs(h - 1, 2 * QT - 1)
                    exp(h, j)
                    if at(0) and j == 0:
                        round_y(1)
                    if not (at(HEADS - 1) and 2 <= j < 6):
                        task = task_no(h, j)
                        if j < 2:
                            round_queries(task, 1, j, 1)
                        elif j < 4:
                            round_a(task, j - 2, -1.0 / 16)
                        elif j < 6:
                            round_queries(task, 0, j - 4, 1)
                        else:
                            if j == 6 and not at(0):
                                act.wait_ge(b_split, h + 1)
                            keep_b(task, j - 6)
                    if at(0) and j == 0:
                        round_keys(PC_KA1, 1)
                    if at(0) and j == 1:
                        round_values(PC_V10, 1)
                    if j == 1 and not at(HEADS - 1):
                        if not at(0):
                            act.wait_ge(task_done, task_no(h, 0))
                        round_weights(16 * h + 16 * (PC_V11 // 2 + 1), 1)
                    if j == 3:
                        act.wait_ge(task_done, task_no(h, 4) if not at(HEADS - 1) else TASKS0 + 8 * h + 2)
                        round_weights(16 * h + 16 * (PC_V11 // 2 + 2), 0)
                        if not at(0):
                            round_outputs(h - 1, 1)
                    if j == 2 * QT - 1:
                        round_outputs(h, 0)

            body(0)
            with act.Fori(1, HEADS - 1) as h:
                body(h)
            body(HEADS - 1)
            round_probs(HEADS - 1, 2 * QT - 1)
            round_outputs(HEADS - 1, 1)

        @block.vector
        def _(dve):
            def invert(j):
                dve.reciprocal(row_inv[:, j:j + 1], row_sum[:, j:j + 1]).then_inc(inv_made, 1)

            def minimum(h, j, layer):
                s, b = slot_no(h, j), j // QT
                if not (isinstance(s, int) and s == 0):
                    dve.wait_ge(exped, s)
                if not (isinstance(s, int) and s <= 8):
                    dve.wait_ge(added, s - 8)
                dve.wait_ge(scored, s + 1)
                if not (isinstance(s, int) and s in (0, 8)):
                    invert((j - 1) % (2 * QT))
                if layer:
                    dve.wait_ge(mask_made, 2)
                    dve.tensor_tensor_reduce(
                        out=neg_scores[:, :], in0=ps_scores[:, :], in1=mask_bias[:, b, :], scale=1.0, scalar=BIG,
                        op0=ALU.add, op1=ALU.min, accum_out=row_min[:, j:j + 1]).then_inc(min_made, 1)
                else:
                    dve.wait_ge(shift_made, 2 * (b + 1))
                    dve.tensor_scalar(neg_scores[:, :], ps_scores[:, :], neg_shift[:, j:j + 1], None,
                                      ALU.add, ALU.min, accum_out=row_min[:, j:j + 1]).then_inc(min_made, 1)

            def split_probs(h, j):
                s, b = slot_no(h, j), j // QT
                q = slice((j % QT) * P, (j % QT + 1) * P)
                for c in range(2):
                    dve.wait_ge(pt_hi_made, 2 * s + (c + 1))
                    dve.tensor_tensor(probs_t_lo[b][:, 4 * c:4 * c + 4, q],
                                      ps_turn[c][:, :].rearrange("p (k q) -> p k q", k=4),
                                      probs_t_hi[b][:, 4 * c:4 * c + 4, q].bitcast(f32), ALU.subtract)\
                        .then_inc(pt_split, 1)

            def split_outputs(h, b):
                n2 = 4 * h + (4 + 2 * b)
                for k in range(2):
                    dve.wait_ge(o_hi_made, n2 + (k + 1))
                    dve.tensor_tensor(o_lo[:, k, :], ps_o[k][:, :], o_hi[:, k, :].bitcast(f32), ALU.subtract)\
                        .then_inc(o_split, 1)

            def split_a(task, m, scale):
                dve.wait_ge(task_hi, hi_before(task) + 1)
                dve.scalar_tensor_tensor(a_lo[:, m, :], ps_task[:, 0:DIM], scale, a_hi[:, m, :].bitcast(f32),
                                         ALU.mult, ALU.subtract).then_inc(task_free, 1)

            def split_queries(task, b, m, layer):
                dve.wait_ge(task_hi, hi_before(task) + 1)
                hi = q_hi[b][:, m, :].bitcast(f32)
                if layer:
                    dve.tensor_tensor(q_lo[b][:, m, :], ps_task[:, :], hi, ALU.subtract).then_inc(task_free, 1)
                else:
                    dve.scalar_tensor_tensor(q_lo[b][:, m, :], ps_task[:, :], neg_bq[:, m:m + 1], hi,
                                             ALU.add, ALU.subtract).then_inc(task_free, 1)

            def hi_before(task):
                if isinstance(task, int) and task < TASKS0:
                    return sum(t in (T_A0, T_A0b, T_Q0, T_Q0b, T_Q1, T_Q1b, T_A1, T_A1b, T_QH, T_QHb)
                               for t in range(task))
                raise ValueError(task)

            def split_b(count, gain):
                if gain:
                    for k in range(2):
                        dve.wait_ge(task_free, T_B0 + 1 + k)
                        dve.tensor_scalar(b_hi[:, k, :], b_full[:, k, :], cols[:, C_GKV + k:C_GKV + k + 1], None,
                                          ALU.mult).then_inc(b_hi_made, 1)
                    dve.wait_ge(b_hi_made, 2)
                    for k in range(2):
                        last = dve.scalar_tensor_tensor(b_lo[:, k, :], b_full[:, k, :],
                                                        cols[:, C_GKV + k:C_GKV + k + 1],
                                                        b_hi[:, k, :].bitcast(f32), ALU.mult, ALU.subtract)
                    last.then_inc(b_split, 1)
                else:
                    dve.tensor_copy(b_hi[:, :, :], b_full[:, :, :]).then_inc(b_hi_made, 2)
                    dve.wait_ge(b_hi_made, 2 * count)
                    dve.tensor_tensor(b_lo[:, :, :], b_full[:, :, :], b_hi[:, :, :].bitcast(f32), ALU.subtract)\
                        .then_inc(b_split, 1)

            def split_weights(hi_count, r):
                dve.wait_ge(piece_hi, hi_count)
                dve.tensor_tensor(w_lo[:, :], ring[r][:, :], w_hi[:, :].bitcast(f32), ALU.subtract)\
                    .then_inc(piece_split, 1)

            def split_keys(k, b, hi_count):
                dve.wait_ge(piece_hi, hi_count + 1)
                dve.tensor_tensor(key_lo[b][:, :], ring[k % 2][:, :], key_hi[b][:, :].bitcast(f32), ALU.subtract)\
                    .then_inc(piece_split, 1)
                dve.wait_ge(piece_hi, hi_count + 3)
                dve.tensor_tensor(key_rem[b][REM:P, :], ring[(k + 1) % 2][REM:P, :], w_hi[REM:P, :].bitcast(f32),
                                  ALU.subtract).then_inc(piece_split, 1)

            def split_values(k, b, hi_count):
                for g in range(2):
                    src = ring[(k + g) % 2][:, 0:CTX * KT // 2].rearrange("p (t l) -> p t l", l=CTX)
                    t = slice(g * KT // 2, (g + 1) * KT // 2)
                    dve.wait_ge(piece_hi, hi_count + 2 * g + 2)
                    dve.tensor_tensor(val_lo[b][:, t, :], src[:, :, 0:P], val_hi[b][:, t, :].bitcast(f32),
                                      ALU.subtract)
                    dve.tensor_tensor(val_rem[b][:, t, REM:P], src[:, :, P:CTX],
                                      val_rem[b][:, t, 0:REM].bitcast(f32), ALU.subtract).then_inc(piece_split, 1)

            def add(h, j):
                s = slot_no(h, j)
                if isinstance(s, int) and s < 8:
                    dve.wait_ge(biased, j + 1)
                    dve.wait_ge(inv_made, s + 1)
                else:
                    dve.wait_ge(added, s - 7)
                dve.wait_ge(projected, s + 1)
                dve.scalar_tensor_tensor(resid[:, j, :], out_bank(s), row_inv[:, j:j + 1], resid[:, j, :],
                                         ALU.mult, ALU.add).then_inc(added, 1)

            def ln_stats(b):
                for t in range(LN_TILES):
                    if b == 0 and t in (0, KT // 2):
                        dve.wait_ge(ctx_loaded[0], 32)
                    elif b == 1 and t == 0:
                        dve.wait_ge(ctx_loaded[1], 16)
                    elif t == KT:
                        dve.wait_ge(x_loaded[b], 16)
                    if b == 1 and t == 0:
                        dve.wait_ge(moments_made, LN_TILES)
                    src = ctx_raw[:, b * KT + t, :] if t < KT else resid[:, b * QT + t - KT, :]
                    dve.bn_stats(stats[:, t, :], src).then_inc(stats_made, 1)
                for t in range(LN_TILES):
                    n = b * LN_TILES + t
                    dve.wait_ge(stats_made, n + 1)
                    dve.bn_aggr(moments[:, n, :], stats[:, t, :]).then_inc(moments_made, 1)
                n = slice(b * LN_TILES, (b + 1) * LN_TILES)
                dve.wait_ge(moments_made, (b + 1) * LN_TILES)
                dve.tensor_scalar(var_eps[:, n], moments[:, n, 1], EPS, None, ALU.add).then_inc(var_made, 1)

            def ln_apply(b):
                dve.wait_ge(rstd_made, b + 1)
                for t in range(LN_TILES):
                    n = b * LN_TILES + t
                    if t < KT:
                        dst, src = kvn[:, b * KT + t, 0:CTX], ctx_raw[:, b * KT + t, :]
                    else:
                        dst, src = xn[:, b * QT + t - KT, :], resid[:, b * QT + t - KT, :]
                    dve.tensor_scalar(dst, src, moments[:, n, 0:1], rstd[:, n:n + 1], ALU.subtract, ALU.mult)\
                        .then_inc(normed, 1)

            def split_chunk(b, c):
                i = 6 * b + c
                f = c - 4
                n = slice((c % 2) * BANK, (c % 2 + 1) * BANK)
                src = turned[:, i % 2, :]
                dve.wait_ge(chunk_rounded, i + 1)
                if c < 2:
                    dve.tensor_tensor(key_lo[b][:, n], src, key_hi[b][:, n].bitcast(f32), ALU.subtract)\
                        .then_inc(chunk_split, 1)
                elif c < 4:
                    dve.tensor_tensor(key_rem[b][REM:P, n], turned[REM:P, i % 2, :], rem_scratch(b, c).bitcast(f32),
                                      ALU.subtract).then_inc(chunk_split, 1)
                else:
                    q = slice(b * QUERIES, (b + 1) * QUERIES)
                    dve.tensor_tensor(xt_lo[:, f, q], src, xt_hi[:, f, q].bitcast(f32), ALU.subtract)\
                        .then_inc(chunk_split, 1)

            def split_vals0(b):
                t = slice(b * KT, (b + 1) * KT)
                dve.wait_ge(vals0_hi, 2 * (b + 1))
                dve.tensor_tensor(val_lo[b][:, :, :], kvn[:, t, 0:P], val_hi[b][:, :, :].bitcast(f32),
                                  ALU.subtract).then_inc(vals0_split, 1)
                dve.tensor_tensor(val_rem[b][:, :, REM:P], kvn[:, t, P:CTX], val_rem[b][:, :, 0:REM].bitcast(f32),
                                  ALU.subtract).then_inc(vals0_split, 1)

            def take_shift(task, b):
                t = slice(b * QT, (b + 1) * QT)
                dve.wait_ge(task_done, task + 1)
                dve.tensor_reduce(neg_shift[:, t], ps_task[:, 0:2 * QT].rearrange("p (t n) -> p t n", n=2),
                                  axis=AX.X, op=ALU.add).then_inc(task_free, 1)
                dve.wait_ge(task_free, task + 1)
                dve.tensor_scalar(neg_shift[:, t], neg_shift[:, t], bq_bk[:, :], -1.0, ALU.add, ALU.mult)\
                    .then_inc(shift_made, 2)

            def split_y(b):
                q = slice(b * QUERIES, (b + 1) * QUERIES)
                for c in range(DT):
                    dve.wait_ge(y_hi_made, DT * b + c + 1)
                    dve.tensor_tensor(xt_lo[:, c, q], ps_turn[c][:, :], xt_hi[:, c, q].bitcast(f32), ALU.subtract)\
                        .then_inc(y_split, 1)

            dve.memset(spread[:, :, :], 1.0).then_inc(ones_set, 1)
            ln_stats(0)
            split_weights(1, 0)
            dve.wait_ge(small_loaded, 48)
            dve.wait_ge(ones_set, 1)
            for n, c in enumerate((C_BQ, C_BQ + 1, C_BV, C_BV + 1, C_BEKV, C_BEKV + 1)):
                dve.tensor_scalar(spread[:, n, :], spread[:, n, :], cols[:, c:c + 1], None, ALU.mult)\
                    .then_inc(spread_made, 1)
            ln_apply(0)
            split_a(T_A0, 0, -1.0)
            split_a(T_A0b, 1, -1.0)
            dve.wait_ge(task_done, T_VEC + 1)
            dve.tensor_scalar(neg_bq[:, :], ps_task[:, 0:2], -1.0, None, ALU.mult).then_inc(vec_made, 1)
            dve.tensor_copy(wq_bk[:, :, 0], ps_task[:, 2:4]).then_inc(vec_copied, 1)
            dve.tensor_copy(bq_bk[:, :], ps_task[:, 4:5]).then_inc(vec_made, 1)
            dve.wait_ge(vec_copied, 1)
            dve.wait_ge(vec_made, 2)
            dve.tensor_tensor(wq_bk[:, :, 1], ps_task[:, 2:4], wq_bk[:, :, 0].bitcast(f32), ALU.subtract)\
                .then_inc(task_free, 1)
            dve.wait_ge(task_free, T_VEC + 1)
            dve.engine_nop().then_inc(vec_made, 1)
            for c in range(6):
                split_chunk(0, c)
            split_queries(T_Q0, 0, 0, 0)
            split_queries(T_Q0b, 0, 1, 0)
            take_shift(T_C0, 0)
            split_weights(2, 1)
            minimum(-1, 0, 0)
            ln_stats(1)
            split_probs(-1, 0)
            minimum(-1, 1, 0)
            ln_apply(1)
            split_b(1, True)
            for c in range(3):
                split_chunk(1, c)
            split_vals0(0)
            dve.wait_ge(task_done, T_OUTB + 1)
            dve.tensor_tensor(outb, ps_task[:, 0:DIM], outb, ALU.add).then_inc(outb_made, 1)
            dve.wait_ge(outb_made, 1)
            dve.engine_nop().then_inc(task_free, 1)
            split_probs(-1, 1)
            minimum(-1, 2, 0)
            for c in range(3, 6):
                split_chunk(1, c)
            split_probs(-1, 2)
            minimum(-1, 3, 0)
            split_queries(T_Q1, 1, 0, 0)
            split_queries(T_Q1b, 1, 1, 0)
            take_shift(T_C1, 1)
            split_vals0(1)
            split_weights(3, 0)
            dve.wait_ge(mask_loaded, 16)
            dve.tensor_scalar(mask_bias[:, :, :], mask_bias[:, :, :].bitcast(i32), 0.0, BIG, ALU.is_equal, ALU.mult)\
                .then_inc(mask_made, 1)
            dve.wait_ge(mask_made, 1)
            dve.tensor_scalar(mask_bias[:, :, :], mask_bias[:, :, :], 10.0, None, ALU.mult).then_inc(mask_made, 1)
            for j in range(QT):
                split_probs(-1, QT + j - 1)
                minimum(-1, QT + j, 0)
                if j < 2:
                    split_a(T_A1 + j, j, -1.0 / 16)
                if j == 2:
                    split_keys(PC_KA0, 0, 3)
            split_outputs(-1, 0)
            split_probs(-1, 7)
            invert(7)
            for j in range(QT):
                add(-1, j)
            split_values(PC_V00, 0, 6)
            split_y(0)
            split_queries(T_QH, 0, 0, 1)
            split_queries(T_QHb, 0, 1, 1)
            split_outputs(-1, 1)
            for j in range(QT, 2 * QT):
                add(-1, j)

            HI0, PIECES0 = 10, 17

            def body(h):
                at = lambda n: isinstance(h, int) and h == n
                for j in range(2 * QT):
                    if j > 0:
                        split_probs(h, j - 1)
                    elif not at(0):
                        split_probs(h - 1, 2 * QT - 1)
                    minimum(h, j, 1)
                    if at(0) and j == 0:
                        split_y(1)
                    if j < 6 and not (at(HEADS - 1) and j >= 2):
                        dve.wait_ge(task_hi, 6 * h + (HI0 + j + 1))
                        if j in (2, 3):
                            dve.scalar_tensor_tensor(a_lo[:, j - 2, :], ps_task[:, 0:DIM], -1.0 / 16,
                                                     a_hi[:, j - 2, :].bitcast(f32), ALU.mult, ALU.subtract)\
                                .then_inc(task_free, 1)
                        else:
                            b, m = (1, j) if j < 2 else (0, j - 4)
                            dve.tensor_tensor(q_lo[b][:, m, :], ps_task[:, :], q_hi[b][:, m, :].bitcast(f32),
                                              ALU.subtract).then_inc(task_free, 1)
                    if at(0) and j == 0:
                        split_keys(PC_KA1, 1, 10)
                    if at(0) and j == 1:
                        split_values(PC_V10, 1, 13)
                    if j == 1 and not at(HEADS - 1):
                        split_weights(2 * h + (PIECES0 + 1), 1)
                    if j == 3:
                        split_weights(2 * h + (PIECES0 + (1 if at(HEADS - 1) else 2)), 0)
                    if not at(0):
                        add(h - 1, j)
                    if j == 3 and not at(0):
                        split_outputs(h - 1, 1)
                    if j == 2 * QT - 1:
                        split_outputs(h, 0)
                        dve.wait_ge(projected, 8 * h + 8)
                        dve.wait_ge(task_free, task_no(h, 8) if not at(HEADS - 1) else TASKS0 + 8 * h + 4)
                        split_b(h + 2, False)

            body(0)
            with dve.Fori(1, HEADS - 1) as h:
                body(h)
            body(HEADS - 1)
            split_probs(HEADS - 1, 2 * QT - 1)
            invert(2 * QT - 1)
            for j in range(QT):
                add(HEADS - 1, j)
            split_outputs(HEADS - 1, 1)

            def final(b):
                for t in range(QT):
                    n = b * QT + t
                    if b == 1:
                        add(HEADS - 1, n)
                    dve.wait_ge(added, 8 * HEADS + n + 1)
                    dve.bn_stats(stats[:, n, :], resid[:, n, :]).then_inc(fin_stats, 1)
                for t in range(QT):
                    n = b * QT + t
                    dve.wait_ge(fin_stats, n + 1)
                    dve.bn_aggr(moments[:, n, :], stats[:, n, :]).then_inc(fin_moments, 1)
                n = slice(b * QT, (b + 1) * QT)
                dve.wait_ge(fin_moments, (b + 1) * QT)
                dve.tensor_scalar(var_eps[:, n], moments[:, n, 1], EPS, None, ALU.add).then_inc(fin_var, 1)
                for t in range(QT):
                    n = b * QT + t
                    dve.scalar_tensor_tensor(resid[:, n, :], resid[:, n, :], moments[:, n, 0:1], row_vecs[:, 1, :],
                                             ALU.subtract, ALU.mult).then_inc(fin_centred, 1)
                dve.wait_ge(fin_rstd, b + 1)
                for t in range(QT):
                    n = b * QT + t
                    dve.wait_ge(fin_centred, n + 1)
                    dve.scalar_tensor_tensor(finals[b][:, t * DIM:(t + 1) * DIM], resid[:, n, :], rstd[:, n:n + 1],
                                             row_vecs[:, 2, :], ALU.mult, ALU.add).then_inc(fin_made, 1)

            final(0)
            final(1)


def kernel(x, ctx_768, mask_BxS2_if1, L0_xattn_Wq, L0_xattn_bq, L0_xattn_Wk, L0_xattn_bk, L0_xattn_Wv,
           L0_xattn_bv, L0_xattn_Wd, L0_xattn_bd, L0_xattn_g_q, L0_xattn_be_q, L0_xattn_g_kv, L0_xattn_be_kv,
           L1_xattn_Wq, L1_xattn_Wk, L1_xattn_Wv, L1_xattn_Wo, L1_xattn_gamma, L1_xattn_beta):
    import numpy as np
    import concourse.bacc as bacc
    from concourse.bass_utils import run_bass_kernel_spmd

    def a(v):
        return np.asarray(v)

    twice = np.r_[0:CTX, P:CTX]

    def piece(left, right):
        return np.concatenate([left[:P], left[P:], right[:P], right[P:]], axis=1)

    def head(w, h):
        return a(w)[:, h * DIM:(h + 1) * DIM].T

    wa = [piece(a(L0_xattn_Wq), a(L0_xattn_Wk)[:, twice])]
    wb = [piece(a(L0_xattn_Wv)[:, twice], a(L0_xattn_Wd).T)]
    for h in range(HEADS):
        wa.append(piece(head(L1_xattn_Wq, h), head(L1_xattn_Wk, h)[:, twice]))
        wb.append(piece(head(L1_xattn_Wv, h)[:, twice], a(L1_xattn_Wo)[h * DIM:(h + 1) * DIM]))
    ctx_t = a(ctx_768).transpose(0, 2, 1)[:, twice]

    def col(v):
        return a(v)[twice] if a(v).shape[0] == CTX else a(v)

    vectors = np.concatenate([col(v).reshape(2, P).T for v in (
        L0_xattn_bq, L0_xattn_bk, L0_xattn_bv, L0_xattn_g_q, L0_xattn_be_q, L0_xattn_g_kv, L0_xattn_be_kv)], axis=1)
    arrays = {
        "x": a(x).reshape(BATCHES * QUERIES, DIM),
        "context": a(ctx_768).reshape(BATCHES * KEYS, CTX),
        "mask": a(mask_BxS2_if1),
        "weights_a": np.stack(wa),
        "weights_b": np.stack(wb),
        "keys_t": ctx_t.reshape(BATCHES, 2, P, KEYS),
        "vectors": vectors,
        "rows": np.stack([a(L0_xattn_bd), a(L1_xattn_gamma), a(L1_xattn_beta)]),
        "identity": np.eye(P, dtype=np.float32),
    }
    nc = bacc.Bacc("TRN2", target_bir_lowering=False, num_devices=1)
    arrays = {f"in_{k}": np.ascontiguousarray(v) for k, v in arrays.items()}
    args = [nc.dram_tensor(k, v.shape, mybir.dt.from_np(v.dtype), kind="ExternalInput").ap()
            for k, v in arrays.items()]
    out = nc.dram_tensor("out_0", (BATCHES * QUERIES, DIM), mybir.dt.float32, kind="ExternalOutput").ap()
    build(nc, *args, out)
    r = run_bass_kernel_spmd(nc, [arrays], core_ids=[0])
    return r.results[0]["out_0"].reshape(BATCHES, QUERIES, DIM)
```

```python
import concourse.bass as bass
from concourse import mybir
from concourse.alu_op_type import AluOpType as ALU
from contextlib import ExitStack

P = 128
BATCHES = 2
QUERIES = 512
KEYS = 1024
DIM = 256
CTX = 192
REM = CTX - P
HEADS = 8
QT = QUERIES // P
KT = KEYS // P
DT = DIM // P
BANK = 512
EPS = 1e-5
LN_TILES = KT + QT
CTX_HALF = KT // 2
BIG = 3.0e38

C_BQ, C_BK, C_BV, N_COLS = 0, 2, 4, 6
(PC_A0, PC_B0, PC_A1, PC_KA0, PC_KR0, PC_V00, PC_V01, PC_KA1, PC_KR1, PC_V10, PC_V11) = range(11)
HI_OF = {PC_A0: 1, PC_B0: 2, PC_A1: 3, PC_KA0: 4, PC_KR0: 5, PC_V00: 7, PC_V01: 9,
         PC_KA1: 10, PC_KR1: 11, PC_V10: 13, PC_V11: 15}
(T_VEC, T_A0, T_A0b, T_Q0, T_Q0b, T_B0, T_B0b, T_OUTB, T_Q1, T_Q1b, T_A1, T_A1b, T_QH, T_QHb,
 TASKS0) = range(15)
CHUNKS = 6
X_CHUNKS = DT


def slot_no(h, j):
    return 8 * h + (8 + j)


def task_no(h, j):
    if isinstance(h, int) and h == HEADS - 1 and j >= 6:
        return TASKS0 + 8 * h + (j - 4)
    return 8 * h + (TASKS0 + j)


def pieces_a(h):
    return 2 * h + (PC_V11 + 2)


def pieces_b(h):
    if isinstance(h, int) and h == HEADS - 1:
        return 2 * h + (PC_V11 + 2)
    return 2 * h + (PC_V11 + 3)


def build(nc, x, context, mask, weights_a, weights_b, keys_t, vectors, rows, rows_kv, rows_q, identity, out):
    f32, f32r, i32 = mybir.dt.float32, mybir.dt.float32r, mybir.dt.int32
    ACT = mybir.ActivationFunctionType
    AX = mybir.AxisListType

    x_tiles = x.rearrange("(t p) d -> p t d", p=P)
    out_tiles = out.rearrange("(t p) d -> p t d", p=P)
    ctx_tiles = context.rearrange("(t p) l -> p t l", p=P)

    with ExitStack() as stack:
        def sb(name, shape, dt=f32, on=stack):
            return on.enter_context(nc.sbuf_tensor(name, shape, dt))

        def sem(name):
            return stack.enter_context(nc.semaphore(name))

        key_hi = [sb(f"key_hi{b}", [P, KEYS], f32r) for b in range(BATCHES)]
        key_lo = [sb(f"key_lo{b}", [P, KEYS], f32r) for b in range(BATCHES)]
        key_rem = [sb(f"key_rem{b}", [P, KEYS], f32r) for b in range(BATCHES)]
        val_hi = [sb(f"val_hi{b}", [P, KT, P], f32r) for b in range(BATCHES)]
        val_lo = [sb(f"val_lo{b}", [P, KT, P], f32r) for b in range(BATCHES)]
        val_rem = [sb(f"val_rem{b}", [P, KT, P], f32r) for b in range(BATCHES)]
        xt_hi = sb("xt_hi", [P, DT, BATCHES * QUERIES], f32r)
        xt_lo = sb("xt_lo", [P, DT, BATCHES * QUERIES], f32r)
        q_hi = [sb(f"q_hi{b}", [P, 2, QUERIES], f32r) for b in range(BATCHES)]
        q_lo = [sb(f"q_lo{b}", [P, 2, QUERIES], f32r) for b in range(BATCHES)]
        a_hi, a_lo = sb("a_hi", [P, DT, DIM], f32r), sb("a_lo", [P, DT, DIM], f32r)
        b_hi, b_lo = sb("b_hi", [P, 2, DIM], f32r), sb("b_lo", [P, 2, DIM], f32r)
        b_full = sb("b_full", [P, 2, DIM])
        ring = [sb(f"ring{r}", [P, 1024]) for r in range(2)]
        w_hi, w_lo = sb("w_hi", [P, 1024], f32r), sb("w_lo", [P, 1024], f32r)
        neg_scores = sb("neg_scores", [P, KEYS])
        probs = sb("probs", [P, KEYS])
        mask_bias = sb("mask_bias", [P, BATCHES, KEYS])
        resid = sb("resid", [P, BATCHES * QT, DIM])
        ident = sb("ident", [P, P])
        cols = sb("cols", [P, N_COLS])
        row_vecs = sb("row_vecs", [P, 3, DIM])
        vec = sb("vec", [P, 3])
        stats = sb("stats", [P, LN_TILES, 6])
        moments = sb("moments", [P, BATCHES * LN_TILES, 2])
        var_eps = sb("var_eps", [P, BATCHES * LN_TILES])
        rstd = sb("rstd", [P, BATCHES * LN_TILES])
        minus_half = sb("minus_half", [P, BATCHES * LN_TILES])
        row_min = sb("row_min", [P, 2 * QT])
        row_sum = sb("row_sum", [P, 2 * QT])
        row_inv = sb("row_inv", [P, 2 * QT])
        neg_shift = sb("neg_shift", [P, BATCHES * QT])
        probs_t_hi = [sb("probs_t_hi0", [P, KT, QUERIES], f32r)]
        probs_t_lo = [sb("probs_t_lo0", [P, KT, QUERIES], f32r)]
        with ExitStack() as early:
            ctx_raw = sb("ctx_raw", [P, BATCHES * KT, CTX], on=early)
            kvn = [sb("kvn0", [P, KT, 2 * P], on=early)]
            xn = sb("xn", [P, BATCHES * QT, DIM], on=early)
            kv_rows = sb("kv_rows", [P, 2, CTX], on=early)
            q_rows = sb("q_rows", [P, 2, DIM], on=early)
            ones = sb("ones", [P, P], on=early)
            kvn.append(sb("kvn1", [P, KT, 2 * P], on=early))
            neg_w_row = sb("neg_w_row", [P, DIM], on=early)
        probs_t_hi.append(sb("probs_t_hi1", [P, KT, QUERIES], f32r))
        probs_t_lo.append(sb("probs_t_lo1", [P, KT, QUERIES], f32r))
        o_hi, o_lo = sb("o_hi", [P, 2, QUERIES], f32r), sb("o_lo", [P, 2, QUERIES], f32r)
        spread = b_full[:, :, :].rearrange("p k (n q) -> p (k n) q", q=P)
        outb = row_vecs[:, 0, :]
        finals = [probs, neg_scores]

        def ps(name, width):
            return stack.enter_context(nc.psum_tensor(name, [P, width], f32))
        ps_scores = ps("ps_scores", 2 * BANK)
        ps_turn = [ps(f"ps_turn{c}", BANK) for c in range(2)]
        ps_o = [ps(f"ps_o{c}", BANK) for c in range(2)]
        ps_out = ps("ps_out", BANK)
        ps_task = ps("ps_task", BANK)

        def out_bank(idx):
            if isinstance(idx, int) and idx < 8:
                return (ps_out, ps_task)[idx % 2][:, 0:DIM]
            last = {69: ps_scores[:, 0:DIM], 70: ps_scores[:, BANK:BANK + DIM], 71: ps_turn[0][:, 0:DIM]}
            return last.get(idx, ps_out[:, 0:DIM]) if isinstance(idx, int) else ps_out[:, 0:DIM]

        def task_bank(task):
            return ps_out if isinstance(task, int) and task < TASKS0 + 6 and task % 2 else ps_task

        def chunk_bank(b, c):
            first = [ps_turn[0], ps_turn[1], ps_scores[:, 0:BANK], ps_o[0], ps_scores[:, BANK:2 * BANK], ps_o[1]]
            return ps_o[c % 2] if b else first[c]

        ring_loaded = [sem(f"ring_loaded{r}") for r in range(2)]
        ctx_loaded = [sem(f"ctx_loaded{b}") for b in range(BATCHES)]
        x_loaded = [sem(f"x_loaded{b}") for b in range(BATCHES)]
        cols_loaded = sem("cols_loaded")
        ident_loaded = sem("ident_loaded")
        ln_rows_loaded = sem("ln_rows_loaded")
        row_vecs_loaded = sem("row_vecs_loaded")
        mask_loaded = sem("mask_loaded")
        mask_made = sem("mask_made")
        stored = sem("stored")
        half_set = sem("half_set")
        ones_set = sem("ones_set")
        spread_made = sem("spread_made")
        stats_made = sem("stats_made")
        moments_made = sem("moments_made")
        var_made = sem("var_made")
        rstd_made = sem("rstd_made")
        centred = sem("centred")
        scaled = sem("scaled")
        x_normed = sem("x_normed")
        ctx_normed = [sem(f"ctx_normed{half}") for half in range(2)]
        doubled = sem("doubled")
        chunk_turned = sem("chunk_turned")
        chunk_rounded = sem("chunk_rounded")
        chunk_split = sem("chunk_split")
        piece_hi = sem("piece_hi")
        piece_split = sem("piece_split")
        vals0_hi = sem("vals0_hi")
        vals0_split = sem("vals0_split")
        vec_made = sem("vec_made")
        shift_summed = sem("shift_summed")
        shift_made = sem("shift_made")
        outb_made = sem("outb_made")
        biased = sem("biased")
        task_done = sem("task_done")
        task_hi = sem("task_hi")
        task_free = sem("task_free")
        b_scaled = sem("b_scaled")
        b_hi_made = sem("b_hi_made")
        b_split = sem("b_split")
        scored = sem("scored")
        min_made = sem("min_made")
        exped = sem("exped")
        probs_turned = sem("probs_turned")
        pt_hi_made = sem("pt_hi_made")
        pt_split = sem("pt_split")
        inv_made = sem("inv_made")
        valued = sem("valued")
        o_hi_made = sem("o_hi_made")
        o_split = sem("o_split")
        projected = sem("projected")
        added = sem("added")
        y_turned = sem("y_turned")
        y_hi_made = sem("y_hi_made")
        y_split = sem("y_split")
        fin_stats = sem("fin_stats")
        fin_moments = sem("fin_moments")
        fin_var = sem("fin_var")
        fin_rstd = sem("fin_rstd")
        fin_centred = sem("fin_centred")
        fin_made = sem("fin_made")

        block = stack.enter_context(nc.Block())

        @block.sync
        def _(sp):
            sp.dma_start(resid[:, 0:QT, :], x_tiles[:, 0:QT, :]).then_inc(x_loaded[0], 16)
            sp.dma_start(ctx_raw[:, 0:KT, :], ctx_tiles[:, 0:KT, :]).then_inc(ctx_loaded[0], 16)
            sp.dma_start(ring[0][:, :], weights_a[0]).then_inc(ring_loaded[0], 16)
            sp.dma_start(ring[1][:, :], weights_b[0]).then_inc(ring_loaded[1], 16)
            sp.dma_start(resid[:, QT:, :], x_tiles[:, QT:, :]).then_inc(x_loaded[1], 16)
            sp.dma_start(ctx_raw[:, KT:, :], ctx_tiles[:, KT:, :]).then_inc(ctx_loaded[1], 16)
            sp.dma_start(row_vecs[:, :, :], rows.partition_broadcast(P)).then_inc(row_vecs_loaded, 16)

            def piece(k, src, dst=None):
                dst = ring[k % 2][:, :] if dst is None else dst
                sp.wait_ge(piece_split, k - 1)
                sp.dma_start(dst, src).then_inc(ring_loaded[k % 2], 16)

            def values(k, b, g):
                t = b * KT + g * KT // 2
                piece(k, ctx_tiles[:, t:t + KT // 2, :],
                      ring[k % 2][:, 0:CTX * KT // 2].rearrange("p (t l) -> p t l", l=CTX))

            sp.wait_ge(task_done, T_VEC + 1)
            piece(PC_A1, weights_a[1])
            sp.dma_start(mask_bias[:, :, :].bitcast(i32), mask.partition_broadcast(P)).then_inc(mask_loaded, 16)
            sp.wait_ge(task_done, T_OUTB + 1)
            piece(PC_KA0, keys_t[0, 0])
            piece(PC_KR0, keys_t[0, 1])
            values(PC_V00, 0, 0)
            values(PC_V01, 0, 1)
            piece(PC_KA1, keys_t[1, 0])
            piece(PC_KR1, keys_t[1, 1])
            values(PC_V10, 1, 0)
            values(PC_V11, 1, 1)

            def body(h):
                if not (isinstance(h, int) and h == HEADS - 1):
                    sp.wait_ge(piece_split, pieces_a(h) - 2)
                    sp.dma_start(ring[1][:, :], weights_a[h + 2]).then_inc(ring_loaded[1], 16)
                sp.wait_ge(piece_split, 2 * h + (PC_V11 + 1))
                sp.dma_start(ring[0][:, :], weights_b[h + 1]).then_inc(ring_loaded[0], 16)

            body(0)
            with sp.Fori(1, HEADS - 1) as h:
                body(h)
            body(HEADS - 1)

            for b in range(BATCHES):
                sp.wait_ge(fin_made, QT * (b + 1))
                sp.dma_start(out_tiles[:, b * QT:(b + 1) * QT, :],
                             finals[b][:, :].rearrange("p (t d) -> p t d", t=QT)).then_inc(stored, 16)
            sp.wait_ge(stored, 16 * BATCHES)

        @block.gpsimd
        def _(pool):
            def rsqrt(b, first, end, count):
                t = slice(b * LN_TILES + first, b * LN_TILES + end)
                pool.wait_ge(var_made, count)
                nc.gpsimd.tensor_tensor(rstd[:, t], var_eps[:, t], minus_half[:, t], ALU.pow)\
                    .then_inc(rstd_made, 1)

            def bias_tiles(b, tiles, scaled_before, done):
                for i, t in enumerate(tiles):
                    dst = kvn[b][:, t, 0:CTX] if t < KT else xn[:, b * QT + t - KT, :]
                    bias = kv_rows[:, 1, :] if t < KT else q_rows[:, 1, :]
                    pool.wait_ge(scaled, scaled_before + i + 1)
                    nc.gpsimd.tensor_tensor(dst, dst, bias, ALU.add).then_inc(done, 1)

            def split_weights(hi_count, r):
                pool.wait_ge(piece_hi, hi_count)
                nc.gpsimd.tensor_tensor(w_lo[:, :], ring[r][:, :], w_hi[:, :].bitcast(f32), ALU.subtract)\
                    .then_inc(piece_split, 1)

            def split_keys(k, b):
                pool.wait_ge(piece_hi, HI_OF[k])
                nc.gpsimd.tensor_tensor(key_lo[b][:, :], ring[k % 2][:, :], key_hi[b][:, :].bitcast(f32),
                                        ALU.subtract).then_inc(piece_split, 1)
                lo = key_rem[b][REM:P, :]
                pool.wait_ge(piece_hi, HI_OF[k + 1])
                pool.wait_ge(piece_split, k + 1)
                nc.gpsimd.tensor_tensor(lo, ring[(k + 1) % 2][REM:P, :], lo.bitcast(f32), ALU.subtract)\
                    .then_inc(piece_split, 1)

            def split_values(k, b):
                pool.wait_ge(piece_split, k)
                for g in range(2):
                    src = ring[(k + g) % 2][:, 0:CTX * KT // 2].rearrange("p (t l) -> p t l", l=CTX)
                    t = slice(g * KT // 2, (g + 1) * KT // 2)
                    pool.wait_ge(piece_hi, HI_OF[k + g])
                    nc.gpsimd.tensor_tensor(val_lo[b][:, t, :], src[:, :, 0:P], val_hi[b][:, t, :].bitcast(f32),
                                            ALU.subtract)
                    nc.gpsimd.tensor_tensor(val_rem[b][:, t, REM:P], src[:, :, P:CTX],
                                            val_rem[b][:, t, 0:REM].bitcast(f32), ALU.subtract)\
                        .then_inc(piece_split, 1)

            def split_vals0(b):
                pool.wait_ge(vals0_hi, 2 * (b + 1))
                nc.gpsimd.tensor_tensor(val_lo[b][:, :, :], kvn[b][:, :, 0:P], val_hi[b][:, :, :].bitcast(f32),
                                        ALU.subtract).then_inc(vals0_split, 1)
                nc.gpsimd.tensor_tensor(val_rem[b][:, :, REM:P], kvn[b][:, :, P:CTX],
                                        val_rem[b][:, :, 0:REM].bitcast(f32), ALU.subtract).then_inc(vals0_split, 1)

            nc.gpsimd.memset(ones[:, :], 1.0).then_inc(ones_set, 1)
            nc.gpsimd.memset(minus_half[:, :], -0.5).then_inc(half_set, 1)
            pool.wait_ge(half_set, 1)
            rsqrt(0, KT, LN_TILES, 1)
            rsqrt(0, 0, KT, 2)
            split_weights(HI_OF[PC_A0], 0)
            pool.wait_ge(ln_rows_loaded, 32)
            bias_tiles(0, range(CTX_HALF, KT), 0, ctx_normed[1])
            split_weights(HI_OF[PC_B0], 1)
            rsqrt(1, KT, LN_TILES, 3)
            split_vals0(0)
            bias_tiles(1, range(KT, LN_TILES), CTX_HALF, x_normed)
            rsqrt(1, 0, KT, 4)
            bias_tiles(1, range(CTX_HALF), CTX_HALF + QT, ctx_normed[0])
            bias_tiles(1, range(CTX_HALF, KT), KT + QT, ctx_normed[1])
            split_weights(HI_OF[PC_A1], 0)
            pool.wait_ge(centred, LN_TILES + QT)
            pool.wait_ge(outb_made, 1)
            for t in range(BATCHES * QT):
                nc.gpsimd.tensor_tensor(resid[:, t, :], resid[:, t, :], outb, ALU.add)\
                    .then_inc(biased, 1)
            split_vals0(1)
            split_keys(PC_KA0, 0)
            split_values(PC_V00, 0)
            split_keys(PC_KA1, 1)
            split_values(PC_V10, 1)

            def body(h):
                if not (isinstance(h, int) and h == HEADS - 1):
                    split_weights(2 * h + (HI_OF[PC_V11] + 1), 1)
                    split_weights(2 * h + (HI_OF[PC_V11] + 2), 0)
                else:
                    split_weights(2 * h + (HI_OF[PC_V11] + 1), 0)

            with pool.Fori(0, HEADS - 1) as h:
                body(h)
            body(HEADS - 1)
            for b in range(BATCHES):
                t = slice(b * QT, (b + 1) * QT)
                pool.wait_ge(fin_var, b + 1)
                nc.gpsimd.tensor_tensor(rstd[:, t], var_eps[:, t], minus_half[:, t], ALU.pow)\
                    .then_inc(fin_rstd, 1)

        @block.tensor
        def _(pe):
            def three(dst, left, right, start, stop):
                (lh, ll), (rh, rl) = left, right
                pe.matmul(dst, lh, rh, start=start, stop=False)
                pe.matmul(dst, lh, rl, start=False, stop=False)
                return pe.matmul(dst, ll, rh, start=False, stop=stop)

            def absorb(task, m):
                dst = task_bank(task)[:, 0:DIM]
                for k in range(DT):
                    left, right = slice(k * DIM + m * P, k * DIM + (m + 1) * P), slice((DT + k) * DIM, (DT + k + 1) * DIM)
                    last = three(dst, (w_hi[:, left], w_lo[:, left]), (w_hi[:, right], w_lo[:, right]),
                                 k == 0, k == DT - 1)
                last.then_inc(task_done, 1)

            def queries(task, b, m):
                for k in range(DT):
                    s, mv = slice(m * P, (m + 1) * P), slice(b * QUERIES, (b + 1) * QUERIES)
                    last = three(task_bank(task)[:, :], (a_hi[:, k, s], a_lo[:, k, s]),
                                 (xt_hi[:, k, mv], xt_lo[:, k, mv]), k == 0, k == DT - 1)
                last.then_inc(task_done, 1)

            def scores(h, j):
                b, q = j // QT, slice((j % QT) * P, (j % QT + 1) * P)
                s = slot_no(h, j)
                if not (isinstance(s, int) and s == 0):
                    pe.wait_ge(min_made, s)
                passes = ((q_hi[b][:, 0, q], key_hi[b]), (q_hi[b][:, 0, q], key_lo[b]),
                          (q_lo[b][:, 0, q], key_hi[b]), (q_hi[b][:, 1, q], key_rem[b]),
                          (q_lo[b][:, 1, q], key_rem[b]))
                for i, (left, right) in enumerate(passes):
                    for half in range(2):
                        n = slice(half * BANK, (half + 1) * BANK)
                        last = pe.matmul(ps_scores[:, n], left, right[:, n],
                                         start=(i == 0), stop=(i == len(passes) - 1))
                last.then_inc(scored, 1)

            def turn_probs(h, j):
                s = slot_no(h, j)
                for c in range(2):
                    if c == 0:
                        pe.wait_ge(exped, s + 1)
                    if not (isinstance(s, int) and s == 0):
                        pe.wait_ge(pt_split, 2 * s + (c - 1))
                    for k in range(4):
                        kt = 4 * c + k
                        last = pe.transpose(ps_turn[c][:, k * P:(k + 1) * P],
                                            probs[:, kt * P:(kt + 1) * P], ident[:, :])
                    last.then_inc(probs_turned, 1)

            def values(h, b, c):
                if c == 0:
                    s = slot_no(h, b * QT)
                    pe.wait_ge(pt_split, 2 * s + 2 * QT)
                    if not (isinstance(s, int) and s == 0):
                        pe.wait_ge(o_split, 4 * h + (4 + 2 * b))
                hi, lo = probs_t_hi[b], probs_t_lo[b]
                for kt in (2 * c, 2 * c + 1):
                    first, end = kt == 0, kt == KT - 1
                    pe.matmul(ps_o[0][:, :], val_hi[b][:, kt, :], hi[:, kt, :], start=first, stop=False)
                    pe.matmul(ps_o[0][:, :], val_hi[b][:, kt, :], lo[:, kt, :], start=False, stop=False)
                    pe.matmul(ps_o[0][:, :], val_lo[b][:, kt, :], hi[:, kt, :], start=False, stop=end)
                    pe.matmul(ps_o[1][:, :], val_rem[b][:, kt, :], hi[:, kt, :], start=first, stop=False)
                    last = pe.matmul(ps_o[1][:, :], val_rem[b][:, kt, :], lo[:, kt, :], start=False, stop=end)
                last.then_inc(valued, 1)

            def project(h, j):
                s = slot_no(h, j)
                q = slice((j % QT) * P, (j % QT + 1) * P)
                if j % QT == 0:
                    pe.wait_ge(o_split, 4 * h + (4 + 2 * (j // QT) + 2))
                    if j == 0:
                        if isinstance(h, int) and h == -1:
                            pe.wait_ge(task_free, T_B0b + 1)
                        else:
                            pe.wait_ge(b_split, h + 1)
                if isinstance(s, int) and s in (69, 70, 71):
                    pass
                elif isinstance(s, int) and s < 8:
                    if s == 0:
                        pe.wait_ge(task_free, T_A1b + 1)
                    elif s >= 2:
                        pe.wait_ge(added, s - 1)
                else:
                    pe.wait_ge(added, s)
                dst = out_bank(s)
                for k in range(2):
                    last = three(dst, (o_hi[:, k, q], o_lo[:, k, q]), (b_hi[:, k, :], b_lo[:, k, :]),
                                 k == 0, k == 1)
                last.then_inc(projected, 1)

            def turn_y(b):
                pe.wait_ge(added, QT * (b + 1))
                for c in range(DT):
                    for t in range(QT):
                        last = pe.transpose(ps_o[c][:, t * P:(t + 1) * P],
                                            resid[:, b * QT + t, c * P:(c + 1) * P], ident[:, :])
                    last.then_inc(y_turned, 1)

            def turn_chunk(b, c):
                i = CHUNKS * b + c
                if c < X_CHUNKS:
                    src = [xn[:, b * QT + t, c * P:(c + 1) * P] for t in range(QT)]
                    pe.wait_ge(x_normed, QT * (b + 1))
                else:
                    half, f = (c - X_CHUNKS) // 2, (c - X_CHUNKS) % 2
                    src = [kvn[b][:, half * CTX_HALF + t, f * P:(f + 1) * P] for t in range(CTX_HALF)]
                    if f == 0:
                        pe.wait_ge(ctx_normed[half], CTX_HALF * (b + 1))
                    else:
                        pe.wait_ge(doubled, 2 * b + half + 1)
                if b:
                    pe.wait_ge(chunk_split, i - 1 if c >= 2 else CHUNKS)
                dst = chunk_bank(b, c)
                for t in range(4):
                    last = pe.transpose(dst[:, t * P:(t + 1) * P], src[t], ident[:, :])
                last.then_inc(chunk_turned, 1)

            def free(task):
                if task >= 2:
                    pe.wait_ge(task_free, task - 1)

            pe.wait_ge(spread_made, DT)
            pe.wait_ge(ring_loaded[0], 16)
            raw = ring[0]
            for k in range(DT):
                pe.matmul(ps_task[:, DIM:2 * DIM], spread[:, k, :], raw[:, k * DIM:(k + 1) * DIM],
                          start=(k == 0), stop=(k == DT - 1))
            for n in range(3):
                for k in range(DT):
                    left = spread[:, k, :] if n == 2 else raw[:, (DT + k) * DIM + n * P:(DT + k) * DIM + (n + 1) * P]
                    last = pe.matmul(ps_task[:, n:n + 1], left, cols[:, C_BQ + k:C_BQ + k + 1],
                                     start=(k == 0), stop=(k == DT - 1))
            last.then_inc(task_done, 1)
            pe.wait_ge(ident_loaded, 16)
            for c in range(X_CHUNKS):
                turn_chunk(0, c)
            pe.wait_ge(piece_split, PC_A0 + 1)
            absorb(T_A0, 0)
            pe.wait_ge(vec_made, 1)
            free(T_A0b)
            absorb(T_A0b, 1)
            for c in range(X_CHUNKS, X_CHUNKS + 2):
                turn_chunk(0, c)
            pe.wait_ge(chunk_split, X_CHUNKS)
            pe.wait_ge(task_free, T_A0b + 1)
            queries(T_Q0, 0, 0)
            queries(T_Q0b, 0, 1)
            for c in range(X_CHUNKS + 2, CHUNKS):
                turn_chunk(0, c)

            pe.wait_ge(task_free, T_Q0b + 1)
            pe.wait_ge(chunk_split, CHUNKS)
            scores(-1, 0)
            pe.wait_ge(piece_split, PC_B0 + 1)
            absorb(T_B0, 0)
            absorb(T_B0b, 1)
            turn_probs(-1, 0)
            scores(-1, 1)
            free(T_OUTB)
            pe.wait_ge(spread_made, 2 * DT)
            raw = ring[1]
            for k in range(DT):
                last = pe.matmul(ps_out[:, 0:DIM], spread[:, DT + k, :], raw[:, (DT + k) * DIM:(DT + k + 1) * DIM],
                                 start=(k == 0), stop=(k == DT - 1))
            last.then_inc(task_done, 1)
            turn_probs(-1, 1)
            scores(-1, 2)
            turn_chunk(1, 0)
            turn_chunk(1, 1)
            turn_probs(-1, 2)
            scores(-1, 3)
            turn_chunk(1, 2)
            turn_chunk(1, 3)
            free(T_Q1)
            queries(T_Q1, 1, 0)
            turn_chunk(1, 4)
            turn_chunk(1, 5)
            free(T_Q1b)
            queries(T_Q1b, 1, 1)

            for j in range(QT):
                turn_probs(-1, QT + j - 1)
                if j == 0:
                    pe.wait_ge(task_free, T_Q1b + 1)
                    pe.wait_ge(chunk_split, 2 * CHUNKS)
                scores(-1, QT + j)
                if j < 2:
                    if j == 0:
                        pe.wait_ge(piece_split, PC_A1 + 1)
                        pe.wait_ge(vals0_split, 2)
                    free(T_A1 + j)
                    absorb(T_A1 + j, j)
                    values(-1, 0, 2 * j)
                    values(-1, 0, 2 * j + 1)
                elif j == 2:
                    for t in range(QT):
                        project(-1, t)
                else:
                    turn_y(0)
            pe.wait_ge(y_split, DT)
            queries(T_QH, 0, 0)
            queries(T_QHb, 0, 1)
            turn_probs(-1, 7)
            pe.wait_ge(vals0_split, 4)
            values(-1, 1, 0)

            def first_body():
                for j in range(2 * QT):
                    if j > 0:
                        turn_probs(0, j - 1)
                    if j == 0:
                        pe.wait_ge(piece_split, PC_KR0 + 1)
                        pe.wait_ge(task_free, T_QHb + 1)
                    if j == 3:
                        turn_y(1)
                    if j == QT:
                        pe.wait_ge(piece_split, PC_V11 + 1)
                        pe.wait_ge(task_free, task_no(0, 2))
                    scores(0, j)
                    if j == 0:
                        values(-1, 1, 1)
                        values(-1, 1, 2)
                    if j == 1:
                        values(-1, 1, 3)
                    if j == 2:
                        for t in range(QT, 2 * QT):
                            project(-1, t)
                    if j == 3:
                        pe.wait_ge(y_split, 2 * DT)
                        queries(task_no(0, 0), 1, 0)
                        queries(task_no(0, 1), 1, 1)
                    if j == 4:
                        pe.wait_ge(piece_split, pieces_a(0))
                        pe.wait_ge(task_free, task_no(0, 2))
                        absorb(task_no(0, 2), 0)
                    if j == 5:
                        pe.wait_ge(task_free, task_no(0, 4))
                        queries(task_no(0, 4), 0, 0)
                    if j >= 6:
                        if j == 6:
                            pe.wait_ge(piece_split, pieces_b(0))
                        pe.wait_ge(task_free, task_no(0, j))
                        absorb(task_no(0, j), j - 6)
                    if j >= QT:
                        values(0, 0, j - QT)
                    if j == 4:
                        absorb(task_no(0, 3), 1)
                    if j == 5:
                        queries(task_no(0, 5), 0, 1)

            def body(h):
                last_head = isinstance(h, int) and h == HEADS - 1
                for j in range(2 * QT):
                    b = j // QT
                    if j > 0:
                        turn_probs(h, j - 1)
                    else:
                        turn_probs(h - 1, 2 * QT - 1)
                    if j % QT == 0:
                        pe.wait_ge(task_free, task_no(h, -2 if j == 0 else 2))
                    scores(h, j)
                    if not (last_head and 2 <= j < 6):
                        pe.wait_ge(task_free, task_no(h, j))
                        if j < 2:
                            queries(None, 1, j)
                        elif j < 4:
                            if j == 2:
                                pe.wait_ge(piece_split, pieces_a(h))
                            absorb(None, j - 2)
                        elif j < 6:
                            queries(None, 0, j - 4)
                        else:
                            if j == 6:
                                pe.wait_ge(piece_split, pieces_b(h))
                            absorb(None, j - 6)
                    if b == 1:
                        values(h, 0, j - QT)
                    else:
                        values(h - 1, 1, j)
                    project(h - 1, j)

            first_body()
            with pe.Fori(1, HEADS - 1) as h:
                body(h)
            body(HEADS - 1)
            turn_probs(HEADS - 1, 2 * QT - 1)
            for c in range(QT):
                values(HEADS - 1, 1, c)
                project(HEADS - 1, c)
            for c in range(QT):
                project(HEADS - 1, QT + c)

        @block.scalar
        def _(act):
            act.dma_start(cols[:, :], vectors).then_inc(cols_loaded, 16)
            act.dma_start(kv_rows[:, :, :], rows_kv.partition_broadcast(P)).then_inc(ln_rows_loaded, 16)
            act.dma_start(q_rows[:, :, :], rows_q.partition_broadcast(P)).then_inc(ln_rows_loaded, 16)
            act.dma_start(ident[:, :], identity).then_inc(ident_loaded, 16)

            def exp(h, j):
                s = slot_no(h, j)
                if not (isinstance(s, int) and s == 0):
                    act.wait_ge(probs_turned, 2 * s)
                act.wait_ge(min_made, s + 1)
                act.activation(probs[:, :], neg_scores[:, :], ACT.Exp, bias=row_min[:, j:j + 1],
                               scale=-1.0, accum_out=row_sum[:, j:j + 1]).then_inc(exped, 1)

            def round_probs(h, j):
                s, b = slot_no(h, j), j // QT
                if j % QT == 0 and not (isinstance(s, int) and s < 8):
                    act.wait_ge(valued, s - 4)
                q = slice((j % QT) * P, (j % QT + 1) * P)
                for c in range(2):
                    act.wait_ge(probs_turned, 2 * s + (c + 1))
                    act.activation(probs_t_hi[b][:, 4 * c:4 * c + 4, q],
                                   ps_turn[c][:, :].rearrange("p (k q) -> p k q", k=4), ACT.Copy)\
                        .then_inc(pt_hi_made, 1)

            def round_outputs(h, b):
                s = slot_no(h, b * QT)
                act.wait_ge(valued, s + 4)
                if isinstance(s, int) and s == 0:
                    act.wait_ge(vals0_split, 4)
                else:
                    act.wait_ge(projected, s)
                for k in range(2):
                    act.activation(o_hi[:, k, :], ps_o[k][:, :], ACT.Copy).then_inc(o_hi_made, 1)

            def round_a(task, m, scale):
                act.wait_ge(task_done, task + 1)
                act.activation(a_hi[:, m, :], task_bank(task)[:, 0:DIM], ACT.Copy, scale=scale).then_inc(task_hi, 1)

            def round_b(task, m):
                act.wait_ge(task_done, task + 1)
                act.activation(b_hi[:, m, :], task_bank(task)[:, 0:DIM], ACT.Copy).then_inc(task_hi, 1)

            def round_queries(task, b, m, layer):
                act.wait_ge(task_done, task + 1)
                if layer:
                    act.activation(q_hi[b][:, m, :], task_bank(task)[:, :], ACT.Copy).then_inc(task_hi, 1)
                else:
                    act.activation(q_hi[b][:, m, :], task_bank(task)[:, :], ACT.Identity,
                                   bias=vec[:, m:m + 1]).then_inc(task_hi, 1)

            def keep_b(task, m):
                act.wait_ge(task_done, task + 1)
                act.activation(b_full[:, m, :], ps_task[:, 0:DIM], ACT.Copy).then_inc(task_free, 1)

            def round_weights(loaded, r):
                act.wait_ge(ring_loaded[r], loaded)
                act.activation(w_hi[:, :], ring[r][:, :], ACT.Copy).then_inc(piece_hi, 1)

            def round_keys(k, b):
                act.wait_ge(scored, 4 * (b + 1))
                act.wait_ge(ring_loaded[k % 2], 16 * (k // 2 + 1))
                act.activation(key_hi[b][:, :], ring[k % 2][:, :], ACT.Copy).then_inc(piece_hi, 1)
                k += 1
                act.wait_ge(ring_loaded[k % 2], 16 * (k // 2 + 1))
                act.activation(key_rem[b][:, :], ring[k % 2][:, :], ACT.Copy).then_inc(piece_hi, 1)

            def round_values(k, b):
                act.wait_ge(valued, 4 * (b + 1))
                for g in range(2):
                    src = ring[(k + g) % 2][:, 0:CTX * KT // 2].rearrange("p (t l) -> p t l", l=CTX)
                    t = slice(g * KT // 2, (g + 1) * KT // 2)
                    act.wait_ge(ring_loaded[(k + g) % 2], 16 * ((k + g) // 2 + 1))
                    act.activation(val_hi[b][:, t, :], src[:, :, 0:P], ACT.Copy).then_inc(piece_hi, 1)
                    act.activation(val_rem[b][:, t, 0:REM], src[:, :, P:CTX], ACT.Copy).then_inc(piece_hi, 1)

            def scale_tiles(b, tiles, rstds):
                act.wait_ge(rstd_made, rstds)
                for t in tiles:
                    n = b * LN_TILES + t
                    dst = kvn[b][:, t, 0:CTX] if t < KT else xn[:, b * QT + t - KT, :]
                    act.wait_ge(centred, b * LN_TILES + (t + QT if t < KT else t - KT) + 1)
                    act.activation(dst, dst, ACT.Copy, scale=rstd[:, n:n + 1]).then_inc(scaled, 1)

            def double_context(b, half):
                t = slice(half * CTX_HALF, (half + 1) * CTX_HALF)
                act.wait_ge(ctx_normed[half], CTX_HALF * (b + 1))
                act.activation(kvn[b][:, t, CTX:2 * P], kvn[b][:, t, P:CTX], ACT.Copy).then_inc(doubled, 1)

            def round_chunk(b, c):
                if c < X_CHUNKS:
                    dst = xt_hi[:, c, b * QUERIES:(b + 1) * QUERIES]
                else:
                    half, f = (c - X_CHUNKS) // 2, (c - X_CHUNKS) % 2
                    dst = (key_rem if f else key_hi)[b][:, half * BANK:(half + 1) * BANK]
                act.wait_ge(chunk_turned, CHUNKS * b + c + 1)
                act.activation(dst, chunk_bank(b, c)[:, 0:BANK], ACT.Copy).then_inc(chunk_rounded, 1)

            def round_vals0(b):
                act.activation(val_hi[b][:, :, :], kvn[b][:, :, 0:P], ACT.Copy).then_inc(vals0_hi, 1)
                act.activation(val_rem[b][:, :, 0:REM], kvn[b][:, :, P:CTX], ACT.Copy).then_inc(vals0_hi, 1)

            def round_y(b):
                for c in range(DT):
                    act.wait_ge(y_turned, DT * b + c + 1)
                    act.activation(xt_hi[:, c, b * QUERIES:(b + 1) * QUERIES], ps_o[c][:, :], ACT.Copy)\
                        .then_inc(y_hi_made, 1)

            act.wait_ge(ones_set, 1)
            act.wait_ge(cols_loaded, 16)
            for n in range(2 * DT):
                act.activation(spread[:, n, :], ones[:, :], ACT.Copy, scale=cols[:, C_BK + n:C_BK + n + 1])\
                    .then_inc(spread_made, 1)
            round_weights(16, 0)
            for c in range(X_CHUNKS):
                round_chunk(0, c)
            scale_tiles(0, range(CTX_HALF, KT), 2)
            round_a(T_A0, 0, -1.0)
            round_a(T_A0b, 1, -1.0)
            double_context(0, 0)
            round_chunk(0, 2)
            double_context(0, 1)
            round_chunk(0, 3)
            round_weights(16, 1)
            act.wait_ge(vec_made, 1)
            round_queries(T_Q0, 0, 0, 0)
            round_queries(T_Q0b, 0, 1, 0)
            round_chunk(0, 4)
            round_chunk(0, 5)
            exp(-1, 0)
            round_b(T_B0, 0)
            round_b(T_B0b, 1)
            round_probs(-1, 0)
            exp(-1, 1)
            round_vals0(0)
            scale_tiles(1, range(KT, LN_TILES), 3)
            round_probs(-1, 1)
            exp(-1, 2)
            round_chunk(1, 0)
            round_chunk(1, 1)
            scale_tiles(1, range(KT), 4)
            round_weights(32, 0)
            round_probs(-1, 2)
            double_context(1, 0)
            exp(-1, 3)
            double_context(1, 1)
            round_chunk(1, 2)
            round_chunk(1, 3)
            round_queries(T_Q1, 1, 0, 0)
            round_chunk(1, 4)
            round_chunk(1, 5)
            round_queries(T_Q1b, 1, 1, 0)
            for j in range(QT):
                round_probs(-1, QT + j - 1)
                exp(-1, QT + j)
                if j == 0:
                    round_vals0(1)
                if j < 2:
                    round_a(T_A1 + j, j, -1.0 / 16)
                if j == 1:
                    round_keys(PC_KA0, 0)
                    round_outputs(-1, 0)
                if j == 2:
                    round_values(PC_V00, 0)
            round_y(0)
            round_queries(T_QH, 0, 0, 1)
            round_queries(T_QHb, 0, 1, 1)
            round_probs(-1, 7)

            def first_body():
                for j in range(2 * QT):
                    if j > 0:
                        round_probs(0, j - 1)
                    if j == 3:
                        round_y(1)
                    exp(0, j)
                    if j == 0:
                        round_keys(PC_KA1, 1)
                    if j == 1:
                        round_outputs(-1, 1)
                    if j == 2:
                        round_values(PC_V10, 1)
                    if j == 3:
                        round_weights(16 * (PC_V11 // 2 + 1), 1)
                        round_queries(task_no(0, 0), 1, 0, 1)
                        round_queries(task_no(0, 1), 1, 1, 1)
                    if j == 4:
                        round_a(task_no(0, 2), 0, -1.0 / 16)
                        round_a(task_no(0, 3), 1, -1.0 / 16)
                    if j == 5:
                        round_weights(16 * (PC_V11 // 2 + 2), 0)
                        round_queries(task_no(0, 4), 0, 0, 1)
                        round_queries(task_no(0, 5), 0, 1, 1)
                    if j >= 6:
                        keep_b(task_no(0, j), j - 6)
                round_outputs(0, 0)

            def body(h):
                last_head = isinstance(h, int) and h == HEADS - 1
                for j in range(2 * QT):
                    if j > 0:
                        round_probs(h, j - 1)
                    else:
                        round_probs(h - 1, 2 * QT - 1)
                    exp(h, j)
                    if not (last_head and 2 <= j < 6):
                        task = task_no(h, j)
                        if j < 2:
                            round_queries(task, 1, j, 1)
                        elif j < 4:
                            round_a(task, j - 2, -1.0 / 16)
                        elif j < 6:
                            round_queries(task, 0, j - 4, 1)
                        else:
                            if j == 6:
                                act.wait_ge(b_split, h)
                            keep_b(task, j - 6)
                    if j == 1 and not last_head:
                        act.wait_ge(task_done, task_no(h, 0))
                        round_weights(16 * h + 16 * (PC_V11 // 2 + 1), 1)
                    if j == 3:
                        act.wait_ge(task_done, task_no(h, 4) if not last_head else TASKS0 + 8 * h + 2)
                        round_weights(16 * h + 16 * (PC_V11 // 2 + 2), 0)
                        round_outputs(h - 1, 1)
                    if j == 2 * QT - 1:
                        round_outputs(h, 0)

            first_body()
            with act.Fori(1, HEADS - 1) as h:
                body(h)
            body(HEADS - 1)
            round_probs(HEADS - 1, 2 * QT - 1)
            round_outputs(HEADS - 1, 1)

        @block.vector
        def _(dve):
            def invert(j):
                dve.reciprocal(row_inv[:, j:j + 1], row_sum[:, j:j + 1]).then_inc(inv_made, 1)

            def minimum(h, j, layer):
                s, b = slot_no(h, j), j // QT
                if not (isinstance(s, int) and s == 0):
                    dve.wait_ge(exped, s)
                if not (isinstance(s, int) and s <= 8):
                    dve.wait_ge(added, s - 8)
                dve.wait_ge(scored, s + 1)
                if not (isinstance(s, int) and s in (0, 8)):
                    invert((j - 1) % (2 * QT))
                if layer:
                    dve.wait_ge(mask_made, 2)
                    dve.tensor_tensor_reduce(
                        out=neg_scores[:, :], in0=ps_scores[:, :], in1=mask_bias[:, b, :], scale=1.0, scalar=BIG,
                        op0=ALU.add, op1=ALU.min, accum_out=row_min[:, j:j + 1]).then_inc(min_made, 1)
                else:
                    dve.wait_ge(shift_made, b + 1)
                    dve.tensor_scalar(neg_scores[:, :], ps_scores[:, :], neg_shift[:, j:j + 1], None,
                                      ALU.add, ALU.min, accum_out=row_min[:, j:j + 1]).then_inc(min_made, 1)

            def split_probs(h, j):
                s, b = slot_no(h, j), j // QT
                q = slice((j % QT) * P, (j % QT + 1) * P)
                for c in range(2):
                    dve.wait_ge(pt_hi_made, 2 * s + (c + 1))
                    dve.tensor_tensor(probs_t_lo[b][:, 4 * c:4 * c + 4, q],
                                      ps_turn[c][:, :].rearrange("p (k q) -> p k q", k=4),
                                      probs_t_hi[b][:, 4 * c:4 * c + 4, q].bitcast(f32), ALU.subtract)\
                        .then_inc(pt_split, 1)

            def split_outputs(h, b):
                n2 = 4 * h + (4 + 2 * b)
                for k in range(2):
                    dve.wait_ge(o_hi_made, n2 + (k + 1))
                    dve.tensor_tensor(o_lo[:, k, :], ps_o[k][:, :], o_hi[:, k, :].bitcast(f32), ALU.subtract)\
                        .then_inc(o_split, 1)

            def split_a(task, m, scale):
                dve.wait_ge(task_hi, hi_before(task) + 1)
                dve.scalar_tensor_tensor(a_lo[:, m, :], task_bank(task)[:, 0:DIM], scale,
                                         a_hi[:, m, :].bitcast(f32), ALU.mult, ALU.subtract).then_inc(task_free, 1)

            def split_b0(task, m):
                dve.wait_ge(task_hi, hi_before(task) + 1)
                dve.tensor_tensor(b_lo[:, m, :], task_bank(task)[:, 0:DIM], b_hi[:, m, :].bitcast(f32), ALU.subtract)\
                    .then_inc(task_free, 1)

            def split_queries(task, b, m, layer):
                dve.wait_ge(task_hi, hi_before(task) + 1)
                hi = q_hi[b][:, m, :].bitcast(f32)
                if layer:
                    dve.tensor_tensor(q_lo[b][:, m, :], task_bank(task)[:, :], hi, ALU.subtract).then_inc(task_free, 1)
                else:
                    dve.scalar_tensor_tensor(q_lo[b][:, m, :], task_bank(task)[:, :], vec[:, m:m + 1], hi,
                                             ALU.add, ALU.subtract).then_inc(task_free, 1)

            def hi_before(task):
                return task - (1 if task > T_VEC else 0) - (1 if task > T_OUTB else 0)

            def split_b(count):
                dve.tensor_copy(b_hi[:, :, :], b_full[:, :, :]).then_inc(b_hi_made, 1)
                dve.wait_ge(b_hi_made, count)
                dve.tensor_tensor(b_lo[:, :, :], b_full[:, :, :], b_hi[:, :, :].bitcast(f32), ALU.subtract)\
                    .then_inc(b_split, 1)

            def add(h, j):
                s = slot_no(h, j)
                if isinstance(s, int) and s < 8:
                    dve.wait_ge(biased, j + 1)
                    dve.wait_ge(inv_made, s + 1)
                else:
                    dve.wait_ge(added, s - 7)
                dve.wait_ge(projected, s + 1)
                dve.scalar_tensor_tensor(resid[:, j, :], out_bank(s), row_inv[:, j:j + 1], resid[:, j, :],
                                         ALU.mult, ALU.add).then_inc(added, 1)

            def ln_stats(b, first, end, loaded):
                dve.wait_ge(loaded, 16)
                for t in range(first, end):
                    if b == 1:
                        dve.wait_ge(moments_made, LN_TILES)
                    src = ctx_raw[:, b * KT + t, :] if t < KT else resid[:, b * QT + t - KT, :]
                    dve.bn_stats(stats[:, t, :], src).then_inc(stats_made, 1)
                done = b * LN_TILES + (QT if first == 0 else 0)
                for i, t in enumerate(range(first, end)):
                    dve.wait_ge(stats_made, done + i + 1)
                    dve.bn_aggr(moments[:, b * LN_TILES + t, :], stats[:, t, :]).then_inc(moments_made, 1)
                n = slice(b * LN_TILES + first, b * LN_TILES + end)
                dve.wait_ge(moments_made, done + end - first)
                dve.tensor_scalar(var_eps[:, n], moments[:, n, 1], EPS, None, ALU.add).then_inc(var_made, 1)

            def ln_centre(b, tiles):
                for t in tiles:
                    n = b * LN_TILES + t
                    if t < KT:
                        dst, src, gain = kvn[b][:, t, 0:CTX], ctx_raw[:, b * KT + t, :], kv_rows[:, 0, :]
                    else:
                        x_tile = b * QT + t - KT
                        dst, src, gain = xn[:, x_tile, :], resid[:, x_tile, :], q_rows[:, 0, :]
                    dve.scalar_tensor_tensor(dst, src, moments[:, n, 0:1], gain, ALU.subtract, ALU.mult)\
                        .then_inc(centred, 1)

            def ln_scale(tiles, done):
                for t in tiles:
                    dst = kvn[0][:, t, 0:CTX] if t < KT else xn[:, t - KT, :]
                    bias = kv_rows[:, 1, :] if t < KT else q_rows[:, 1, :]
                    dve.wait_ge(centred, (t + QT if t < KT else t - KT) + 1)
                    dve.scalar_tensor_tensor(dst, dst, rstd[:, t:t + 1], bias, ALU.mult, ALU.add).then_inc(done, 1)

            def split_chunk(b, c):
                src = chunk_bank(b, c)
                dve.wait_ge(chunk_rounded, CHUNKS * b + c + 1)
                if c < X_CHUNKS:
                    q = slice(b * QUERIES, (b + 1) * QUERIES)
                    dve.tensor_tensor(xt_lo[:, c, q], src[:, 0:BANK], xt_hi[:, c, q].bitcast(f32), ALU.subtract)\
                        .then_inc(chunk_split, 1)
                    return
                half, f = (c - X_CHUNKS) // 2, (c - X_CHUNKS) % 2
                n = slice(half * BANK, (half + 1) * BANK)
                if f == 0:
                    dve.tensor_tensor(key_lo[b][:, n], src[:, 0:BANK], key_hi[b][:, n].bitcast(f32), ALU.subtract)\
                        .then_inc(chunk_split, 1)
                else:
                    dve.tensor_tensor(key_rem[b][REM:P, n], src[REM:P, 0:BANK], key_rem[b][REM:P, n].bitcast(f32),
                                      ALU.subtract).then_inc(chunk_split, 1)

            def shift(b):
                halves = "p (n q) -> p n q"
                dve.wait_ge(x_normed, QT * (b + 1))
                dve.wait_ge(centred, (b + 1) * LN_TILES)
                for t in range(QT):
                    n = b * QT + t
                    spare = ctx_raw[:, b * KT + 2 * t:b * KT + 2 * t + 2, 0:P]
                    dve.tensor_tensor_reduce(
                        out=spare, in0=xn[:, n, :].rearrange(halves, n=2), in1=neg_w_row[:, :].rearrange(halves, n=2),
                        scale=1.0, scalar=0.0, op0=ALU.mult, op1=ALU.add, accum_out=neg_shift[:, n:n + 1])\
                        .then_inc(shift_summed, 1)
                t = slice(b * QT, (b + 1) * QT)
                dve.wait_ge(shift_summed, QT * (b + 1))
                dve.tensor_scalar(neg_shift[:, t], neg_shift[:, t], vec[:, 2:3], None, ALU.add).then_inc(shift_made, 1)

            def split_y(b):
                q = slice(b * QUERIES, (b + 1) * QUERIES)
                for c in range(DT):
                    dve.wait_ge(y_hi_made, DT * b + c + 1)
                    dve.tensor_tensor(xt_lo[:, c, q], ps_o[c][:, :], xt_hi[:, c, q].bitcast(f32), ALU.subtract)\
                        .then_inc(y_split, 1)

            x_tiles_, first_half = range(KT, LN_TILES), range(CTX_HALF)
            ln_stats(0, KT, LN_TILES, x_loaded[0])
            ln_stats(0, 0, KT, ctx_loaded[0])
            dve.wait_ge(ln_rows_loaded, 32)
            ln_centre(0, x_tiles_)
            dve.wait_ge(rstd_made, 1)
            ln_scale(x_tiles_, x_normed)
            ln_centre(0, range(KT))
            dve.wait_ge(task_done, T_VEC + 1)
            dve.tensor_scalar(vec[:, :], ps_task[:, 0:3], -1.0, None, ALU.mult).then_inc(vec_made, 1)
            dve.tensor_scalar(neg_w_row[:, :], ps_task[:, DIM:2 * DIM], -1.0, None, ALU.mult).then_inc(task_free, 1)
            dve.wait_ge(rstd_made, 2)
            ln_scale(first_half, ctx_normed[0])
            for c in range(X_CHUNKS):
                split_chunk(0, c)
            split_a(T_A0, 0, -1.0)
            split_a(T_A0b, 1, -1.0)
            split_chunk(0, 2)
            split_chunk(0, 3)
            dve.wait_ge(task_free, T_VEC + 1)
            shift(0)
            split_queries(T_Q0, 0, 0, 0)
            split_queries(T_Q0b, 0, 1, 0)
            split_chunk(0, 4)
            split_chunk(0, 5)
            minimum(-1, 0, 0)
            ln_stats(1, KT, LN_TILES, x_loaded[1])
            split_b0(T_B0, 0)
            split_b0(T_B0b, 1)
            split_probs(-1, 0)
            minimum(-1, 1, 0)
            ln_centre(1, x_tiles_)
            ln_stats(1, 0, KT, ctx_loaded[1])
            split_probs(-1, 1)
            minimum(-1, 2, 0)
            dve.wait_ge(row_vecs_loaded, 16)
            dve.wait_ge(task_done, T_OUTB + 1)
            dve.tensor_tensor(outb, ps_out[:, 0:DIM], outb, ALU.add).then_inc(outb_made, 1)
            dve.wait_ge(outb_made, 1)
            dve.engine_nop().then_inc(task_free, 1)
            ln_centre(1, range(KT))
            split_chunk(1, 0)
            split_chunk(1, 1)
            split_probs(-1, 2)
            minimum(-1, 3, 0)
            shift(1)
            split_chunk(1, 2)
            split_chunk(1, 3)
            split_queries(T_Q1, 1, 0, 0)
            split_chunk(1, 4)
            split_chunk(1, 5)
            split_queries(T_Q1b, 1, 1, 0)
            for j in range(QT):
                split_probs(-1, QT + j - 1)
                minimum(-1, QT + j, 0)
                if j < 2:
                    split_a(T_A1 + j, j, -1.0 / 16)
                if j == 0:
                    dve.wait_ge(mask_loaded, 16)
                    dve.tensor_scalar(mask_bias[:, :, :], mask_bias[:, :, :].bitcast(i32), 0.0, BIG,
                                      ALU.is_equal, ALU.mult).then_inc(mask_made, 1)
                if j == 1:
                    dve.wait_ge(mask_made, 1)
                    dve.tensor_scalar(mask_bias[:, :, :], mask_bias[:, :, :], 10.0, None, ALU.mult)\
                        .then_inc(mask_made, 1)
                    split_outputs(-1, 0)
                if j == 2:
                    for t in range(QT):
                        add(-1, t)
            split_y(0)
            split_queries(T_QH, 0, 0, 1)
            split_queries(T_QHb, 0, 1, 1)
            split_probs(-1, 7)
            invert(7)

            def split_task(h, j):
                bank = task_bank(task_no(h, j))
                if isinstance(h, int):
                    dve.wait_ge(task_hi, 6 * h + HI0 + j + 1)
                else:
                    dve.wait_ge(task_hi, 6 * h + (HI0 + j + 1))
                if j in (2, 3):
                    dve.scalar_tensor_tensor(a_lo[:, j - 2, :], bank[:, 0:DIM], -1.0 / 16,
                                             a_hi[:, j - 2, :].bitcast(f32), ALU.mult, ALU.subtract)\
                        .then_inc(task_free, 1)
                else:
                    b, m = (1, j) if j < 2 else (0, j - 4)
                    dve.tensor_tensor(q_lo[b][:, m, :], bank[:, :], q_hi[b][:, m, :].bitcast(f32),
                                      ALU.subtract).then_inc(task_free, 1)

            HI0 = hi_before(TASKS0)

            def first_body():
                for j in range(2 * QT):
                    if j > 0:
                        split_probs(0, j - 1)
                    if j == 3:
                        split_y(1)
                    minimum(0, j, 1)
                    if j == 1:
                        split_outputs(-1, 1)
                    if j == 2:
                        for t in range(QT, 2 * QT):
                            add(-1, t)
                    if j in (3, 4, 5):
                        split_task(0, 2 * (j - 3))
                        split_task(0, 2 * (j - 3) + 1)
                split_outputs(0, 0)
                dve.wait_ge(projected, 8)
                dve.wait_ge(task_free, task_no(0, 8))
                split_b(1)

            def body(h):
                last_head = isinstance(h, int) and h == HEADS - 1
                for j in range(2 * QT):
                    if j > 0:
                        split_probs(h, j - 1)
                    else:
                        split_probs(h - 1, 2 * QT - 1)
                    minimum(h, j, 1)
                    if j < (2 if last_head else 6):
                        split_task(h, j)
                    add(h - 1, j)
                    if j == 3:
                        split_outputs(h - 1, 1)
                    if j == 2 * QT - 1:
                        split_outputs(h, 0)
                        dve.wait_ge(projected, 8 * h + 8)
                        dve.wait_ge(task_free, task_no(h, 8) if not last_head else TASKS0 + 8 * h + 4)
                        split_b(h + 1)

            first_body()
            with dve.Fori(1, HEADS - 1) as h:
                body(h)
            body(HEADS - 1)
            split_probs(HEADS - 1, 2 * QT - 1)
            invert(2 * QT - 1)
            for j in range(QT):
                add(HEADS - 1, j)
            split_outputs(HEADS - 1, 1)

            def final(b):
                for t in range(QT):
                    n = b * QT + t
                    if b == 1:
                        add(HEADS - 1, n)
                    dve.wait_ge(added, 8 * HEADS + n + 1)
                    dve.bn_stats(stats[:, n, :], resid[:, n, :]).then_inc(fin_stats, 1)
                for t in range(QT):
                    n = b * QT + t
                    dve.wait_ge(fin_stats, n + 1)
                    dve.bn_aggr(moments[:, n, :], stats[:, n, :]).then_inc(fin_moments, 1)
                n = slice(b * QT, (b + 1) * QT)
                dve.wait_ge(fin_moments, (b + 1) * QT)
                dve.tensor_scalar(var_eps[:, n], moments[:, n, 1], EPS, None, ALU.add).then_inc(fin_var, 1)
                for t in range(QT):
                    n = b * QT + t
                    dve.scalar_tensor_tensor(resid[:, n, :], resid[:, n, :], moments[:, n, 0:1], row_vecs[:, 1, :],
                                             ALU.subtract, ALU.mult).then_inc(fin_centred, 1)
                dve.wait_ge(fin_rstd, b + 1)
                for t in range(QT):
                    n = b * QT + t
                    dve.wait_ge(fin_centred, n + 1)
                    dve.scalar_tensor_tensor(finals[b][:, t * DIM:(t + 1) * DIM], resid[:, n, :], rstd[:, n:n + 1],
                                             row_vecs[:, 2, :], ALU.mult, ALU.add).then_inc(fin_made, 1)

            final(0)
            final(1)


def kernel(x, ctx_768, mask_BxS2_if1, L0_xattn_Wq, L0_xattn_bq, L0_xattn_Wk, L0_xattn_bk, L0_xattn_Wv,
           L0_xattn_bv, L0_xattn_Wd, L0_xattn_bd, L0_xattn_g_q, L0_xattn_be_q, L0_xattn_g_kv, L0_xattn_be_kv,
           L1_xattn_Wq, L1_xattn_Wk, L1_xattn_Wv, L1_xattn_Wo, L1_xattn_gamma, L1_xattn_beta):
    import numpy as np
    import concourse.bacc as bacc
    from concourse.bass_utils import run_bass_kernel_spmd

    def a(v):
        return np.asarray(v)

    twice = np.r_[0:CTX, P:CTX]

    def piece(left, right):
        return np.concatenate([left[:P], left[P:], right[:P], right[P:]], axis=1)

    def head(w, h):
        return a(w)[:, h * DIM:(h + 1) * DIM].T

    wa = [piece(a(L0_xattn_Wq), a(L0_xattn_Wk)[:, twice])]
    wb = [piece(a(L0_xattn_Wv)[:, twice], a(L0_xattn_Wd).T)]
    for h in range(HEADS):
        wa.append(piece(head(L1_xattn_Wq, h), head(L1_xattn_Wk, h)[:, twice]))
        wb.append(piece(head(L1_xattn_Wv, h)[:, twice], a(L1_xattn_Wo)[h * DIM:(h + 1) * DIM]))
    ctx_t = a(ctx_768).transpose(0, 2, 1)[:, twice]

    vectors = np.concatenate([a(v).reshape(2, P).T for v in (L0_xattn_bq, L0_xattn_bk, L0_xattn_bv)], axis=1)
    arrays = {
        "x": a(x).reshape(BATCHES * QUERIES, DIM),
        "context": a(ctx_768).reshape(BATCHES * KEYS, CTX),
        "mask": a(mask_BxS2_if1),
        "weights_a": np.stack(wa),
        "weights_b": np.stack(wb),
        "keys_t": ctx_t.reshape(BATCHES, 2, P, KEYS),
        "vectors": vectors,
        "rows": np.stack([a(L0_xattn_bd), a(L1_xattn_gamma), a(L1_xattn_beta)]),
        "rows_kv": np.stack([a(L0_xattn_g_kv), a(L0_xattn_be_kv)]),
        "rows_q": np.stack([a(L0_xattn_g_q), a(L0_xattn_be_q)]),
        "identity": np.eye(P, dtype=np.float32),
    }
    nc = bacc.Bacc("TRN2", target_bir_lowering=False, num_devices=1)
    arrays = {f"in_{k}": np.ascontiguousarray(v) for k, v in arrays.items()}
    args = [nc.dram_tensor(k, v.shape, mybir.dt.from_np(v.dtype), kind="ExternalInput").ap()
            for k, v in arrays.items()]
    out = nc.dram_tensor("out_0", (BATCHES * QUERIES, DIM), mybir.dt.float32, kind="ExternalOutput").ap()
    build(nc, *args, out)
    r = run_bass_kernel_spmd(nc, [arrays], core_ids=[0])
    return r.results[0]["out_0"].reshape(BATCHES, QUERIES, DIM)
```

```python
import concourse.bass as bass
from concourse import mybir
from concourse.alu_op_type import AluOpType as ALU
from contextlib import ExitStack

P = 128
BATCHES = 2
QUERIES = 512
KEYS = 1024
DIM = 256
CTX = 192
REM = CTX - P
HEADS = 8
QT = QUERIES // P
KT = KEYS // P
DT = DIM // P
BANK = 512
EPS = 1e-5
LN_TILES = KT + QT
CTX_HALF = KT // 2
CTX_ORDER = [*range(CTX_HALF, KT), *range(CTX_HALF)]
FIN_SHARED = (QT, 1)
HALF_Q = QUERIES // 2
BIG = 3.0e38

C_BQ, C_BK, C_BV, N_COLS = 0, 2, 4, 6
(PC_A0, PC_B0, PC_A1, PC_KA0, PC_KR0, PC_V00, PC_V01, PC_KA1, PC_KR1, PC_V10, PC_V11) = range(11)
HI_OF = {PC_A0: 1, PC_B0: 2, PC_A1: 3, PC_KA0: 4, PC_KR0: 5, PC_V00: 7, PC_V01: 9,
         PC_KA1: 10, PC_KR1: 11, PC_V10: 13, PC_V11: 15}
(T_A0, T_A0b, T_VEC, T_Q0, T_Q0b, T_B0, T_B0b, T_OUTB, T_Q1, T_Q1b, T_A1, T_A1b, T_QH, T_QHb,
 TASKS0) = range(15)
CHUNKS = 6
X_CHUNKS = DT


def centred_no(b, t):
    return b * LN_TILES + (t - KT if t >= KT else QT + CTX_ORDER.index(t))


def slot_no(h, j):
    return 8 * h + (8 + j)


def task_no(h, j):
    if isinstance(h, int) and h == HEADS - 1 and j >= 6:
        return TASKS0 + 8 * h + (j - 4)
    return 8 * h + (TASKS0 + j)


def hi_before(task):
    return task - (1 if task > T_VEC else 0) - (1 if task > T_OUTB else 0)


def pieces_a(h):
    return 2 * h + (PC_V11 + 2)


def pieces_b(h):
    if isinstance(h, int) and h == HEADS - 1:
        return 2 * h + (PC_V11 + 2)
    return 2 * h + (PC_V11 + 3)


def build(nc, x, context, mask, weights_a, weights_b, keys_t, vectors, rows, rows_kv, rows_q, identity, out):
    f32, f32r, i32 = mybir.dt.float32, mybir.dt.float32r, mybir.dt.int32
    ACT = mybir.ActivationFunctionType

    x_tiles = x.rearrange("(t p) d -> p t d", p=P)
    out_tiles = out.rearrange("(t p) d -> p t d", p=P)
    ctx_tiles = context.rearrange("(t p) l -> p t l", p=P)

    with ExitStack() as stack:
        def sb(name, shape, dt=f32, on=stack):
            return on.enter_context(nc.sbuf_tensor(name, shape, dt))

        def sem(name):
            return stack.enter_context(nc.semaphore(name))

        key_hi = [sb(f"key_hi{b}", [P, KEYS], f32r) for b in range(BATCHES)]
        key_lo = [sb(f"key_lo{b}", [P, KEYS], f32r) for b in range(BATCHES)]
        key_rem = [sb(f"key_rem{b}", [P, KEYS], f32r) for b in range(BATCHES)]
        val_hi = [sb(f"val_hi{b}", [P, KT, P], f32r) for b in range(BATCHES)]
        val_lo = [sb(f"val_lo{b}", [P, KT, P], f32r) for b in range(BATCHES)]
        val_rem = [sb(f"val_rem{b}", [P, KT, P], f32r) for b in range(BATCHES)]
        xt_hi = sb("xt_hi", [P, DT, BATCHES * QUERIES], f32r)
        xt_lo = sb("xt_lo", [P, DT, BATCHES * QUERIES], f32r)
        q_hi = [sb(f"q_hi{b}", [P, 2, QUERIES], f32r) for b in range(BATCHES)]
        q_lo = [sb(f"q_lo{b}", [P, 2, QUERIES], f32r) for b in range(BATCHES)]
        a_hi, a_lo = sb("a_hi", [P, DT, DIM], f32r), sb("a_lo", [P, DT, DIM], f32r)
        b_hi, b_lo = sb("b_hi", [P, 2, DIM], f32r), sb("b_lo", [P, 2, DIM], f32r)
        b_full = sb("b_full", [P, 2, DIM])
        rem_sum = sb("rem_sum", [P, QUERIES])
        ring = [sb(f"ring{r}", [P, 1024]) for r in range(2)]
        w_hi, w_lo = sb("w_hi", [P, 1024], f32r), sb("w_lo", [P, 1024], f32r)
        neg_scores = sb("neg_scores", [P, KEYS])
        probs = sb("probs", [P, KEYS])
        mask_bias = sb("mask_bias", [P, BATCHES, KEYS])
        resid = sb("resid", [P, BATCHES * QT, DIM])
        ident = sb("ident", [P, P])
        cols = sb("cols", [P, N_COLS])
        row_vecs = sb("row_vecs", [P, 2, DIM])
        vec = sb("vec", [P, 3])
        stats = sb("stats", [P, LN_TILES, 6])
        moments = sb("moments", [P, BATCHES * LN_TILES, 2])
        var_eps = sb("var_eps", [P, BATCHES * LN_TILES])
        rstd = sb("rstd", [P, BATCHES * LN_TILES])
        minus_half = sb("minus_half", [P, BATCHES * LN_TILES])
        row_min = sb("row_min", [P, 2 * QT])
        row_sum = sb("row_sum", [P, 2 * QT])
        row_inv = sb("row_inv", [P, 2 * QT])
        neg_shift = sb("neg_shift", [P, BATCHES * QT])
        probs_t_hi = [sb("probs_t_hi0", [P, KT, QUERIES], f32r)]
        probs_t_lo = [sb("probs_t_lo0", [P, KT, QUERIES], f32r)]
        with ExitStack() as early:
            ctx_raw = sb("ctx_raw", [P, BATCHES * KT, CTX], on=early)
            kvn = [sb("kvn0", [P, KT, 2 * P], on=early)]
            xn = sb("xn", [P, BATCHES * QT, DIM], on=early)
            kv_rows = sb("kv_rows", [P, 2, CTX], on=early)
            q_rows = sb("q_rows", [P, 2, DIM], on=early)
            ones = sb("ones", [P, P], on=early)
            kvn.append(sb("kvn1", [P, KT, 2 * P], on=early))
        probs_t_hi.append(sb("probs_t_hi1", [P, KT, QUERIES], f32r))
        o_hi, o_lo = sb("o_hi", [P, 2, QUERIES], f32r), sb("o_lo", [P, 2, QUERIES], f32r)
        probs_t_lo.append(sb("probs_t_lo1", [P, KT, QUERIES], f32r))
        spread = b_full[:, :, :].rearrange("p k (n q) -> p (k n) q", q=P)
        outb = rem_sum[:, 0:DIM]
        neg_w_row = rem_sum[:, DIM:2 * DIM]
        finals = [probs, neg_scores]

        def ps(name, width):
            return stack.enter_context(nc.psum_tensor(name, [P, width], f32))
        ps_scores = ps("ps_scores", 2 * BANK)
        ps_turn = [ps(f"ps_turn{c}", BANK) for c in range(2)]
        ps_o = [ps(f"ps_o{c}", BANK) for c in range(2)]
        ps_out = ps("ps_out", BANK)
        ps_task = ps("ps_task", BANK)

        def out_bank(idx):
            if isinstance(idx, int) and idx < 8:
                return (ps_out, ps_task, ps_o[0], ps_o[1])[idx % 4][:, 0:DIM]
            if isinstance(idx, int) and idx >= 8 * HEADS:
                return (ps_out, ps_task, ps_turn[0], ps_turn[1])[idx % 4][:, 0:DIM]
            return ps_out[:, 0:DIM]

        def task_bank(task):
            return ps_out if isinstance(task, int) and task < TASKS0 + 6 and task % 2 else ps_task

        def last_banks(half):
            if half == 0:
                return [ps_scores[:, 0:HALF_Q], ps_scores[:, BANK:BANK + HALF_Q]]
            return [ps_o[0][:, 0:HALF_Q], ps_o[1][:, 0:HALF_Q]]

        vec_bank = ps_o[1]

        def chunk_bank(b, c):
            sides = [ps_scores[:, 0:BANK], ps_scores[:, BANK:2 * BANK]]
            if b == 0:
                return [ps_turn[0], ps_turn[1], sides[0], ps_o[0], sides[1], ps_o[1]][c]
            return [ps_o[0], ps_o[1], sides[0], sides[1], ps_turn[0], ps_turn[1]][c]

        ring_loaded = [sem(f"ring_loaded{r}") for r in range(2)]
        ctx_loaded = [sem(f"ctx_loaded{b}") for b in range(BATCHES)]
        x_loaded = [sem(f"x_loaded{b}") for b in range(BATCHES)]
        cols_loaded = sem("cols_loaded")
        ident_loaded = sem("ident_loaded")
        q_rows_loaded = sem("q_rows_loaded")
        kv_rows_loaded = sem("kv_rows_loaded")
        row_vecs_loaded = sem("row_vecs_loaded")
        mask_loaded = sem("mask_loaded")
        mask_made = sem("mask_made")
        stored = sem("stored")
        half_set = sem("half_set")
        ones_set = sem("ones_set")
        spread_made = sem("spread_made")
        stats_made = sem("stats_made")
        moments_made = sem("moments_made")
        var_made = sem("var_made")
        rstd_made = sem("rstd_made")
        centred = sem("centred")
        scaled = sem("scaled")
        x_normed = sem("x_normed")
        ctx_normed = [sem(f"ctx_normed{half}") for half in range(2)]
        doubled = sem("doubled")
        chunk_turned = sem("chunk_turned")
        chunk_rounded = sem("chunk_rounded")
        chunk_split = sem("chunk_split")
        piece_hi = sem("piece_hi")
        piece_split = sem("piece_split")
        vals0_hi = sem("vals0_hi")
        vals0_split = sem("vals0_split")
        vec_made = sem("vec_made")
        shift_summed = sem("shift_summed")
        shift_made = sem("shift_made")
        outb_made = sem("outb_made")
        biased = sem("biased")
        task_done = sem("task_done")
        task_hi = sem("task_hi")
        task_free = sem("task_free")
        b_hi_made = sem("b_hi_made")
        b_split = sem("b_split")
        folded_hi = sem("folded_hi")
        folded = sem("folded")
        scored = sem("scored")
        min_made = sem("min_made")
        exped = sem("exped")
        probs_turned = sem("probs_turned")
        pt_hi_made = sem("pt_hi_made")
        pt_split = sem("pt_split")
        inv_made = sem("inv_made")
        valued = sem("valued")
        o_hi_made = sem("o_hi_made")
        o_split = sem("o_split")
        projected = sem("projected")
        added = sem("added")
        y_turned = sem("y_turned")
        y_hi_made = sem("y_hi_made")
        y_split = sem("y_split")
        fin_stats = sem("fin_stats")
        fin_moments = sem("fin_moments")
        fin_var = sem("fin_var")
        fin_rstd = sem("fin_rstd")
        fin_centred = sem("fin_centred")
        fin_scaled = sem("fin_scaled")
        fin_made = [sem(f"fin_made{half}") for half in range(2)]

        block = stack.enter_context(nc.Block())

        @block.sync
        def _(sp):
            sp.dma_start(resid[:, 0:QT, :], x_tiles[:, 0:QT, :]).then_inc(x_loaded[0], 16)
            sp.dma_start(q_rows[:, :, :], rows_q.partition_broadcast(P)).then_inc(q_rows_loaded, 16)
            sp.dma_start(ctx_raw[:, 0:KT, :], ctx_tiles[:, 0:KT, :]).then_inc(ctx_loaded[0], 16)
            sp.dma_start(kv_rows[:, :, :], rows_kv.partition_broadcast(P)).then_inc(kv_rows_loaded, 16)
            sp.dma_start(ring[0][:, :], weights_a[0]).then_inc(ring_loaded[0], 16)
            sp.dma_start(ring[1][:, :], weights_b[0]).then_inc(ring_loaded[1], 16)
            sp.dma_start(resid[:, QT:, :], x_tiles[:, QT:, :]).then_inc(x_loaded[1], 16)
            sp.dma_start(ctx_raw[:, KT:, :], ctx_tiles[:, KT:, :]).then_inc(ctx_loaded[1], 16)
            sp.dma_start(outb, rows[0].partition_broadcast(P)).then_inc(row_vecs_loaded, 16)
            sp.dma_start(row_vecs[:, :, :], rows[1:3].partition_broadcast(P)).then_inc(row_vecs_loaded, 16)

            def piece(k, src, dst=None):
                dst = ring[k % 2][:, :] if dst is None else dst
                sp.wait_ge(piece_split, k - 1)
                sp.dma_start(dst, src).then_inc(ring_loaded[k % 2], 16)

            def values(k, b, g):
                t = b * KT + g * KT // 2
                piece(k, ctx_tiles[:, t:t + KT // 2, :],
                      ring[k % 2][:, 0:CTX * KT // 2].rearrange("p (t l) -> p t l", l=CTX))

            sp.wait_ge(task_done, T_VEC + 1)
            piece(PC_A1, weights_a[1])
            sp.dma_start(mask_bias[:, :, :].bitcast(i32), mask.partition_broadcast(P)).then_inc(mask_loaded, 16)
            sp.wait_ge(task_done, T_OUTB + 1)
            piece(PC_KA0, keys_t[0, 0])
            piece(PC_KR0, keys_t[0, 1])
            values(PC_V00, 0, 0)
            values(PC_V01, 0, 1)
            piece(PC_KA1, keys_t[1, 0])
            piece(PC_KR1, keys_t[1, 1])
            values(PC_V10, 1, 0)
            values(PC_V11, 1, 1)

            def body(h):
                if not (isinstance(h, int) and h == HEADS - 1):
                    sp.wait_ge(piece_split, pieces_a(h) - 2)
                    sp.dma_start(ring[1][:, :], weights_a[h + 2]).then_inc(ring_loaded[1], 16)
                sp.wait_ge(piece_split, 2 * h + (PC_V11 + 1))
                sp.dma_start(ring[0][:, :], weights_b[h + 1]).then_inc(ring_loaded[0], 16)

            body(0)
            with sp.Fori(1, HEADS - 1) as h:
                body(h)
            body(HEADS - 1)

            def store(b, t, half, count):
                tiles = finals[b][:, :].rearrange("p (t d) -> p t d", t=QT)
                sp.wait_ge(fin_made[half], count)
                sp.dma_start(out_tiles[:, b * QT + t.start:b * QT + t.stop, :], tiles[:, t, :])\
                    .then_inc(stored, 16)

            store(0, slice(0, QT), 0, FIN_SHARED[0])
            store(1, slice(0, FIN_SHARED[1]), 0, sum(FIN_SHARED))
            store(1, slice(FIN_SHARED[1], QT), 1, QT - FIN_SHARED[1])
            sp.wait_ge(stored, 3 * 16)

        @block.gpsimd
        def _(pool):
            def rsqrt(b, first, end, count):
                t = slice(b * LN_TILES + first, b * LN_TILES + end)
                pool.wait_ge(var_made, count)
                nc.gpsimd.tensor_tensor(rstd[:, t], var_eps[:, t], minus_half[:, t], ALU.pow)\
                    .then_inc(rstd_made, 1)

            def bias_tiles(b, tiles, scaled_before, done):
                for i, t in enumerate(tiles):
                    dst = kvn[b][:, t, 0:CTX] if t < KT else xn[:, b * QT + t - KT, :]
                    bias = kv_rows[:, 1, :] if t < KT else q_rows[:, 1, :]
                    pool.wait_ge(scaled, scaled_before + i + 1)
                    nc.gpsimd.tensor_tensor(dst, dst, bias, ALU.add).then_inc(done, 1)

            def split_weights(hi_count, r):
                pool.wait_ge(piece_hi, hi_count)
                nc.gpsimd.tensor_tensor(w_lo[:, :], ring[r][:, :], w_hi[:, :].bitcast(f32), ALU.subtract)\
                    .then_inc(piece_split, 1)

            def split_keys(k, b):
                pool.wait_ge(piece_hi, HI_OF[k])
                nc.gpsimd.tensor_tensor(key_lo[b][:, :], ring[k % 2][:, :], key_hi[b][:, :].bitcast(f32),
                                        ALU.subtract).then_inc(piece_split, 1)
                lo = key_rem[b][REM:P, :]
                pool.wait_ge(piece_hi, HI_OF[k + 1])
                pool.wait_ge(piece_split, k + 1)
                nc.gpsimd.tensor_tensor(lo, ring[(k + 1) % 2][REM:P, :], lo.bitcast(f32), ALU.subtract)\
                    .then_inc(piece_split, 1)

            def split_values(k, b):
                pool.wait_ge(piece_split, k)
                for g in range(2):
                    src = ring[(k + g) % 2][:, 0:CTX * KT // 2].rearrange("p (t l) -> p t l", l=CTX)
                    t = slice(g * KT // 2, (g + 1) * KT // 2)
                    pool.wait_ge(piece_hi, HI_OF[k + g])
                    nc.gpsimd.tensor_tensor(val_lo[b][:, t, :], src[:, :, 0:P], val_hi[b][:, t, :].bitcast(f32),
                                            ALU.subtract)
                    nc.gpsimd.tensor_tensor(val_rem[b][:, t, REM:P], src[:, :, P:CTX],
                                            val_rem[b][:, t, 0:REM].bitcast(f32), ALU.subtract)\
                        .then_inc(piece_split, 1)

            def split_vals0(b):
                pool.wait_ge(vals0_hi, 2 * (b + 1))
                nc.gpsimd.tensor_tensor(val_lo[b][:, :, :], kvn[b][:, :, 0:P], val_hi[b][:, :, :].bitcast(f32),
                                        ALU.subtract).then_inc(vals0_split, 1)
                nc.gpsimd.tensor_tensor(val_rem[b][:, :, REM:P], kvn[b][:, :, P:CTX],
                                        val_rem[b][:, :, 0:REM].bitcast(f32), ALU.subtract).then_inc(vals0_split, 1)

            nc.gpsimd.memset(ones[:, :], 1.0).then_inc(ones_set, 1)
            nc.gpsimd.memset(minus_half[:, :], -0.5).then_inc(half_set, 1)
            pool.wait_ge(half_set, 1)
            for b in range(BATCHES):
                done = b * (QT + CTX_HALF)
                rsqrt(b, KT, LN_TILES, 2 * b + 1)
                pool.wait_ge(q_rows_loaded, 16)
                bias_tiles(b, range(KT, LN_TILES), done, x_normed)
                if b == 1:
                    split_weights(HI_OF[PC_A1], 0)
                    split_vals0(0)
                rsqrt(b, 0, KT, 2 * b + 2)
                pool.wait_ge(kv_rows_loaded, 16)
                bias_tiles(b, range(CTX_HALF, KT), done + QT, ctx_normed[1])
                if b == 0:
                    split_weights(HI_OF[PC_B0], 1)
            pool.wait_ge(centred, LN_TILES + QT)
            pool.wait_ge(outb_made, 1)
            for t in range(BATCHES * QT):
                nc.gpsimd.tensor_tensor(resid[:, t, :], resid[:, t, :], outb, ALU.add)\
                    .then_inc(biased, 1)
            split_vals0(1)
            split_keys(PC_KA0, 0)
            split_values(PC_V00, 0)
            split_keys(PC_KA1, 1)
            split_values(PC_V10, 1)

            def body(h):
                if not (isinstance(h, int) and h == HEADS - 1):
                    split_weights(2 * h + (HI_OF[PC_V11] + 1), 1)
                    split_weights(2 * h + (HI_OF[PC_V11] + 2), 0)
                else:
                    split_weights(2 * h + (HI_OF[PC_V11] + 1), 0)

            with pool.Fori(0, HEADS - 1) as h:
                body(h)
            body(HEADS - 1)
            for b in range(BATCHES):
                t = slice(b * QT, (b + 1) * QT)
                pool.wait_ge(fin_var, b + 1)
                nc.gpsimd.tensor_tensor(rstd[:, t], var_eps[:, t], minus_half[:, t], ALU.pow)\
                    .then_inc(fin_rstd, 1)
                for t in range(FIN_SHARED[b]):
                    dst = finals[b][:, t * DIM:(t + 1) * DIM]
                    pool.wait_ge(fin_scaled, FIN_SHARED[0] * b + t + 1)
                    nc.gpsimd.tensor_tensor(dst, dst, row_vecs[:, 1, :], ALU.add).then_inc(fin_made[0], 1)

        @block.tensor
        def _(pe):
            def three(dst, left, right, start, stop):
                (lh, ll), (rh, rl) = left, right
                pe.matmul(dst, lh, rh, start=start, stop=False)
                pe.matmul(dst, lh, rl, start=False, stop=False)
                return pe.matmul(dst, ll, rh, start=False, stop=stop)

            def absorb(task, m):
                dst = task_bank(task)[:, 0:DIM]
                for k in range(DT):
                    left, right = slice(k * DIM + m * P, k * DIM + (m + 1) * P), slice((DT + k) * DIM, (DT + k + 1) * DIM)
                    last = three(dst, (w_hi[:, left], w_lo[:, left]), (w_hi[:, right], w_lo[:, right]),
                                 k == 0, k == DT - 1)
                last.then_inc(task_done, 1)

            def queries(task, b, m, chunks=False):
                for k in range(DT):
                    if chunks:
                        pe.wait_ge(chunk_split, CHUNKS * b + k + 1)
                    s, mv = slice(m * P, (m + 1) * P), slice(b * QUERIES, (b + 1) * QUERIES)
                    last = three(task_bank(task)[:, :], (a_hi[:, k, s], a_lo[:, k, s]),
                                 (xt_hi[:, k, mv], xt_lo[:, k, mv]), k == 0, k == DT - 1)
                last.then_inc(task_done, 1)

            def folded_queries(task, b):
                for k in range(DT):
                    mv = slice(b * QUERIES, (b + 1) * QUERIES)
                    pe.matmul(task_bank(task)[:, :], a_hi[:, k, P:2 * P], xt_hi[:, k, mv], start=(k == 0), stop=False)
                    last = pe.matmul(task_bank(task)[:, :], a_hi[:, k, P:2 * P], xt_lo[:, k, mv],
                                     start=False, stop=(k == DT - 1))
                last.then_inc(task_done, 1)

            def scores(h, j, task=None, keys=None):
                b, q = j // QT, slice((j % QT) * P, (j % QT + 1) * P)
                s = slot_no(h, j)
                if not (isinstance(s, int) and s == 0):
                    pe.wait_ge(min_made, s)
                passes = ((q_hi[b][:, 0, q], key_hi[b]), (q_hi[b][:, 0, q], key_lo[b]),
                          (q_lo[b][:, 0, q], key_hi[b]), (q_hi[b][:, 1, q], key_rem[b]),
                          (q_lo[b][0:REM, 1, q], key_rem[b][0:REM]))
                for i, (left, right) in enumerate(passes):
                    if task is not None:
                        if i in (0, 3):
                            pe.wait_ge(task_hi, hi_before(task) + (1 if i == 0 else 2))
                        if i in (2, 4):
                            pe.wait_ge(task_free, task + (1 if i == 2 else 2))
                    if keys is not None and i == 3:
                        pe.wait_ge(piece_split, keys + 1)
                    for half in range(2):
                        n = slice(half * BANK, (half + 1) * BANK)
                        last = pe.matmul(ps_scores[:, n], left, right[:, n],
                                         start=(i == 0), stop=(i == len(passes) - 1))
                last.then_inc(scored, 1)

            def turn_probs(h, j):
                s = slot_no(h, j)
                for c in range(2):
                    if c == 0:
                        pe.wait_ge(exped, s + 1)
                    if not (isinstance(s, int) and s == 0):
                        pe.wait_ge(pt_split, 2 * s + (c - 1))
                    for k in range(4):
                        kt = 4 * c + k
                        last = pe.transpose(ps_turn[c][:, k * P:(k + 1) * P],
                                            probs[:, kt * P:(kt + 1) * P], ident[:, :])
                    last.then_inc(probs_turned, 1)

            def value_passes(o0, o1, b, kt, hi, lo):
                first, end = kt == 0, kt == KT - 1
                pe.matmul(o0, val_hi[b][:, kt, :], hi, start=first, stop=False)
                pe.matmul(o0, val_hi[b][:, kt, :], lo, start=False, stop=False)
                pe.matmul(o0, val_lo[b][:, kt, :], hi, start=False, stop=end)
                pe.matmul(o1, val_rem[b][:, kt, :], hi, start=first, stop=False)
                return pe.matmul(o1, val_rem[b][:, kt, :], lo, start=False, stop=end)

            def values(h, b, c):
                if c == 0:
                    s = slot_no(h, b * QT)
                    pe.wait_ge(pt_split, 2 * s + 2 * QT)
                    if not (isinstance(s, int) and s == 0):
                        pe.wait_ge(o_split, 4 * h + (4 + 2 * b))
                hi, lo = probs_t_hi[b], probs_t_lo[b]
                for kt in (2 * c, 2 * c + 1):
                    last = value_passes(ps_o[0][:, :], ps_o[1][:, :], b, kt, hi[:, kt, :], lo[:, kt, :])
                last.then_inc(valued, 1)

            def last_values(half, key_tiles):
                if key_tiles[0] == 0:
                    pe.wait_ge(pt_split, 2 * slot_no(HEADS - 1, QT) + QT * (half + 1))
                    if half == 0:
                        pe.wait_ge(min_made, 8 * (HEADS + 1))
                    else:
                        pe.wait_ge(o_split, 4 * HEADS + 2)
                q, (o0, o1) = slice(half * HALF_Q, (half + 1) * HALF_Q), last_banks(half)
                for kt in key_tiles:
                    last = value_passes(o0, o1, 1, kt, probs_t_hi[1][:, kt, q], probs_t_lo[1][:, kt, q])
                if key_tiles[-1] == KT - 1:
                    last.then_inc(valued, 1)

            def project(h, j):
                s = slot_no(h, j)
                q = slice((j % QT) * P, (j % QT + 1) * P)
                first, is_last = j % QT == 0, isinstance(s, int) and s >= 8 * HEADS
                second_half = is_last and j == QT + QT // 2
                if second_half:
                    pe.wait_ge(o_split, 4 * HEADS + 5)
                if first:
                    pe.wait_ge(o_split, 4 * h + (4 + 2 * (j // QT) + 2))
                    if j == 0:
                        if isinstance(h, int) and h == -1:
                            pe.wait_ge(task_free, T_B0b + 1)
                        else:
                            pe.wait_ge(b_split, h + 1)
                if isinstance(s, int) and s < 8:
                    if s == 0:
                        pe.wait_ge(task_free, T_A1b + 1)
                    elif s >= QT:
                        pe.wait_ge(added, s - (QT - 1))
                elif is_last:
                    if s == 8 * HEADS:
                        pe.wait_ge(task_free, TASKS0 + 8 * HEADS - 4)
                    pe.wait_ge(added, s if j == 0 else s - (QT - 1) if j >= QT else 8 * HEADS)
                else:
                    pe.wait_ge(added, s)
                dst = out_bank(s)
                for k in range(2):
                    if second_half and k == 1:
                        pe.wait_ge(o_split, 4 * HEADS + 6)
                    if k == 0:
                        three(dst, (o_hi[:, 0, q], o_lo[:, 0, q]), (b_hi[:, 0, :], b_lo[:, 0, :]), True, False)
                    else:
                        pe.matmul(dst, o_hi[:, 1, q], b_hi[:, 1, :], start=False, stop=False)
                        last = pe.matmul(dst, o_lo[:, 1, q], b_lo[:, 1, :], start=False, stop=True)
                last.then_inc(projected, 1)

            def turn_y(b):
                pe.wait_ge(added, QT * (b + 1))
                for c in range(DT):
                    for t in range(QT):
                        last = pe.transpose(ps_o[c][:, t * P:(t + 1) * P],
                                            resid[:, b * QT + t, c * P:(c + 1) * P], ident[:, :])
                    last.then_inc(y_turned, 1)

            def turn_chunk(b, c):
                i = CHUNKS * b + c
                if c < X_CHUNKS:
                    src = [xn[:, b * QT + t, c * P:(c + 1) * P] for t in range(QT)]
                    pe.wait_ge(x_normed, QT * (b + 1))
                else:
                    half, f = (c - X_CHUNKS) // 2, (c - X_CHUNKS) % 2
                    src = [kvn[b][:, half * CTX_HALF + t, f * P:(f + 1) * P] for t in range(CTX_HALF)]
                    if f == 0:
                        pe.wait_ge(ctx_normed[half], CTX_HALF * (b + 1))
                    else:
                        pe.wait_ge(doubled, 2 * b + half + 1)
                if b == 0 and c == CHUNKS - 1:
                    pe.wait_ge(task_free, T_VEC + 1)
                if b and c == 0:
                    pe.wait_ge(chunk_split, CHUNKS)
                elif b and c == 2:
                    pe.wait_ge(min_made, QT)
                elif b and c == 4:
                    pe.wait_ge(pt_split, 2 * QT)
                dst = chunk_bank(b, c)
                for t in range(4):
                    last = pe.transpose(dst[:, t * P:(t + 1) * P], src[t], ident[:, :])
                last.then_inc(chunk_turned, 1)

            def free(task):
                if task >= 2:
                    pe.wait_ge(task_free, task - 1)

            pe.wait_ge(spread_made, DT)
            pe.wait_ge(ring_loaded[0], 16)
            raw = ring[0]
            for k in range(DT):
                pe.matmul(vec_bank[:, DIM:2 * DIM], spread[:, k, :], raw[:, k * DIM:(k + 1) * DIM],
                          start=(k == 0), stop=(k == DT - 1))
            pe.wait_ge(ident_loaded, 16)
            for c in range(X_CHUNKS):
                turn_chunk(0, c)
            pe.wait_ge(piece_split, PC_A0 + 1)
            absorb(T_A0, 0)
            absorb(T_A0b, 1)
            for n in range(3):
                for k in range(DT):
                    left = spread[:, k, :] if n == 2 else raw[:, (DT + k) * DIM + n * P:(DT + k) * DIM + (n + 1) * P]
                    last = pe.matmul(vec_bank[:, n:n + 1], left, cols[:, C_BQ + k:C_BQ + k + 1],
                                     start=(k == 0), stop=(k == DT - 1))
            last.then_inc(task_done, 1)
            for c in range(X_CHUNKS, CHUNKS):
                turn_chunk(0, c)
            pe.wait_ge(chunk_split, X_CHUNKS)
            pe.wait_ge(task_free, T_VEC + 1)
            queries(T_Q0, 0, 0)
            queries(T_Q0b, 0, 1)

            pe.wait_ge(chunk_split, CHUNKS)
            scores(-1, 0, task=T_Q0)
            pe.wait_ge(task_free, T_Q0b + 1)
            pe.wait_ge(piece_split, PC_B0 + 1)
            absorb(T_B0, 0)
            absorb(T_B0b, 1)
            scores(-1, 1)
            turn_probs(-1, 0)
            free(T_OUTB)
            pe.wait_ge(spread_made, 2 * DT)
            raw = ring[1]
            for k in range(DT):
                last = pe.matmul(ps_out[:, 0:DIM], spread[:, DT + k, :], raw[:, (DT + k) * DIM:(DT + k + 1) * DIM],
                                 start=(k == 0), stop=(k == DT - 1))
            last.then_inc(task_done, 1)
            scores(-1, 2)
            turn_probs(-1, 1)
            scores(-1, 3)
            turn_chunk(1, 0)
            turn_chunk(1, 1)
            turn_probs(-1, 2)
            free(T_Q1)
            queries(T_Q1, 1, 0, chunks=True)
            turn_probs(-1, 3)
            free(T_Q1b)
            queries(T_Q1b, 1, 1)
            pe.wait_ge(vals0_split, 2)
            for c in range(QT):
                values(-1, 0, c)
                if c == 2:
                    for n in range(X_CHUNKS, CHUNKS):
                        turn_chunk(1, n)

            pe.wait_ge(chunk_split, 2 * CHUNKS)
            scores(-1, 4, task=T_Q1)
            pe.wait_ge(piece_split, PC_A1 + 1)
            absorb(T_A1, 0)
            absorb(T_A1b, 1)
            scores(-1, 5)
            turn_probs(-1, 4)
            for t in range(QT):
                project(-1, t)
            scores(-1, 6)
            turn_probs(-1, 5)
            turn_y(0)
            scores(-1, 7)
            turn_probs(-1, 6)
            pe.wait_ge(y_split, DT)
            pe.wait_ge(task_free, T_A1b + 1)
            queries(T_QH, 0, 0)
            queries(T_QHb, 0, 1)
            turn_probs(-1, 7)

            def first_body():
                for j in range(2 * QT):
                    if j > 0:
                        turn_probs(0, j - 1)
                    if j == 3:
                        turn_y(1)
                    if j == QT:
                        pe.wait_ge(piece_split, pieces_a(0))
                        pe.wait_ge(task_free, task_no(0, 1))
                        absorb(task_no(0, 2), 0)
                        pe.wait_ge(piece_split, PC_V11 + 1)
                        pe.wait_ge(task_free, task_no(0, 2))
                    if j > 0:
                        scores(0, j)
                    else:
                        pe.wait_ge(piece_split, PC_KA0 + 1)
                        scores(0, 0, task=T_QH, keys=PC_KR0)
                        pe.wait_ge(vals0_split, 4)
                    if j < 2:
                        values(-1, 1, 2 * j)
                        values(-1, 1, 2 * j + 1)
                    if j == 2:
                        for t in range(QT, 2 * QT):
                            project(-1, t)
                    if j == 3:
                        pe.wait_ge(y_split, 2 * DT)
                        queries(task_no(0, 0), 1, 0)
                        queries(task_no(0, 1), 1, 1)
                    if j == 5:
                        pe.wait_ge(task_free, task_no(0, 4))
                        queries(task_no(0, 4), 0, 0)
                    if j >= 6:
                        if j == 6:
                            pe.wait_ge(piece_split, pieces_b(0))
                        pe.wait_ge(task_free, task_no(0, j))
                        absorb(task_no(0, j), j - 6)
                    if j >= QT:
                        values(0, 0, j - QT)
                    if j == 4:
                        absorb(task_no(0, 3), 1)
                    if j == 5:
                        folded_queries(task_no(0, 5), 0)

            def body(h):
                last_head = isinstance(h, int) and h == HEADS - 1
                for j in range(2 * QT):
                    b = j // QT
                    if j > 0:
                        turn_probs(h, j - 1)
                    else:
                        turn_probs(h - 1, 2 * QT - 1)
                    if j % QT == 0:
                        pe.wait_ge(task_free, task_no(h, -2 if j == 0 else 2))
                        pe.wait_ge(folded, 2 * h - 1 if j == 0 else 2 * h)
                    scores(h, j)
                    if not (last_head and (2 <= j < 6 or j == 7)):
                        pe.wait_ge(task_free, task_no(h, j))
                        if j == 0:
                            queries(None, 1, 0)
                        elif j == 1:
                            folded_queries(None, 1)
                        elif j < 4:
                            if j == 2:
                                pe.wait_ge(piece_split, pieces_a(h))
                            absorb(None, j - 2)
                        elif j == 4:
                            queries(None, 0, 0)
                        elif j == 5:
                            folded_queries(None, 0)
                        else:
                            if j == 6:
                                pe.wait_ge(piece_split, pieces_b(h))
                            absorb(None, j - 6)
                    if b == 1:
                        values(h, 0, j - QT)
                    else:
                        values(h - 1, 1, j)
                    if not (last_head and j == 2 * QT - 1):
                        project(h - 1, j)

            first_body()
            with pe.Fori(1, HEADS - 1) as h:
                body(h)
            body(HEADS - 1)
            last_values(0, range(0, 2))
            turn_probs(HEADS - 1, 2 * QT - 1)
            project(HEADS - 2, 2 * QT - 1)
            pe.wait_ge(task_free, task_no(HEADS - 1, 7))
            absorb(None, 1)
            last_values(0, range(2, KT))
            last_values(1, range(0, 2))
            for t in range(QT):
                project(HEADS - 1, t)
            last_values(1, range(2, KT))
            for t in range(QT, 2 * QT):
                project(HEADS - 1, t)

        @block.scalar
        def _(act):
            act.dma_start(cols[:, :], vectors).then_inc(cols_loaded, 16)
            act.dma_start(ident[:, :], identity).then_inc(ident_loaded, 16)

            def exp(h, j):
                s = slot_no(h, j)
                if not (isinstance(s, int) and s == 0):
                    act.wait_ge(probs_turned, 2 * s)
                act.wait_ge(min_made, s + 1)
                act.activation(probs[:, :], neg_scores[:, :], ACT.Exp, bias=row_min[:, j:j + 1],
                               scale=-1.0, accum_out=row_sum[:, j:j + 1]).then_inc(exped, 1)

            def round_probs(h, j):
                s, b = slot_no(h, j), j // QT
                if j % QT == 0 and not (isinstance(s, int) and s < 8):
                    act.wait_ge(valued, s - 4)
                q = slice((j % QT) * P, (j % QT + 1) * P)
                for c in range(2):
                    act.wait_ge(probs_turned, 2 * s + (c + 1))
                    act.activation(probs_t_hi[b][:, 4 * c:4 * c + 4, q],
                                   ps_turn[c][:, :].rearrange("p (k q) -> p k q", k=4), ACT.Copy)\
                        .then_inc(pt_hi_made, 1)

            def round_outputs(h, b):
                s = slot_no(h, b * QT)
                act.wait_ge(valued, s + 4)
                if not (isinstance(s, int) and s == 0):
                    act.wait_ge(projected, s)
                for k in range(2):
                    act.activation(o_hi[:, k, :], ps_o[k][:, :], ACT.Copy).then_inc(o_hi_made, 1)
                act.activation(o_lo[REM:P, 1, :], ps_o[1][0:REM, :], ACT.Copy).then_inc(o_hi_made, 1)

            def round_last_outputs(half):
                q, banks = slice(half * HALF_Q, (half + 1) * HALF_Q), last_banks(half)
                act.wait_ge(valued, 8 * HEADS + 4 + half + 1)
                act.wait_ge(projected, 8 * HEADS + QT)
                for k in range(2):
                    act.activation(o_hi[:, k, q], banks[k], ACT.Copy).then_inc(o_hi_made, 1)
                act.activation(o_lo[REM:P, 1, q], banks[1][0:REM, :], ACT.Copy).then_inc(o_hi_made, 1)

            def round_a(task, m, scale):
                act.wait_ge(task_done, task + 1)
                act.activation(a_hi[:, m, :], task_bank(task)[:, 0:DIM], ACT.Copy, scale=scale).then_inc(task_hi, 1)

            def round_b(task, m):
                act.wait_ge(task_done, task + 1)
                if m == 1:
                    act.activation(b_lo[0:REM, 1, :], task_bank(task)[0:REM, 0:DIM], ACT.Copy)
                act.activation(b_hi[:, m, :], task_bank(task)[:, 0:DIM], ACT.Copy).then_inc(task_hi, 1)

            def round_queries(task, b, m, layer):
                act.wait_ge(task_done, task + 1)
                if layer:
                    act.activation(q_hi[b][:, m, :], task_bank(task)[:, :], ACT.Copy).then_inc(task_hi, 1)
                else:
                    act.activation(q_hi[b][:, m, :], task_bank(task)[:, :], ACT.Identity,
                                   bias=vec[:, m:m + 1]).then_inc(task_hi, 1)

            def move_remainder(task, folds):
                if not (isinstance(folds, int) and folds == 0):
                    act.wait_ge(folded, folds)
                act.wait_ge(task_done, task + 1)
                act.activation(rem_sum[0:REM, :], task_bank(task)[REM:P, :], ACT.Copy).then_inc(task_hi, 1)

            def round_folded(task, b):
                act.wait_ge(task_free, task + 1)
                act.activation(q_hi[b][0:REM, 1, :], rem_sum[0:REM, :], ACT.Copy).then_inc(folded_hi, 1)
                act.activation(q_hi[b][REM:P, 1, :], rem_sum[0:REM, :], ACT.Copy).then_inc(folded_hi, 1)

            def keep_b(task, m):
                act.wait_ge(task_done, task + 1)
                act.activation(b_full[:, m, :], ps_task[:, 0:DIM], ACT.Copy).then_inc(task_free, 1)

            def round_weights(loaded, r):
                act.wait_ge(ring_loaded[r], loaded)
                act.activation(w_hi[:, :], ring[r][:, :], ACT.Copy).then_inc(piece_hi, 1)

            def round_keys(k, b):
                act.wait_ge(scored, 4 * (b + 1))
                act.wait_ge(ring_loaded[k % 2], 16 * (k // 2 + 1))
                act.activation(key_hi[b][:, :], ring[k % 2][:, :], ACT.Copy).then_inc(piece_hi, 1)
                k += 1
                act.wait_ge(ring_loaded[k % 2], 16 * (k // 2 + 1))
                act.activation(key_rem[b][:, :], ring[k % 2][:, :], ACT.Copy).then_inc(piece_hi, 1)

            def round_values(k, b):
                act.wait_ge(valued, 4 * (b + 1))
                for g in range(2):
                    src = ring[(k + g) % 2][:, 0:CTX * KT // 2].rearrange("p (t l) -> p t l", l=CTX)
                    t = slice(g * KT // 2, (g + 1) * KT // 2)
                    act.wait_ge(ring_loaded[(k + g) % 2], 16 * ((k + g) // 2 + 1))
                    act.activation(val_hi[b][:, t, :], src[:, :, 0:P], ACT.Copy).then_inc(piece_hi, 1)
                    act.activation(val_rem[b][:, t, 0:REM], src[:, :, P:CTX], ACT.Copy).then_inc(piece_hi, 1)

            def scale_tiles(b, tiles, rstds):
                act.wait_ge(rstd_made, rstds)
                for t in tiles:
                    n = b * LN_TILES + t
                    dst = kvn[b][:, t, 0:CTX] if t < KT else xn[:, b * QT + t - KT, :]
                    act.wait_ge(centred, centred_no(b, t) + 1)
                    act.activation(dst, dst, ACT.Copy, scale=rstd[:, n:n + 1]).then_inc(scaled, 1)

            def double_context(b, half):
                t = slice(half * CTX_HALF, (half + 1) * CTX_HALF)
                act.wait_ge(ctx_normed[half], CTX_HALF * (b + 1))
                act.activation(kvn[b][:, t, CTX:2 * P], kvn[b][:, t, P:CTX], ACT.Copy).then_inc(doubled, 1)

            def round_chunk(b, c):
                if c < X_CHUNKS:
                    dst = xt_hi[:, c, b * QUERIES:(b + 1) * QUERIES]
                else:
                    half, f = (c - X_CHUNKS) // 2, (c - X_CHUNKS) % 2
                    dst = (key_rem if f else key_hi)[b][:, half * BANK:(half + 1) * BANK]
                act.wait_ge(chunk_turned, CHUNKS * b + c + 1)
                act.activation(dst, chunk_bank(b, c)[:, 0:BANK], ACT.Copy).then_inc(chunk_rounded, 1)

            def round_vals0(b):
                act.activation(val_hi[b][:, :, :], kvn[b][:, :, 0:P], ACT.Copy).then_inc(vals0_hi, 1)
                act.activation(val_rem[b][:, :, 0:REM], kvn[b][:, :, P:CTX], ACT.Copy).then_inc(vals0_hi, 1)

            def round_y(b):
                for c in range(DT):
                    act.wait_ge(y_turned, DT * b + c + 1)
                    act.activation(xt_hi[:, c, b * QUERIES:(b + 1) * QUERIES], ps_o[c][:, :], ACT.Copy)\
                        .then_inc(y_hi_made, 1)

            act.wait_ge(ones_set, 1)
            act.wait_ge(cols_loaded, 16)
            for n in range(2 * DT):
                act.activation(spread[:, n, :], ones[:, :], ACT.Copy, scale=cols[:, C_BK + n:C_BK + n + 1])\
                    .then_inc(spread_made, 1)
            scale_tiles(0, range(KT, LN_TILES), 1)
            round_weights(16, 0)
            for c in range(X_CHUNKS):
                round_chunk(0, c)
            scale_tiles(0, range(CTX_HALF, KT), 2)
            round_a(T_A0, 0, -1.0)
            round_a(T_A0b, 1, -1.0)
            double_context(0, 0)
            round_chunk(0, 2)
            double_context(0, 1)
            for c in range(3, CHUNKS):
                round_chunk(0, c)
            round_weights(16, 1)
            act.wait_ge(vec_made, 1)
            round_queries(T_Q0, 0, 0, 0)
            round_queries(T_Q0b, 0, 1, 0)
            exp(-1, 0)
            round_b(T_B0, 0)
            round_b(T_B0b, 1)
            round_probs(-1, 0)
            exp(-1, 1)
            scale_tiles(1, range(KT, LN_TILES), 3)
            round_weights(32, 0)
            round_probs(-1, 1)
            exp(-1, 2)
            round_vals0(0)
            round_chunk(1, 0)
            round_chunk(1, 1)
            exp(-1, 3)
            round_probs(-1, 2)
            round_queries(T_Q1, 1, 0, 0)
            round_probs(-1, 3)
            round_queries(T_Q1b, 1, 1, 0)
            scale_tiles(1, range(CTX_HALF, KT), 4)
            double_context(1, 0)
            round_chunk(1, 2)
            double_context(1, 1)
            for c in range(3, CHUNKS):
                round_chunk(1, c)
            round_outputs(-1, 0)
            round_vals0(1)
            round_keys(PC_KA0, 0)
            exp(-1, 4)
            round_a(T_A1, 0, -1.0 / 16)
            round_a(T_A1b, 1, -1.0 / 16)
            round_probs(-1, 4)
            exp(-1, 5)
            round_probs(-1, 5)
            exp(-1, 6)
            round_y(0)
            round_probs(-1, 6)
            exp(-1, 7)
            round_queries(T_QH, 0, 0, 1)
            round_queries(T_QHb, 0, 1, 1)
            round_probs(-1, 7)
            round_values(PC_V00, 0)

            def first_body():
                for j in range(2 * QT):
                    if j > 0:
                        round_probs(0, j - 1)
                    if j == 2:
                        round_values(PC_V10, 1)
                    if j == 3:
                        round_y(1)
                        round_weights(16 * (PC_V11 // 2 + 1), 1)
                    exp(0, j)
                    if j == 0:
                        round_keys(PC_KA1, 1)
                    if j == 1:
                        round_outputs(-1, 1)
                    if j == 3:
                        round_queries(task_no(0, 0), 1, 0, 1)
                        round_queries(task_no(0, 1), 1, 1, 1)
                    if j == 4:
                        round_a(task_no(0, 2), 0, -1.0 / 16)
                        round_a(task_no(0, 3), 1, -1.0 / 16)
                    if j == 5:
                        round_weights(16 * (PC_V11 // 2 + 2), 0)
                        round_queries(task_no(0, 4), 0, 0, 1)
                        move_remainder(task_no(0, 5), 0)
                    if j == 6:
                        round_folded(task_no(0, 5), 0)
                    if j >= 6:
                        keep_b(task_no(0, j), j - 6)
                round_outputs(0, 0)

            def body(h):
                last_head = isinstance(h, int) and h == HEADS - 1
                for j in range(2 * QT):
                    if j > 0:
                        round_probs(h, j - 1)
                    else:
                        round_probs(h - 1, 2 * QT - 1)
                    exp(h, j)
                    if not (last_head and 2 <= j < 6):
                        task = task_no(h, j)
                        if j == 0:
                            round_queries(task, 1, 0, 1)
                        elif j == 1:
                            move_remainder(task, 2 * h - 1)
                        elif j < 4:
                            round_a(task, j - 2, -1.0 / 16)
                        elif j == 4:
                            round_queries(task, 0, 0, 1)
                        elif j == 5:
                            move_remainder(task, 2 * h)
                        else:
                            if j == 6:
                                act.wait_ge(b_split, h)
                            if last_head and j == 7:
                                round_probs(h, j)
                            keep_b(task, j - 6)
                    if j == 2:
                        round_folded(task_no(h, 1), 1)
                    if j == 6 and not last_head:
                        round_folded(task_no(h, 5), 0)
                    if j == 1 and not last_head:
                        act.wait_ge(task_done, task_no(h, 0))
                        round_weights(16 * h + 16 * (PC_V11 // 2 + 1), 1)
                    if j == (2 if last_head else 3):
                        act.wait_ge(task_done, TASKS0 + 8 * h + 2 if last_head else task_no(h, 4))
                        round_weights(16 * h + 16 * (PC_V11 // 2 + 2), 0)
                    if j == 3:
                        round_outputs(h - 1, 1)
                    if j == 2 * QT - 1:
                        round_outputs(h, 0)

            first_body()
            with act.Fori(1, HEADS - 1) as h:
                body(h)
            body(HEADS - 1)
            def scale_finals(b):
                act.wait_ge(fin_rstd, b + 1)
                for t in range(FIN_SHARED[b]):
                    n = b * QT + t
                    act.wait_ge(fin_centred, n + 1)
                    act.activation(finals[b][:, t * DIM:(t + 1) * DIM], resid[:, n, :], ACT.Copy,
                                   scale=rstd[:, n:n + 1]).then_inc(fin_scaled, 1)

            round_last_outputs(0)
            round_last_outputs(1)
            scale_finals(0)
            scale_finals(1)

        @block.vector
        def _(dve):
            def invert(j):
                dve.reciprocal(row_inv[:, j:j + 1], row_sum[:, j:j + 1]).then_inc(inv_made, 1)

            def minimum(h, j, layer):
                s, b = slot_no(h, j), j // QT
                if not (isinstance(s, int) and s == 0):
                    dve.wait_ge(exped, s)
                if not (isinstance(s, int) and s <= 8):
                    dve.wait_ge(added, s - 8)
                dve.wait_ge(scored, s + 1)
                if not (isinstance(s, int) and s in (0, 8)):
                    invert((j - 1) % (2 * QT))
                if layer:
                    dve.wait_ge(mask_made, 2)
                    dve.tensor_tensor_reduce(
                        out=neg_scores[:, :], in0=ps_scores[:, :], in1=mask_bias[:, b, :], scale=1.0, scalar=BIG,
                        op0=ALU.add, op1=ALU.min, accum_out=row_min[:, j:j + 1]).then_inc(min_made, 1)
                else:
                    dve.wait_ge(shift_made, b + 1)
                    dve.tensor_scalar(neg_scores[:, :], ps_scores[:, :], neg_shift[:, j:j + 1], None,
                                      ALU.add, ALU.min, accum_out=row_min[:, j:j + 1]).then_inc(min_made, 1)

            def split_probs(h, j):
                s, b = slot_no(h, j), j // QT
                q = slice((j % QT) * P, (j % QT + 1) * P)
                for c in range(2):
                    dve.wait_ge(pt_hi_made, 2 * s + (c + 1))
                    dve.tensor_tensor(probs_t_lo[b][:, 4 * c:4 * c + 4, q],
                                      ps_turn[c][:, :].rearrange("p (k q) -> p k q", k=4),
                                      probs_t_hi[b][:, 4 * c:4 * c + 4, q].bitcast(f32), ALU.subtract)\
                        .then_inc(pt_split, 1)

            def split_outputs(h, b):
                n3 = 6 * h + (6 + 3 * b)
                dve.wait_ge(o_hi_made, n3 + 1)
                dve.tensor_tensor(o_lo[:, 0, :], ps_o[0][:, :], o_hi[:, 0, :].bitcast(f32), ALU.subtract)\
                    .then_inc(o_split, 1)
                dve.wait_ge(o_hi_made, n3 + 3)
                dve.tensor_tensor(o_lo[0:REM, 1, :], ps_o[1][0:REM, :], o_hi[0:REM, 1, :].bitcast(f32), ALU.subtract)\
                    .then_inc(o_split, 1)

            def split_last_outputs(half):
                q, banks = slice(half * HALF_Q, (half + 1) * HALF_Q), last_banks(half)
                n3 = 6 * HEADS + 3 + 3 * half
                dve.wait_ge(o_hi_made, n3 + 1)
                dve.tensor_tensor(o_lo[:, 0, q], banks[0], o_hi[:, 0, q].bitcast(f32), ALU.subtract)\
                    .then_inc(o_split, 1)
                dve.wait_ge(o_hi_made, n3 + 3)
                dve.tensor_tensor(o_lo[0:REM, 1, q], banks[1][0:REM, :], o_hi[0:REM, 1, q].bitcast(f32), ALU.subtract)\
                    .then_inc(o_split, 1)

            def split_a(task, m, scale):
                dve.wait_ge(task_hi, hi_before(task) + 1)
                dve.scalar_tensor_tensor(a_lo[:, m, :], task_bank(task)[:, 0:DIM], scale,
                                         a_hi[:, m, :].bitcast(f32), ALU.mult, ALU.subtract).then_inc(task_free, 1)

            def split_b0(task, m):
                rows_of = slice(m * REM, P)
                dve.wait_ge(task_hi, hi_before(task) + 1)
                dve.tensor_tensor(b_lo[rows_of, m, :], task_bank(task)[rows_of, 0:DIM],
                                  b_hi[rows_of, m, :].bitcast(f32), ALU.subtract).then_inc(task_free, 1)

            def split_queries(task, b, m, layer):
                dve.wait_ge(task_hi, hi_before(task) + 1)
                hi = q_hi[b][:, m, :].bitcast(f32)
                if layer:
                    dve.tensor_tensor(q_lo[b][:, m, :], task_bank(task)[:, :], hi, ALU.subtract).then_inc(task_free, 1)
                else:
                    dve.scalar_tensor_tensor(q_lo[b][:, m, :], task_bank(task)[:, :], vec[:, m:m + 1], hi,
                                             ALU.add, ALU.subtract).then_inc(task_free, 1)

            def split_b(count):
                dve.tensor_copy(b_hi[:, :, :], b_full[:, :, :]).then_inc(b_hi_made, 1)
                dve.tensor_copy(b_lo[0:REM, 1, :], b_full[0:REM, 1, :])
                dve.wait_ge(b_hi_made, count)
                dve.tensor_tensor(b_lo[:, 0, :], b_full[:, 0, :], b_hi[:, 0, :].bitcast(f32), ALU.subtract)
                dve.tensor_tensor(b_lo[REM:P, 1, :], b_full[REM:P, 1, :], b_hi[REM:P, 1, :].bitcast(f32), ALU.subtract)\
                    .then_inc(b_split, 1)

            def add(h, j):
                s = slot_no(h, j)
                if isinstance(s, int) and s < 8:
                    dve.wait_ge(biased, j + 1)
                    dve.wait_ge(inv_made, s + 1)
                else:
                    dve.wait_ge(added, s - 7)
                dve.wait_ge(projected, s + 1)
                dve.scalar_tensor_tensor(resid[:, j, :], out_bank(s), row_inv[:, j:j + 1], resid[:, j, :],
                                         ALU.mult, ALU.add).then_inc(added, 1)

            def ln_stats(b, tiles, loaded):
                dve.wait_ge(loaded, 16)
                for t in tiles:
                    if b == 1:
                        dve.wait_ge(moments_made, LN_TILES)
                    src = ctx_raw[:, b * KT + t, :] if t < KT else resid[:, b * QT + t - KT, :]
                    dve.bn_stats(stats[:, t, :], src).then_inc(stats_made, 1)

            def ln_moments(b, first, end):
                done = b * LN_TILES + (QT if first == 0 else 0)
                for i, t in enumerate(range(first, end)):
                    dve.wait_ge(stats_made, done + i + 1)
                    dve.bn_aggr(moments[:, b * LN_TILES + t, :], stats[:, t, :]).then_inc(moments_made, 1)
                n = slice(b * LN_TILES + first, b * LN_TILES + end)
                dve.wait_ge(moments_made, done + end - first)
                dve.tensor_scalar(var_eps[:, n], moments[:, n, 1], EPS, None, ALU.add).then_inc(var_made, 1)

            def ln_centre(b, tiles):
                for t in tiles:
                    n = b * LN_TILES + t
                    if t < KT:
                        dst, src, gain = kvn[b][:, t, 0:CTX], ctx_raw[:, b * KT + t, :], kv_rows[:, 0, :]
                    else:
                        x_tile = b * QT + t - KT
                        dst, src, gain = xn[:, x_tile, :], resid[:, x_tile, :], q_rows[:, 0, :]
                    dve.scalar_tensor_tensor(dst, src, moments[:, n, 0:1], gain, ALU.subtract, ALU.mult)\
                        .then_inc(centred, 1)

            def ln_scale_context(b):
                dve.wait_ge(rstd_made, 2 * b + 2)
                for t in range(CTX_HALF):
                    n, dst = b * LN_TILES + t, kvn[b][:, t, 0:CTX]
                    dve.wait_ge(centred, centred_no(b, t) + 1)
                    dve.scalar_tensor_tensor(dst, dst, rstd[:, n:n + 1], kv_rows[:, 1, :], ALU.mult, ALU.add)\
                        .then_inc(ctx_normed[0], 1)

            def split_chunk(b, c):
                src = chunk_bank(b, c)
                dve.wait_ge(chunk_rounded, CHUNKS * b + c + 1)
                if c < X_CHUNKS:
                    q = slice(b * QUERIES, (b + 1) * QUERIES)
                    dve.tensor_tensor(xt_lo[:, c, q], src[:, 0:BANK], xt_hi[:, c, q].bitcast(f32), ALU.subtract)\
                        .then_inc(chunk_split, 1)
                    return
                half, f = (c - X_CHUNKS) // 2, (c - X_CHUNKS) % 2
                n = slice(half * BANK, (half + 1) * BANK)
                if f == 0:
                    dve.tensor_tensor(key_lo[b][:, n], src[:, 0:BANK], key_hi[b][:, n].bitcast(f32), ALU.subtract)\
                        .then_inc(chunk_split, 1)
                else:
                    dve.tensor_tensor(key_rem[b][REM:P, n], src[REM:P, 0:BANK], key_rem[b][REM:P, n].bitcast(f32),
                                      ALU.subtract).then_inc(chunk_split, 1)

            def sum_shift(b, tiles):
                halves = "p (n q) -> p n q"
                dve.wait_ge(x_normed, QT * (b + 1))
                dve.wait_ge(centred, (b + 1) * LN_TILES)
                for t in tiles:
                    n = b * QT + t
                    spare = ctx_raw[:, b * KT + 2 * t:b * KT + 2 * t + 2, 0:P]
                    dve.tensor_tensor_reduce(
                        out=spare, in0=xn[:, n, :].rearrange(halves, n=2), in1=neg_w_row[:, :].rearrange(halves, n=2),
                        scale=1.0, scalar=0.0, op0=ALU.mult, op1=ALU.add, accum_out=neg_shift[:, n:n + 1])\
                        .then_inc(shift_summed, 1)

            def finish_shift(b):
                t = slice(b * QT, (b + 1) * QT)
                dve.wait_ge(shift_summed, QT * (b + 1))
                dve.tensor_scalar(neg_shift[:, t], neg_shift[:, t], vec[:, 2:3], None, ALU.add).then_inc(shift_made, 1)

            def split_y(b):
                q = slice(b * QUERIES, (b + 1) * QUERIES)
                for c in range(DT):
                    dve.wait_ge(y_hi_made, DT * b + c + 1)
                    dve.tensor_tensor(xt_lo[:, c, q], ps_o[c][:, :], xt_hi[:, c, q].bitcast(f32), ALU.subtract)\
                        .then_inc(y_split, 1)

            x_token_tiles = range(KT, LN_TILES)
            ln_stats(0, x_token_tiles, x_loaded[0])
            ln_moments(0, KT, LN_TILES)
            dve.wait_ge(q_rows_loaded, 16)
            ln_centre(0, x_token_tiles)
            ln_stats(0, range(KT), ctx_loaded[0])
            ln_moments(0, 0, KT)
            dve.wait_ge(piece_hi, HI_OF[PC_A0])
            dve.tensor_tensor(w_lo[:, :], ring[0][:, :], w_hi[:, :].bitcast(f32), ALU.subtract)\
                .then_inc(piece_split, 1)
            dve.wait_ge(kv_rows_loaded, 16)
            ln_centre(0, CTX_ORDER)
            ln_scale_context(0)
            for c in range(X_CHUNKS):
                split_chunk(0, c)
            split_a(T_A0, 0, -1.0)
            split_a(T_A0b, 1, -1.0)
            dve.wait_ge(task_done, T_VEC + 1)
            dve.tensor_scalar(vec[:, :], vec_bank[:, 0:3], -1.0, None, ALU.mult).then_inc(vec_made, 1)
            dve.tensor_scalar(neg_w_row[:, :], vec_bank[:, DIM:2 * DIM], -1.0, None, ALU.mult).then_inc(task_free, 1)
            for c in range(2, CHUNKS):
                split_chunk(0, c)
            dve.wait_ge(task_free, T_VEC + 1)
            sum_shift(0, range(0, 2))
            split_queries(T_Q0, 0, 0, 0)
            sum_shift(0, range(2, QT))
            split_queries(T_Q0b, 0, 1, 0)
            finish_shift(0)
            minimum(-1, 0, 0)
            ln_stats(1, x_token_tiles, x_loaded[1])
            ln_moments(1, KT, LN_TILES)
            split_b0(T_B0, 0)
            split_b0(T_B0b, 1)
            minimum(-1, 1, 0)
            ln_centre(1, x_token_tiles)
            split_probs(-1, 0)
            minimum(-1, 2, 0)
            ln_stats(1, range(0, 3), ctx_loaded[1])
            split_probs(-1, 1)
            dve.wait_ge(row_vecs_loaded, 32)
            dve.wait_ge(task_done, T_OUTB + 1)
            dve.tensor_tensor(outb, ps_out[:, 0:DIM], outb, ALU.add).then_inc(outb_made, 1)
            dve.wait_ge(outb_made, 1)
            dve.engine_nop().then_inc(task_free, 1)
            minimum(-1, 3, 0)
            split_chunk(1, 0)
            split_chunk(1, 1)
            ln_stats(1, range(3, 6), ctx_loaded[1])
            split_probs(-1, 2)
            ln_stats(1, range(6, KT), ctx_loaded[1])
            split_probs(-1, 3)
            ln_moments(1, 0, KT)
            ln_centre(1, CTX_ORDER)
            split_queries(T_Q1, 1, 0, 0)
            split_queries(T_Q1b, 1, 1, 0)
            ln_scale_context(1)
            sum_shift(1, range(QT))
            finish_shift(1)
            for c in range(2, CHUNKS):
                split_chunk(1, c)
            dve.wait_ge(shift_made, 2)
            split_outputs(-1, 0)
            minimum(-1, 4, 0)
            split_a(T_A1, 0, -1.0 / 16)
            split_a(T_A1b, 1, -1.0 / 16)
            dve.wait_ge(mask_loaded, 16)
            dve.tensor_scalar(mask_bias[:, :, :], mask_bias[:, :, :].bitcast(i32), 0.0, BIG,
                              ALU.is_equal, ALU.mult).then_inc(mask_made, 1)
            minimum(-1, 5, 0)
            dve.wait_ge(vals0_split, 4)
            split_probs(-1, 4)
            for t in range(QT):
                add(-1, t)
            minimum(-1, 6, 0)
            split_probs(-1, 5)
            split_y(0)
            minimum(-1, 7, 0)
            split_probs(-1, 6)
            dve.wait_ge(mask_made, 1)
            dve.tensor_scalar(mask_bias[:, :, :], mask_bias[:, :, :], 10.0, None, ALU.mult).then_inc(mask_made, 1)
            split_queries(T_QH, 0, 0, 1)
            split_queries(T_QHb, 0, 1, 1)
            split_probs(-1, 7)
            invert(7)

            def split_task(h, j):
                bank = task_bank(task_no(h, j))
                at_first = isinstance(h, int) and h == 0
                if isinstance(h, int):
                    dve.wait_ge(task_hi, 6 * h + HI0 + j + 1)
                else:
                    dve.wait_ge(task_hi, 6 * h + (HI0 + j + 1))
                if j in (2, 3):
                    m = j - 2
                    dve.scalar_tensor_tensor(a_lo[:, m, 0:P], bank[:, 0:P], -1.0 / 16, a_hi[:, m, 0:P].bitcast(f32),
                                             ALU.mult, ALU.subtract)
                    dve.scalar_tensor_tensor(a_hi[:, m, CTX:DIM], bank[:, CTX:DIM], -1.0 / 16,
                                             a_hi[:, m, CTX:DIM].bitcast(f32), ALU.mult, ALU.subtract)\
                        .then_inc(task_free, 1)
                elif j == 5 or (j == 1 and not at_first):
                    dve.tensor_tensor(rem_sum[0:REM, :], bank[0:REM, :], rem_sum[0:REM, :], ALU.add)\
                        .then_inc(task_free, 1)
                else:
                    b, m = (1, j) if j < 2 else (0, j - 4)
                    dve.tensor_tensor(q_lo[b][:, m, :], bank[:, :], q_hi[b][:, m, :].bitcast(f32),
                                      ALU.subtract).then_inc(task_free, 1)

            def split_folded(b, folds):
                dve.wait_ge(folded_hi, 2 * folds + 2)
                dve.tensor_tensor(q_lo[b][0:REM, 1, :], rem_sum[0:REM, :], q_hi[b][0:REM, 1, :].bitcast(f32),
                                  ALU.subtract).then_inc(folded, 1)

            HI0 = hi_before(TASKS0)

            def first_body():
                for j in range(2 * QT):
                    if j > 0:
                        split_probs(0, j - 1)
                    if j == 3:
                        split_y(1)
                    minimum(0, j, 1)
                    if j == 1:
                        split_outputs(-1, 1)
                    if j == 2:
                        for t in range(QT, 2 * QT):
                            add(-1, t)
                    if j in (3, 4, 5):
                        split_task(0, 2 * (j - 3))
                        split_task(0, 2 * (j - 3) + 1)
                    if j == 6:
                        split_folded(0, 0)
                split_outputs(0, 0)

            def body(h):
                last_head = isinstance(h, int) and h == HEADS - 1
                for j in range(2 * QT):
                    if j > 0:
                        split_probs(h, j - 1)
                    else:
                        split_probs(h - 1, 2 * QT - 1)
                    minimum(h, j, 1)
                    if j == 0:
                        dve.wait_ge(projected, 8 * h)
                        dve.wait_ge(task_free, task_no(h, 0))
                        split_b(h)
                    if j < (2 if last_head else 6):
                        split_task(h, j)
                    if not (last_head and j == 2 * QT - 1):
                        add(h - 1, j)
                    if j == 2:
                        split_folded(1, 2 * h - 1)
                    if j == 6 and not last_head:
                        split_folded(0, 2 * h)
                    if j == 3:
                        split_outputs(h - 1, 1)
                if last_head:
                    split_probs(h, 2 * QT - 1)
                    add(h - 1, 2 * QT - 1)
                split_outputs(h, 0)

            first_body()
            with dve.Fori(1, HEADS - 1) as h:
                body(h)
            body(HEADS - 1)

            def final_stats(b, tiles):
                for t in tiles:
                    n = b * QT + t
                    dve.wait_ge(added, 8 * HEADS + n + 1)
                    dve.bn_stats(stats[:, n, :], resid[:, n, :]).then_inc(fin_stats, 1)

            def final_moments(b):
                for n in range(b * QT, (b + 1) * QT):
                    dve.wait_ge(fin_stats, n + 1)
                    dve.bn_aggr(moments[:, n, :], stats[:, n, :]).then_inc(fin_moments, 1)
                n = slice(b * QT, (b + 1) * QT)
                dve.wait_ge(fin_moments, (b + 1) * QT)
                dve.tensor_scalar(var_eps[:, n], moments[:, n, 1], EPS, None, ALU.add).then_inc(fin_var, 1)

            def final_centre(b, tiles):
                for t in tiles:
                    n = b * QT + t
                    dve.scalar_tensor_tensor(resid[:, n, :], resid[:, n, :], moments[:, n, 0:1], row_vecs[:, 0, :],
                                             ALU.subtract, ALU.mult).then_inc(fin_centred, 1)

            def final_scale(b):
                for t in range(FIN_SHARED[b], QT):
                    n = b * QT + t
                    dve.wait_ge(fin_rstd, b + 1)
                    dve.wait_ge(fin_centred, n + 1)
                    dve.scalar_tensor_tensor(finals[b][:, t * DIM:(t + 1) * DIM], resid[:, n, :], rstd[:, n:n + 1],
                                             row_vecs[:, 1, :], ALU.mult, ALU.add).then_inc(fin_made[1], 1)

            dve.wait_ge(projected, 8 * HEADS)
            dve.wait_ge(task_free, TASKS0 + 8 * (HEADS - 1) + 4)
            split_b(HEADS)
            dve.wait_ge(added, 8 * HEADS)
            invert(2 * QT - 1)
            for t in range(QT):
                add(HEADS - 1, t)
            final_stats(0, range(0, 1))
            split_last_outputs(0)
            final_stats(0, range(1, QT))
            final_moments(0)
            final_centre(0, range(0, 1))
            split_last_outputs(1)
            final_centre(0, range(1, QT))
            for t in range(QT, 2 * QT):
                add(HEADS - 1, t)
            final_stats(1, range(QT))
            final_moments(1)
            final_centre(1, range(QT))
            final_scale(1)


def kernel(x, ctx_768, mask_BxS2_if1, L0_xattn_Wq, L0_xattn_bq, L0_xattn_Wk, L0_xattn_bk, L0_xattn_Wv,
           L0_xattn_bv, L0_xattn_Wd, L0_xattn_bd, L0_xattn_g_q, L0_xattn_be_q, L0_xattn_g_kv, L0_xattn_be_kv,
           L1_xattn_Wq, L1_xattn_Wk, L1_xattn_Wv, L1_xattn_Wo, L1_xattn_gamma, L1_xattn_beta):
    import numpy as np
    import concourse.bacc as bacc
    from concourse.bass_utils import run_bass_kernel_spmd

    def a(v):
        return np.asarray(v)

    twice = np.r_[0:CTX, P:CTX]

    def piece(left, right):
        return np.concatenate([left[:P], left[P:], right[:P], right[P:]], axis=1)

    def head(w, h):
        return a(w)[:, h * DIM:(h + 1) * DIM].T

    wa = [piece(a(L0_xattn_Wq), a(L0_xattn_Wk)[:, twice])]
    wb = [piece(a(L0_xattn_Wv)[:, twice], a(L0_xattn_Wd).T)]
    for h in range(HEADS):
        wa.append(piece(head(L1_xattn_Wq, h), head(L1_xattn_Wk, h)[:, twice]))
        wb.append(piece(head(L1_xattn_Wv, h)[:, twice], a(L1_xattn_Wo)[h * DIM:(h + 1) * DIM]))
    ctx_t = a(ctx_768).transpose(0, 2, 1)[:, twice]

    vectors = np.concatenate([a(v).reshape(2, P).T for v in (L0_xattn_bq, L0_xattn_bk, L0_xattn_bv)], axis=1)
    arrays = {
        "x": a(x).reshape(BATCHES * QUERIES, DIM),
        "context": a(ctx_768).reshape(BATCHES * KEYS, CTX),
        "mask": a(mask_BxS2_if1),
        "weights_a": np.stack(wa),
        "weights_b": np.stack(wb),
        "keys_t": ctx_t.reshape(BATCHES, 2, P, KEYS),
        "vectors": vectors,
        "rows": np.stack([a(L0_xattn_bd), a(L1_xattn_gamma), a(L1_xattn_beta)]),
        "rows_kv": np.stack([a(L0_xattn_g_kv), a(L0_xattn_be_kv)]),
        "rows_q": np.stack([a(L0_xattn_g_q), a(L0_xattn_be_q)]),
        "identity": np.eye(P, dtype=np.float32),
    }
    nc = bacc.Bacc("TRN2", target_bir_lowering=False, num_devices=1)
    arrays = {f"in_{k}": np.ascontiguousarray(v) for k, v in arrays.items()}
    args = [nc.dram_tensor(k, v.shape, mybir.dt.from_np(v.dtype), kind="ExternalInput").ap()
            for k, v in arrays.items()]
    out = nc.dram_tensor("out_0", (BATCHES * QUERIES, DIM), mybir.dt.float32, kind="ExternalOutput").ap()
    build(nc, *args, out)
    r = run_bass_kernel_spmd(nc, [arrays], core_ids=[0])
    return r.results[0]["out_0"].reshape(BATCHES, QUERIES, DIM)
```
